# Optimizing a Trainium2 kernel written in Bass

```python
import numpy as np
import jax
import jax.numpy as jnp

def _softmax(x, axis=-1):
    return jax.nn.softmax(x, axis=axis)

def _gelu(x):
    return jax.nn.gelu(x, approximate=True)

def _silu(x):
    return jax.nn.silu(x)

def _sigmoid(x):
    return jax.nn.sigmoid(x)

def _layernorm(x, axis=-1, eps=1e-05):
    m = jnp.mean(x, axis=axis, keepdims=True)
    v = jnp.var(x, axis=axis, keepdims=True)
    return (x - m) / jnp.sqrt(v + eps)

def _scatter_add(tgt, idx, src, axis=0):
    return tgt.at[idx].add(src)

def _segment_sum(src, seg, n):
    return jax.ops.segment_sum(src, seg, n)
kernel_name = 'mk_sandwich_d1_jaxref_r8_205f3d'

def setup_inputs(seed: int=0):
    np.random.seed(seed)
    _w = jnp.asarray

    def _L0_attn_setup():
        import jax, jax.numpy as jnp
        import numpy as np
        D_MODEL = 128
        HEADS = 4
        DK = 128
        DV = 256
        HDK = DK // HEADS
        HDV = DV // HEADS
        LOW_RANK = 16
        CHUNK = 64
        GATE_NORM = 16.0
        EPS = 1e-05

        def _gla_chunked(q, k, v, g):
            B, H, T, _ = q.shape
            NC = T // CHUNK
            scale = HDK ** (-0.5)

            def to_chunks(t, d):
                return t.reshape(B, H, NC, CHUNK, d).transpose(2, 0, 1, 3, 4)
            qc = to_chunks(q, HDK)
            kc = to_chunks(k, HDK)
            vc = to_chunks(v, HDV)
            bc = jnp.cumsum(to_chunks(g, HDK), axis=-2)
            mask = jnp.tril(jnp.ones((CHUNK, CHUNK), bool))

            def step(S, inp):
                qb, kb, vb, bb = inp
                qg = qb * jnp.exp(bb) * scale
                kd = kb * jnp.exp(-bb)
                A = jnp.einsum('bhtd,bhsd->bhts', qg, kd)
                A = jnp.where(mask, A, 0.0)
                o = jnp.einsum('bhts,bhsv->bhtv', A, vb) + jnp.einsum('bhtd,bhdv->bhtv', qg, S)
                b_last = bb[:, :, -1:, :]
                kg = kb * jnp.exp(b_last - bb)
                S = S * jnp.exp(b_last[:, :, 0, :])[..., None] + jnp.einsum('bhtd,bhtv->bhdv', kg, vb)
                return (S, o)
            S0 = jnp.zeros((B, H, HDK, HDV), q.dtype)
            _, o = jax.lax.scan(step, S0, (qc, kc, vc, bc))
            return o.transpose(1, 2, 0, 3, 4).reshape(B, H, T, HDV)
        key = jax.random.key(seed)
        ks = jax.random.split(key, 10)
        gain = 2.0 ** (-2.5)

        def xavier(k, shape):
            lim = gain * np.sqrt(6.0 / (shape[0] + shape[1]))
            return jax.random.uniform(k, shape, jnp.float32, -lim, lim)
        return {'x': jax.random.normal(ks[0], (2, 256, D_MODEL), jnp.float32), 'Wq': xavier(ks[1], (D_MODEL, DK)), 'Wk': xavier(ks[2], (D_MODEL, DK)), 'Wv': xavier(ks[3], (D_MODEL, DV)), 'Wg': xavier(ks[4], (D_MODEL, DV)), 'Wgk1': xavier(ks[5], (D_MODEL, LOW_RANK)), 'Wgk2': xavier(ks[6], (LOW_RANK, DK)), 'bgk2': jnp.zeros((DK,), jnp.float32), 'Wo': xavier(ks[7], (DV, D_MODEL)), 'rms_w': jnp.ones((HDV,), jnp.float32)}
    _L0_attn_in = _L0_attn_setup()

    def _L0_ffn_setup():
        import jax, jax.numpy as jnp
        import numpy as np
        DIM = 128
        DEPTH = 2
        HEADS = 8
        DIM_HEAD = 64
        WINDOW = 64
        INNER = HEADS * DIM_HEAD
        HID = int(DIM * 4 * 2 / 3)
        B, N = (2, 1024)
        QK_SCALE = 8.0

        def shift_token(t):
            t1, t2 = jnp.split(t, 2, axis=-1)
            t2 = jnp.pad(t2, ((0, 0), (1, 0), (0, 0)))[:, :-1]
            return jnp.concatenate([t1, t2], axis=-1)

        def l2norm(t):
            return t / jnp.clip(jnp.linalg.norm(t, axis=-1, keepdims=True), 1e-12)

        def rotate_half(x):
            x1, x2 = jnp.split(x, 2, axis=-1)
            return jnp.concatenate([-x2, x1], axis=-1)

        def rotary_xpos(q, k):
            n = q.shape[-2]
            half_idx = jnp.arange(0, DIM_HEAD, 2, dtype=jnp.float32)
            inv_freq = 1.0 / 10000.0 ** (half_idx / DIM_HEAD)
            t = jnp.arange(n, dtype=jnp.float32)
            freqs = t[:, None] * inv_freq[None, :]
            freqs = jnp.concatenate([freqs, freqs], axis=-1)
            base = (half_idx + 0.4 * DIM_HEAD) / (1.4 * DIM_HEAD)
            power = (t - n // 2) / float(WINDOW // 2)
            scale = base[None, :] ** power[:, None]
            scale = jnp.concatenate([scale, scale], axis=-1)
            cos, sin = (jnp.cos(freqs), jnp.sin(freqs))
            q = q * cos * scale + rotate_half(q) * sin * scale
            k = k * cos / scale + rotate_half(k) * sin / scale
            return (q, k)

        def local_attention(q, k, v):
            b, h, n, d = q.shape
            w = n // WINDOW
            bq = q.reshape(b, h, w, WINDOW, d) * QK_SCALE
            bk = k.reshape(b, h, w, WINDOW, d)
            bv = v.reshape(b, h, w, WINDOW, d)

            def look_around(t):
                p = jnp.pad(t, ((0, 0), (0, 0), (1, 0), (0, 0), (0, 0)))
                return jnp.concatenate([p[:, :, :w], p[:, :, 1:]], axis=3)
            bk, bv = (look_around(bk), look_around(bv))
            bt = jnp.arange(n).reshape(w, WINDOW)
            btp = jnp.pad(bt, ((1, 0), (0, 0)), constant_values=-1)
            btk = jnp.concatenate([btp[:w], btp[1:]], axis=1)
            sim = jnp.einsum('bhwid,bhwjd->bhwij', bq, bk)
            i = bt[:, :, None]
            j = btk[:, None, :]
            mask = (i < j) | (i > j + WINDOW) | (j == -1)
            sim = jnp.where(mask, -jnp.finfo(sim.dtype).max, sim)
            attn = jax.nn.softmax(sim, axis=-1)
            out = jnp.einsum('bhwij,bhwjd->bhwid', attn, bv)
            return out.reshape(b, h, n, d)

        def _layer(x, wqkv, qs, ksc, wo, lg, lb, w1, b1, w2, b2):
            b, n, _ = x.shape
            h = shift_token(x)
            qkv = h @ wqkv
            q, k, v = jnp.split(qkv, 3, axis=-1)
            to_heads = lambda t: t.reshape(b, n, HEADS, DIM_HEAD).transpose(0, 2, 1, 3)
            q, k, v = (to_heads(q), to_heads(k), to_heads(v))
            q = l2norm(q) * qs
            k = l2norm(k) * ksc
            q, k = rotary_xpos(q, k)
            o = local_attention(q, k, v)
            o = o.transpose(0, 2, 1, 3).reshape(b, n, INNER)
            x = x + o @ wo
            h = shift_token(x)
            mu = h.mean(-1, keepdims=True)
            var = h.var(-1, keepdims=True)
            h = (h - mu) / jnp.sqrt(var + 1e-05) * lg + lb
            h = h @ w1 + b1
            a, g = jnp.split(h, 2, axis=-1)
            h = a * jax.nn.gelu(g, approximate=False)
            x = x + h @ w2 + b2
            return x
        key = jax.random.key(seed)
        ks = jax.random.split(key, 6)
        return {'x': jax.random.normal(ks[0], (B, N, DIM), jnp.float32), 'wqkv': jax.random.normal(ks[1], (DEPTH, DIM, 3 * INNER), jnp.float32) * 0.02, 'q_scale': jnp.ones((DEPTH, DIM_HEAD), jnp.float32), 'k_scale': jnp.ones((DEPTH, DIM_HEAD), jnp.float32), 'wo': jax.random.normal(ks[2], (DEPTH, INNER, DIM), jnp.float32) * 0.02, 'ln_g': jnp.ones((DEPTH, DIM), jnp.float32), 'ln_b': jnp.zeros((DEPTH, DIM), jnp.float32), 'w1': jax.random.normal(ks[3], (DEPTH, DIM, 2 * HID), jnp.float32) * 0.02, 'b1': jnp.zeros((DEPTH, 2 * HID), jnp.float32), 'w2': jax.random.normal(ks[4], (DEPTH, HID, DIM), jnp.float32) * 0.02, 'b2': jnp.zeros((DEPTH, DIM), jnp.float32)}
    _L0_ffn_in = _L0_ffn_setup()
    _d = {'L0_attn_x': _L0_attn_in['x'], 'L0_attn_Wq': _L0_attn_in['Wq'], 'L0_attn_Wk': _L0_attn_in['Wk'], 'L0_attn_Wv': _L0_attn_in['Wv'], 'L0_attn_Wg': _L0_attn_in['Wg'], 'L0_attn_Wgk1': _L0_attn_in['Wgk1'], 'L0_attn_Wgk2': _L0_attn_in['Wgk2'], 'L0_attn_bgk2': _L0_attn_in['bgk2'], 'L0_attn_Wo': _L0_attn_in['Wo'], 'L0_attn_rms_w': _L0_attn_in['rms_w'], 'L0_ffn_wqkv': _L0_ffn_in['wqkv'], 'L0_ffn_q_scale': _L0_ffn_in['q_scale'], 'L0_ffn_k_scale': _L0_ffn_in['k_scale'], 'L0_ffn_wo': _L0_ffn_in['wo'], 'L0_ffn_ln_g': _L0_ffn_in['ln_g'], 'L0_ffn_ln_b': _L0_ffn_in['ln_b'], 'L0_ffn_w1': _L0_ffn_in['w1'], 'L0_ffn_b1': _L0_ffn_in['b1'], 'L0_ffn_w2': _L0_ffn_in['w2'], 'L0_ffn_b2': _L0_ffn_in['b2']}
    _x0 = _d['L0_attn_x']
    _d['L0_attn_x'] = jax.random.normal(jax.random.fold_in(jax.random.key(seed), 1), (2, 1024, 128), dtype=_x0.dtype)
    del _x0
    return _d

def reference(L0_attn_x, L0_attn_Wq, L0_attn_Wk, L0_attn_Wv, L0_attn_Wg, L0_attn_Wgk1, L0_attn_Wgk2, L0_attn_bgk2, L0_attn_Wo, L0_attn_rms_w, L0_ffn_wqkv, L0_ffn_q_scale, L0_ffn_k_scale, L0_ffn_wo, L0_ffn_ln_g, L0_ffn_ln_b, L0_ffn_w1, L0_ffn_b1, L0_ffn_w2, L0_ffn_b2):

    def _L0_attn_ref(x, Wq, Wk, Wv, Wg, Wgk1, Wgk2, bgk2, Wo, rms_w):
        import jax, jax.numpy as jnp
        import numpy as np
        D_MODEL = 128
        HEADS = 4
        DK = 128
        DV = 256
        HDK = DK // HEADS
        HDV = DV // HEADS
        LOW_RANK = 16
        CHUNK = 64
        GATE_NORM = 16.0
        EPS = 1e-05

        def _gla_chunked(q, k, v, g):
            B, H, T, _ = q.shape
            NC = T // CHUNK
            scale = HDK ** (-0.5)

            def to_chunks(t, d):
                return t.reshape(B, H, NC, CHUNK, d).transpose(2, 0, 1, 3, 4)
            qc = to_chunks(q, HDK)
            kc = to_chunks(k, HDK)
            vc = to_chunks(v, HDV)
            bc = jnp.cumsum(to_chunks(g, HDK), axis=-2)
            mask = jnp.tril(jnp.ones((CHUNK, CHUNK), bool))

            def step(S, inp):
                qb, kb, vb, bb = inp
                qg = qb * jnp.exp(bb) * scale
                kd = kb * jnp.exp(-bb)
                A = jnp.einsum('bhtd,bhsd->bhts', qg, kd)
                A = jnp.where(mask, A, 0.0)
                o = jnp.einsum('bhts,bhsv->bhtv', A, vb) + jnp.einsum('bhtd,bhdv->bhtv', qg, S)
                b_last = bb[:, :, -1:, :]
                kg = kb * jnp.exp(b_last - bb)
                S = S * jnp.exp(b_last[:, :, 0, :])[..., None] + jnp.einsum('bhtd,bhtv->bhdv', kg, vb)
                return (S, o)
            S0 = jnp.zeros((B, H, HDK, HDV), q.dtype)
            _, o = jax.lax.scan(step, S0, (qc, kc, vc, bc))
            return o.transpose(1, 2, 0, 3, 4).reshape(B, H, T, HDV)
        B, T, _ = x.shape
        q = (x @ Wq).reshape(B, T, HEADS, HDK).transpose(0, 2, 1, 3)
        k = (x @ Wk).reshape(B, T, HEADS, HDK).transpose(0, 2, 1, 3)
        v = (x @ Wv).reshape(B, T, HEADS, HDV).transpose(0, 2, 1, 3)
        gk = x @ Wgk1 @ Wgk2 + bgk2
        g = jax.nn.log_sigmoid(gk.astype(jnp.float32)) / GATE_NORM
        g = g.reshape(B, T, HEADS, HDK).transpose(0, 2, 1, 3)
        o = _gla_chunked(q, k, v, g)
        o = o.transpose(0, 2, 1, 3)
        o = o * jax.lax.rsqrt(jnp.mean(o * o, axis=-1, keepdims=True) + EPS) * rms_w
        o = o.reshape(B, T, HEADS * HDV)
        o = o * jax.nn.silu(x @ Wg)
        return o @ Wo

    def _L0_ffn_ref(x, wqkv, q_scale, k_scale, wo, ln_g, ln_b, w1, b1, w2, b2):
        import jax, jax.numpy as jnp
        import numpy as np
        DIM = 128
        DEPTH = 2
        HEADS = 8
        DIM_HEAD = 64
        WINDOW = 64
        INNER = HEADS * DIM_HEAD
        HID = int(DIM * 4 * 2 / 3)
        B, N = (2, 1024)
        QK_SCALE = 8.0

        def shift_token(t):
            t1, t2 = jnp.split(t, 2, axis=-1)
            t2 = jnp.pad(t2, ((0, 0), (1, 0), (0, 0)))[:, :-1]
            return jnp.concatenate([t1, t2], axis=-1)

        def l2norm(t):
            return t / jnp.clip(jnp.linalg.norm(t, axis=-1, keepdims=True), 1e-12)

        def rotate_half(x):
            x1, x2 = jnp.split(x, 2, axis=-1)
            return jnp.concatenate([-x2, x1], axis=-1)

        def rotary_xpos(q, k):
            n = q.shape[-2]
            half_idx = jnp.arange(0, DIM_HEAD, 2, dtype=jnp.float32)
            inv_freq = 1.0 / 10000.0 ** (half_idx / DIM_HEAD)
            t = jnp.arange(n, dtype=jnp.float32)
            freqs = t[:, None] * inv_freq[None, :]
            freqs = jnp.concatenate([freqs, freqs], axis=-1)
            base = (half_idx + 0.4 * DIM_HEAD) / (1.4 * DIM_HEAD)
            power = (t - n // 2) / float(WINDOW // 2)
            scale = base[None, :] ** power[:, None]
            scale = jnp.concatenate([scale, scale], axis=-1)
            cos, sin = (jnp.cos(freqs), jnp.sin(freqs))
            q = q * cos * scale + rotate_half(q) * sin * scale
            k = k * cos / scale + rotate_half(k) * sin / scale
            return (q, k)

        def local_attention(q, k, v):
            b, h, n, d = q.shape
            w = n // WINDOW
            bq = q.reshape(b, h, w, WINDOW, d) * QK_SCALE
            bk = k.reshape(b, h, w, WINDOW, d)
            bv = v.reshape(b, h, w, WINDOW, d)

            def look_around(t):
                p = jnp.pad(t, ((0, 0), (0, 0), (1, 0), (0, 0), (0, 0)))
                return jnp.concatenate([p[:, :, :w], p[:, :, 1:]], axis=3)
            bk, bv = (look_around(bk), look_around(bv))
            bt = jnp.arange(n).reshape(w, WINDOW)
            btp = jnp.pad(bt, ((1, 0), (0, 0)), constant_values=-1)
            btk = jnp.concatenate([btp[:w], btp[1:]], axis=1)
            sim = jnp.einsum('bhwid,bhwjd->bhwij', bq, bk)
            i = bt[:, :, None]
            j = btk[:, None, :]
            mask = (i < j) | (i > j + WINDOW) | (j == -1)
            sim = jnp.where(mask, -jnp.finfo(sim.dtype).max, sim)
            attn = jax.nn.softmax(sim, axis=-1)
            out = jnp.einsum('bhwij,bhwjd->bhwid', attn, bv)
            return out.reshape(b, h, n, d)

        def _layer(x, wqkv, qs, ksc, wo, lg, lb, w1, b1, w2, b2):
            b, n, _ = x.shape
            h = shift_token(x)
            qkv = h @ wqkv
            q, k, v = jnp.split(qkv, 3, axis=-1)
            to_heads = lambda t: t.reshape(b, n, HEADS, DIM_HEAD).transpose(0, 2, 1, 3)
            q, k, v = (to_heads(q), to_heads(k), to_heads(v))
            q = l2norm(q) * qs
            k = l2norm(k) * ksc
            q, k = rotary_xpos(q, k)
            o = local_attention(q, k, v)
            o = o.transpose(0, 2, 1, 3).reshape(b, n, INNER)
            x = x + o @ wo
            h = shift_token(x)
            mu = h.mean(-1, keepdims=True)
            var = h.var(-1, keepdims=True)
            h = (h - mu) / jnp.sqrt(var + 1e-05) * lg + lb
            h = h @ w1 + b1
            a, g = jnp.split(h, 2, axis=-1)
            h = a * jax.nn.gelu(g, approximate=False)
            x = x + h @ w2 + b2
            return x
        for l in range(DEPTH):
            x = _layer(x, wqkv[l], q_scale[l], k_scale[l], wo[l], ln_g[l], ln_b[l], w1[l], b1[l], w2[l], b2[l])
        return x
    x = L0_attn_x
    x = x + _layernorm(_L0_attn_ref(_layernorm(x, axis=-1), L0_attn_Wq, L0_attn_Wk, L0_attn_Wv, L0_attn_Wg, L0_attn_Wgk1, L0_attn_Wgk2, L0_attn_bgk2, L0_attn_Wo, L0_attn_rms_w), axis=-1)
    x = x + _layernorm(_L0_ffn_ref(_layernorm(x, axis=-1), L0_ffn_wqkv, L0_ffn_q_scale, L0_ffn_k_scale, L0_ffn_wo, L0_ffn_ln_g, L0_ffn_ln_b, L0_ffn_w1, L0_ffn_b1, L0_ffn_w2, L0_ffn_b2), axis=-1)
    return x

_drawn_inputs = setup_inputs


def setup_inputs(seed=0):
    import zlib

    import numpy as np

    out = dict(_drawn_inputs(seed))
    spreads = {'L0_attn_bgk2': (0.0, 0.1),
     'L0_attn_rms_w': (1.0, 0.2),
     'L0_ffn_q_scale': (1.0, 0.6),
     'L0_ffn_k_scale': (1.0, 0.6),
     'L0_ffn_ln_g': (1.0, 0.6),
     'L0_ffn_ln_b': (0.0, 0.8),
     'L0_ffn_b1': (0.0, 0.8),
     'L0_ffn_b2': (0.0, 0.8)}
    factors = {'L0_attn_Wgk1': 8.0,
     'L0_attn_Wgk2': 8.0,
     'L0_ffn_wqkv': 4.705,
     'L0_ffn_wo': 4.718,
     'L0_ffn_w1': 7.474,
     'L0_ffn_w2': 7.366}
    for name, (base, spread) in spreads.items():
        noise = np.random.default_rng([zlib.crc32(name.encode()), seed]).standard_normal(out[name].shape)
        drawn = base * np.exp(spread * noise) if base else spread * noise
        out[name] = jnp.asarray(drawn.astype(out[name].dtype))
    for name, factor in factors.items():
        out[name] = (out[name] * factor).astype(out[name].dtype)
    return out
```

```python
from contextlib import ExitStack

import concourse.bass as bass
from concourse import mybir

F32 = mybir.dt.float32
BF16 = mybir.dt.bfloat16
U32 = mybir.dt.uint32
ALU = mybir.AluOpType
ACT = mybir.ActivationFunctionType
AX = mybir.AxisListType

P = 128
EPS = 1e-5
LN2 = 0.6931471805599453


def wait(engine, semaphore, count):
    if isinstance(count, int) and count <= 0:
        return
    engine.wait_ge(semaphore, count)


def build_program(nc, x, Wq, Wk, Wv, Wg, Wgk1, Wgk2, bgk2, Wo, rms_w,
                  wqkv, q_scale, k_scale, wo, ln_g, ln_b, w1, b1, w2, b2,
                  square_consts, rotary_cos, rotary_sin, out):
    B, T, D = x.shape
    TILES_PER_BATCH = T // P
    NT = B * TILES_PER_BATCH
    GH, GDK, GDV = 4, Wq.shape[1] // 4, Wv.shape[1] // 4
    GV = GH * GDV
    RANK = Wgk1.shape[1]
    CH = 64
    GATE = 1.0 / 16.0
    DEPTH, _, QKV = wqkv.shape
    INNER = QKV // 3
    DH = q_scale.shape[1]
    AH = INNER // DH
    PAIRS = AH // 2
    W = 64
    HID = w2.shape[1]
    NJ = (HID + P - 1) // P
    ROWS = [min(P, HID - j * P) for j in range(NJ)]
    GROUP = 4
    assert B == 2 and D == P and 2 * CH == P and 2 * W == P

    ctx = ExitStack()
    with ctx:
        def sb(name, cols, dt=F32):
            return ctx.enter_context(nc.sbuf_tensor(name, [P, cols], dt))

        def sems(names):
            return {k: ctx.enter_context(nc.semaphore(k)) for k in names.split()}

        bank = [ctx.enter_context(nc.psum_tensor(f"bank{i}", [P, 512], F32)) for i in range(8)]

        consts = sb("consts", 8 * P)
        ident, shift, carry, mask_a, mask_b, mask_a0, causal, keep = (
            consts[:, i * P:(i + 1) * P] for i in range(8))
        causal_bits = causal.bitcast(U32)
        ident_bf = sb("ident_bf", P, BF16)
        masks_bf = sb("masks_bf", 3 * P, BF16)
        cos_base = sb("cos_base", TILES_PER_BATCH * 2 * DH)
        sin_base = sb("sin_base", TILES_PER_BATCH * 2 * DH)
        cos_t = sb("cos_t", TILES_PER_BATCH * 2 * DH)
        sin_t = sb("sin_t", TILES_PER_BATCH * 2 * DH)
        scales = sb("scales", DEPTH * 2 * DH)
        wqk_sb = sb("wqk_sb", 2 * P)
        wvg_sb = sb("wvg_sb", 2 * GV)
        wgk1_sb = sb("wgk1_sb", RANK)
        wgk2_sb = sb("wgk2_sb", P)
        wout_sb = sb("wout_sb", 2 * D)
        columns = sb("columns", 4 + 2 * DEPTH + DEPTH * 2 * NJ)
        bgk2_col, rms_col = columns[:, 0:1], columns[:, 1:2]
        eps_col, norm_bias_col = columns[:, 2:3], columns[:, 3:4]
        lng_col = [columns[:, 4 + l:5 + l] for l in range(DEPTH)]
        lnb_col = [columns[:, 4 + DEPTH + l:5 + DEPTH + l] for l in range(DEPTH)]
        B1_AT = 4 + 2 * DEPTH
        wqkv_sb = sb("wqkv_sb", DEPTH * QKV)
        wo_sb = sb("wo_sb", DEPTH * PAIRS * D)
        w1_sb = sb("w1_sb", DEPTH * 2 * HID)
        w2_sb = sb("w2_sb", DEPTH * NJ * D)

        def b1_col(l, half, j):
            at = B1_AT + (l * 2 + half) * NJ + j
            return columns[0:ROWS[j], at:at + 1]

        x_in = sb("x_in", NT * D)
        x_attn = sb("x_attn", NT * D)
        ping, pong = sb("ping", NT * D), sb("pong", NT * D)
        stream = [(ping, pong)[l % 2] for l in range(DEPTH + 1)]
        middle = sb("middle", (NT + 2) * D)
        z_t = sb("z_t", NT * P)

        def tile_of(buf, n):
            return buf[:, bass.ds(n * D, D)]

        st_x = sb("st_x", 2 * 6)
        mv_x = sb("mv_x", 2 * 2)
        ln_x = sb("ln_x", 2)
        rstd_x = sb("rstd_x", 2)
        xn = sb("xn", 2 * P)
        xn_t = sb("xn_t", 2 * P)
        v_sb = sb("v_sb", 2 * GV)
        eg = sb("eg", GV)
        eg1 = sb("eg1", GV)
        rec = sb("rec", GV)
        silu = sb("silu", 2 * GV)
        low = sb("low", P)
        gkb = sb("gkb", P)
        gk_abs = sb("gk_abs", P)
        gk_exp = sb("gk_exp", P)
        gk_ln = sb("gk_ln", P)
        gk_min = sb("gk_min", P)
        logsig = sb("logsig", P)
        cum = sb("cum", P)
        last16 = sb("last16", 2)
        dlast = sb("dlast", 2 * 2)
        dec_q = sb("dec_q", P)
        dec_k = sb("dec_k", P)
        dec_g = sb("dec_g", P)
        qg = sb("qg", 2 * GH * P)
        kd = sb("kd", 2 * P)
        kg = sb("kg", P)
        kg_tok = sb("kg_tok", 2 * 2 * P)
        a_t = sb("a_t", 2 * GH * P)
        state = sb("state", 2 * 2 * GDV)
        o_sq = sb("o_sq", GV)
        o_ss = sb("o_ss", GH)
        o_ln = sb("o_ln", GH)
        o_r = sb("o_r", GH)
        og1 = sb("og1", GV)
        og2 = sb("og2", 2 * GV)
        og_t = sb("og_t", 2 * 2 * P)
        st_y = sb("st_y", 6)
        mv_y = sb("mv_y", 2)
        ln_y = sb("ln_y", 1)
        rstd_y = sb("rstd_y", 1)
        yn = sb("yn", P)
        st_f = sb("st_f", 6)
        mv_f = sb("mv_f", 2)
        ln_f = sb("ln_f", 1)
        rstd_f = sb("rstd_f", 1)

        h_t = sb("h_t", 2 * (P + 1))
        x_slot = sb("x_slot", 2 * P)
        sq = sb("sq", 2 * INNER)
        ss = sb("ss", 2 * AH)
        ssc = sb("ssc", 2 * AH)
        ss_ln = sb("ss_ln", 2 * AH)
        inv = sb("inv", 2 * AH)
        qn = sb("qn", 2 * INNER)
        rot1 = sb("rot1", 2 * INNER)
        rot2 = sb("rot2", 2 * INNER)
        qr = sb("qr", 2 * 2 * INNER)
        q_bd = sb("q_bd", 2 * PAIRS * 2 * P)
        KC = P + W
        k_t = sb("k_t", 2 * PAIRS * KC)
        v_cur = sb("v_cur", 2 * INNER)
        v_mix = sb("v_mix", 2 * INNER)
        neg_max = sb("neg_max", 2 * PAIRS)
        row_sum = sb("row_sum", 2 * 2 * PAIRS)
        row_rec = sb("row_rec", 2 * PAIRS)
        PROBS, PROBS_T = 2 * 2 * PAIRS * P, 2 * PAIRS * P
        shared = sb("shared", max(PROBS + PROBS_T, 2 * NJ * GROUP * P))
        probs, probs_t = shared[:, 0:PROBS], shared[:, PROBS:PROBS + PROBS_T]
        o_t = sb("o_t", 2 * PAIRS * P)
        hcat = sb("hcat", 2 * P)
        st_z = sb("st_z", 6)
        mv_z = sb("mv_z", 2)
        ln_z = sb("ln_z", 1)
        rstd_z = sb("rstd_z", 1)
        zn = sb("zn", 2 * P)

        gelu = sq[:, 0:2 * GROUP * P]
        hid = shared[:, 0:2 * NJ * GROUP * P]
        st_o = sb("st_o", NT * 6)
        mv_o = sb("mv_o", NT * 2)
        ln_o = sb("ln_o", NT)
        rstd_o = sb("rstd_o", NT)
        xo, res = x_in, stream[DEPTH - 1]

        d = sems("d_const d_x0 d_x1 d_gla d_qkv d_cols d_scales d_tab d_ffn d_out")
        s = sems(
            "zero_dve zero_pool cast_consts col_consts "
            "x_stats x_aggr x_ln x_rstd xn_ready xt_done xnt_ready vg_done proj_done v_ready eg_ready eg1_ready "
            "rec_ready silu_ready low_ready gk_done gkb_ready gabs_ready gexp_ready gln_ready gmin_ready "
            "logsig_ready cum_ready last_ready decq_ready deck_ready decg_ready qg_ready kd_ready kg_ready "
            "at_done kgt_done atm_ready kgtok_ready kv_done s1_ready s2_ready go_done osq_ready oss_ready oln_ready "
            "or_ready og1_ready og2_ready ogt_done ogt_ready y_done y_stats y_aggr y_ln y_rstd yn_ready "
            "x1_ready f_stats f_aggr f_ln f_rstd xf_ready "
            "slot_ready carry_zero table_ready cos_ready xtr_done carried ht_ready qk_done sq_ready ss_ready ssc_ready ssl_ready inv_ready "
            "qn_ready rot1_ready rot2_ready qr_ready qt_done kt_done qbd0_ready qbd1_ready kprev_ready kt_ready "
            "sc0_done sc1_done max0_ready max1_ready p0_ready p1_ready rec_sum_ready pn_ready pt0_done pt1_done "
            "pt0_ready pt1_ready v_done vup_ready vcur_ready vmix_ready pv_done ot_ready wo_done mid_ready "
            "hs_done hs_ready z_stats z_aggr z_ln z_rstd zn_ready zt_done z_ready "
            "ones_ready h1_done gelu_ready hid_ready h2_done ffn_ready sto_ready mvo_ready "
            "lno_ready rstdo_ready xo_ready res_ready")

        def q_blocks(par, b_t, h2):
            r = slice(h2 * DH, (h2 + 1) * DH)
            dst = q_bd[r, par * PAIRS * 2 * P:(par + 1) * PAIRS * 2 * P].rearrange("p (c w i) -> p c w i", c=PAIRS, w=2)
            return (dst[:, :, :, h2 * W:(h2 + 1) * W],
                    b_t[r, :].rearrange("p (c w i) -> p c w i", c=PAIRS, w=2))

        dve_engine = nc.vector

        def wait_apart(engine, *waits):
            if not isinstance(waits[0][1], int):
                waits = [(semaphore, engine.snap(engine.to_reg(count))) for semaphore, count in waits]
                engine.wait_ge(s["zero_dve" if engine is dve_engine else "zero_pool"], 1)
            for semaphore, count in waits:
                wait(engine, semaphore, count)

        block = ctx.enter_context(nc.Block())

        def iterate(engine, step):
            for k in range(-2, 4):
                step(k, k % 2)
            with engine.Fori(4, NT - 3, 2) as k:
                step(k, 0)
                step(k + 1, 1)
            for k in range(NT - 2, NT + 2):
                step(k, k % 2)

        def staged(fn, k, parity, lag, *args):
            n = k + lag
            if isinstance(n, int) and not 0 <= n < NT:
                return
            fn(n, (parity + lag) % 2, *args)

        def capped(count, most):
            return min(count, most) if isinstance(count, int) else count

        @block.sync
        def _(sp):
            xv = x_in[:, :].rearrange("p (n d) -> p n d", d=D)
            sp.dma_start(xv[:, 0:B, :], x[:, 0:P, :].rearrange("b p d -> p b d")).then_inc(d["d_x0"], 16)
            sp.dma_start(consts[:, :], square_consts).then_inc(d["d_const"], 16)
            sp.dma_start(wvg_sb[:, 0:GV], Wv).then_inc(d["d_gla"], 16)
            sp.dma_start(wvg_sb[:, GV:2 * GV], Wg).then_inc(d["d_gla"], 16)
            sp.dma_start(wqk_sb[:, 0:P], Wq).then_inc(d["d_gla"], 16)
            sp.dma_start(wqk_sb[:, P:2 * P], Wk).then_inc(d["d_gla"], 16)
            sp.dma_start(wgk1_sb[:, :], Wgk1).then_inc(d["d_gla"], 16)
            sp.dma_start(wgk2_sb[0:RANK, :], Wgk2).then_inc(d["d_gla"], 16)
            sp.dma_start(wout_sb[:, :].rearrange("p (c n) -> p c n", c=2),
                         Wo.rearrange("(c p) n -> p c n", p=P)).then_inc(d["d_gla"], 16)
            for b in range(B):
                sp.dma_start(xv[:, B + b:NT:B, :],
                             x[b, P:T, :].rearrange("(t p) d -> p t d", p=P)).then_inc(d["d_x1"], 16)
            sp.dma_start(cos_base[:, :], rotary_cos).then_inc(d["d_tab"], 16)
            sp.dma_start(sin_base[:, :], rotary_sin).then_inc(d["d_tab"], 16)
            sp.dma_start(wqkv_sb[:, :].rearrange("p (l n) -> p l n", l=DEPTH),
                         wqkv.rearrange("l k n -> k l n")).then_inc(d["d_qkv"], 16)
            sp.dma_start(wo_sb[:, :].rearrange("p (l c n) -> p l c n", l=DEPTH, c=PAIRS),
                         wo.rearrange("l (c p) n -> p l c n", p=P)).then_inc(d["d_qkv"], 16)
            sp.dma_start(w1_sb[:, :].rearrange("p (l n) -> p l n", l=DEPTH),
                         w1.rearrange("l k n -> k l n")).then_inc(d["d_ffn"], 16)
            w2v = w2_sb[:, :].rearrange("p (l c n) -> p l c n", l=DEPTH, c=NJ)
            for l in range(DEPTH):
                sp.dma_start(w2v[:, l, 0:NJ - 1, :],
                             w2[l, 0:(NJ - 1) * P, :].rearrange("(c p) n -> p c n", p=P)).then_inc(d["d_ffn"], 16)
                sp.dma_start(w2v[0:ROWS[-1], l, NJ - 1, :], w2[l, (NJ - 1) * P:HID, :]).then_inc(d["d_ffn"], 16)
                sp.dma_start(w2v[ROWS[-1]:ROWS[-1] + 1, l, NJ - 1, :], b2[l:l + 1, :]).then_inc(d["d_ffn"], 16)
            ov = res[:, :].rearrange("p (n d) -> p n d", d=D)
            for g in range(NT // GROUP):
                sp.wait_ge(s["res_ready"], g + 1)
                for b in range(B):
                    t0 = g * GROUP // B
                    sp.dma_start(out[b, t0 * P:(t0 + GROUP // B) * P, :].rearrange("(t p) d -> p t d", p=P),
                                 ov[:, g * GROUP + b:(g + 1) * GROUP:B, :]).then_inc(d["d_out"], 16)
            sp.wait_ge(d["d_out"], 16 * B * (NT // GROUP))

        @block.gpsimd
        def _(pool):
            pool.dma_start(columns[:, 0:1], bgk2.rearrange("(p a) -> p a", a=1)).then_inc(d["d_cols"], 16)
            for h2 in range(P // GDV):
                pool.dma_start(columns[h2 * GDV:(h2 + 1) * GDV, 1:2],
                               rms_w.rearrange("(p a) -> p a", a=1)).then_inc(d["d_cols"], 16)
            with nc.allow_non_contiguous_dma(reason="per-partition columns of the small vectors"):
                pool.dma_start(columns[:, 4:4 + DEPTH], ln_g.rearrange("l p -> p l")).then_inc(d["d_cols"], 16)
                pool.dma_start(columns[:, 4 + DEPTH:4 + 2 * DEPTH],
                               ln_b.rearrange("l p -> p l")).then_inc(d["d_cols"], 16)
                for l in range(DEPTH):
                    for half in range(2):
                        at = B1_AT + (l * 2 + half) * NJ
                        pool.dma_start(columns[:, at:at + NJ - 1],
                                       b1[l, half * HID:half * HID + (NJ - 1) * P].rearrange("(j p) -> p j", p=P)
                                       ).then_inc(d["d_cols"], 16)
                        pool.dma_start(columns[0:ROWS[-1], at + NJ - 1:at + NJ],
                                       b1[l, half * HID + (NJ - 1) * P:(half + 1) * HID].rearrange("(p a) -> p a", a=1)
                                       ).then_inc(d["d_cols"], 16)
                for l in range(DEPTH):
                    for i, src in enumerate((q_scale, k_scale)):
                        pool.dma_start(scales[:, (l * 2 + i) * DH:(l * 2 + i + 1) * DH],
                                       src[l, :].partition_broadcast(P)).then_inc(d["d_scales"], 16)
            for buf in (q_bd, k_t, v_cur, v_mix):
                pool.memset(buf[:, :], 0.0)
            pool.memset(middle[:, 0:2 * D], 0.0)
            pool.memset(h_t[:, :], 0.0).then_inc(s["zero_pool"], 1)
            pool.wait_ge(s["zero_pool"], 1)

            for l in range(DEPTH):
                base = NT * l

                def copy_in(n, par):
                    N = base + n
                    wait(pool, s["vmix_ready"], N - 1)
                    wait(pool, s["xtr_done"], N - 1)
                    pool.tensor_copy(x_slot[:, par * P:(par + 1) * P], tile_of(stream[l], n)
                                     ).then_inc(s["slot_ready"], 1)

                def keep_prev_keys(n, par):
                    N = base + n
                    kv = k_t[:, par * PAIRS * KC:(par + 1) * PAIRS * KC].rearrange("p (c k) -> p c k", k=KC)
                    wait_apart(pool, (s["sc1_done"], N - 1), (s["kt_ready"], N - 1), (s["vmix_ready"], N + 1))
                    pool.tensor_scalar(kv[:, :, P:KC], kv[:, :, W:P], 1.0, 0.0, ALU.mult, ALU.add
                                       ).then_inc(s["kprev_ready"], 1)

                def keep_prev_values(n, par):
                    N = base + n
                    c = slice(par * INNER, (par + 1) * INNER)
                    wait_apart(pool, (s["pv_done"], N - 1), (s["vcur_ready"], N - 1), (s["rot2_ready"], N + 1))
                    pool.tensor_scalar(v_mix[W:P, c], v_cur[W:P, c], 1.0, 0.0, ALU.mult, ALU.add
                                       ).then_inc(s["vup_ready"], 1)

                def mix_values(n, par):
                    N = base + n
                    c = slice(par * INNER, (par + 1) * INNER)
                    wait_apart(pool, (s["vcur_ready"], N + 1), (s["pn_ready"], N))
                    pool.tensor_scalar(v_mix[0:W, c], v_cur[0:W, c], 1.0, 0.0, ALU.mult, ALU.add
                                       ).then_inc(s["vmix_ready"], 1)

                def rotate_sin(n, par):
                    N = base + n
                    t = (n - par) // 2 if isinstance(n, int) else None
                    wait(pool, s["qn_ready"], N + 1)
                    wait(pool, s["qr_ready"], N)
                    for i in range(2):
                        a = qn[:, i * INNER:(i + 1) * INNER].rearrange("p (h e r) -> p h e r", h=AH, e=2)
                        o = rot2[:, i * INNER:(i + 1) * INNER].rearrange("p (h e r) -> p h e r", h=AH, e=2)
                        tab = sin_t[:, bass.ds((n - par) * DH + i * DH, DH)].rearrange("p (e r) -> p e r", e=2)
                        ins = pool.tensor_tensor(o, a[:, :, ::-1, :], tab.unsqueeze(1).to_broadcast([P, AH, 2, DH // 2]),
                                                 ALU.mult)
                    ins.then_inc(s["rot2_ready"], 1)

                def normalise_probs(n, par):
                    N = base + n
                    wait_apart(pool, (s["rec_sum_ready"], N + 1), (s["vup_ready"], capped(N + 2, base + NT)))
                    for wp in range(2 * PAIRS):
                        at = (par * 2 * PAIRS + wp) * P
                        ins = pool.tensor_scalar(probs[:, at:at + P], probs[:, at:at + P],
                                                 row_rec[:, wp:wp + 1], 1.0, ALU.mult, ALU.mult)
                    ins.then_inc(s["pn_ready"], 1)

                if l:
                    pool.wait_ge(s["ffn_ready"], 2 * (NT // GROUP) * l)
                else:
                    pool.wait_ge(s["xf_ready"], NT)
                if l:
                    pool.wait_ge(s["v_done"], base)
                    pool.wait_ge(s["ht_ready"], base)
                    for b in range(B):
                        c = b * (P + 1) + P
                        ins = pool.memset(h_t[:, c:c + 1], 0.0)
                    ins.then_inc(s["carry_zero"], 1)

                def step(k, par):
                    staged(copy_in, k, par, 2)
                    staged(keep_prev_keys, k, par, 0)
                    staged(rotate_sin, k, par, 1)
                    staged(keep_prev_values, k, par, 1)
                    staged(normalise_probs, k, par, 0)
                    staged(mix_values, k, par, 1)
                iterate(pool, step)

                pool.wait_ge(s["z_ready"], base + NT)
                for slot in range(2):
                    at = (slot * NJ + NJ - 1) * GROUP * P
                    ins = pool.memset(hid[ROWS[-1] // 32 * 32:P, at:at + GROUP * P], 1.0)
                ins.then_inc(s["ones_ready"], 1)
                pool.wait_ge(s["ones_ready"], l + 1)

        @block.tensor
        def _(pe):
            def mm(o, w, m, start=True, stop=True, skip=False):
                return pe.matmul(o, w, m, start=start, stop=stop, skip_group_check=skip)

            b_xt, b_qk, b_vg, b_at, b_kv, b_o, b_og, b_y = bank

            def transpose_x(n, par):
                wait(pe, s["xn_ready"], n + 1)
                wait(pe, s["xnt_ready"], n)
                pe.transpose(b_xt[:, 0:P], xn[:, par * P:(par + 1) * P], ident).then_inc(s["xt_done"], 1)

            def project(n, par):
                a = xn_t[:, par * P:(par + 1) * P]
                wait(pe, s["xnt_ready"], n + 1)
                wait(pe, s["silu_ready"], n)
                mm(b_vg[:, :], a, wvg_sb[:, :]).then_inc(s["vg_done"], 1)
                wait(pe, s["kg_ready"], n)
                mm(b_qk[0:RANK, 3 * P:4 * P], wgk1_sb[:, :], a)
                mm(b_qk[:, 0:P], wqk_sb[:, 0:P], a)
                mm(b_qk[:, P:2 * P], wqk_sb[:, P:2 * P], a).then_inc(s["proj_done"], 1)

            def project_gate(n, par):
                wait(pe, s["low_ready"], n + 1)
                mm(b_qk[:, 2 * P:3 * P], wgk2_sb[0:RANK, :], low[0:RANK, :]).then_inc(s["gk_done"], 1)

            def intra_scores(n, par):
                wait(pe, s["qg_ready"], n + 1)
                wait(pe, s["kd_ready"], n + 1)
                wait(pe, s["atm_ready"], n)
                mm(b_at[:, :], kd[:, par * P:(par + 1) * P], qg[:, par * GH * P:(par + 1) * GH * P]
                   ).then_inc(s["at_done"], 1)
                wait(pe, s["kg_ready"], n + 1)
                wait(pe, s["s2_ready"], n)
                pe.transpose(b_kv[:, 0:P], kg[:, :], ident).then_inc(s["kgt_done"], 1)

            def key_values(n, par):
                wait(pe, s["kgtok_ready"], n + 1)
                wait(pe, s["v_ready"], n + 1)
                for c in range(2):
                    for h in range(GH):
                        at = (par * 2 + c) * P + h * GDK
                        ins = mm(b_kv[h * GDK:(h + 1) * GDK, P + c * GDV:P + (c + 1) * GDV],
                                 kg_tok[:, at:at + GDK], v_sb[:, par * GV + h * GDV:par * GV + (h + 1) * GDV])
                ins.then_inc(s["kv_done"], 1)

            def outputs(n, par):
                wait(pe, s["atm_ready"], n + 1)
                wait(pe, s["v_ready"], n + 1)
                wait(pe, s["og1_ready"], n)
                for h in range(GH):
                    mm(b_o[:, h * GDV:(h + 1) * GDV], a_t[:, (par * GH + h) * P:(par * GH + h + 1) * P],
                       v_sb[:, par * GV + h * GDV:par * GV + (h + 1) * GDV], start=(h == 0), stop=False, skip=True)
                wait(pe, s["s1_ready"], n + 1)
                for c in range(2):
                    for h in range(GH):
                        ins = mm(b_o[c * CH:(c + 1) * CH, h * GDV:(h + 1) * GDV],
                                 qg[:, (par * GH + h) * P + c * CH:(par * GH + h) * P + (c + 1) * CH],
                                 state[:, (par * 2 + c) * GDV:(par * 2 + c + 1) * GDV],
                                 start=False, stop=True, skip=True)
                ins.then_inc(s["go_done"], 1)

            def transpose_o(n, par):
                wait(pe, s["og2_ready"], n + 1)
                wait(pe, s["ogt_ready"], n)
                for c in range(2):
                    ins = pe.transpose(b_og[:, c * P:(c + 1) * P],
                                       og2[:, par * GV + c * P:par * GV + (c + 1) * P], ident)
                ins.then_inc(s["ogt_done"], 1)

            def project_out(n, par):
                wait(pe, s["ogt_ready"], n + 1)
                wait(pe, s["yn_ready"], n)
                for c in range(2):
                    ins = mm(b_y[:, 0:D], og_t[:, (par * 2 + c) * P:(par * 2 + c + 1) * P],
                             wout_sb[:, c * D:(c + 1) * D], start=(c == 0), stop=(c == 1))
                ins.then_inc(s["y_done"], 1)

            def gla_step(k, par):
                staged(transpose_o, k, par, -1)
                staged(intra_scores, k, par, 0)
                staged(project_out, k, par, -1)
                staged(project, k, par, 1)
                staged(key_values, k, par, 0)
                staged(project_gate, k, par, 1)
                staged(outputs, k, par, 0)
                staged(transpose_x, k, par, 2)

            pe.wait_ge(d["d_const"], 16)
            pe.wait_ge(d["d_gla"], 7 * 16)
            pe.wait_ge(s["zero_dve"], 1)
            iterate(pe, gla_step)

            pe.wait_ge(d["d_qkv"], 32)
            pe.wait_ge(s["zero_pool"], 1)
            pe.wait_ge(s["cast_consts"], 2)
            pe.wait_ge(s["xf_ready"], NT)
            for l in range(DEPTH):
                base = NT * l
                b_q, b_k, b_v, b_t0, b_t1, b_s0, b_s1, b_m = bank
                wl = wqkv_sb[:, l * QKV:(l + 1) * QKV]

                def transpose_in(n, par):
                    N = base + n
                    wait(pe, s["ht_ready"], N)
                    wait(pe, s["hs_ready"], N - 3)
                    wait(pe, s["slot_ready"], N + 1)
                    pe.transpose(b_m[:, 0:P], x_slot[:, par * P:(par + 1) * P], ident).then_inc(s["xtr_done"], 1)

                def project_qk(n, par):
                    N = base + n
                    a = h_t[:, par * (P + 1):par * (P + 1) + P]
                    wait(pe, s["ht_ready"], N + 1)
                    wait(pe, s["qn_ready"], N)
                    mm(b_q[:, :], a, wl[:, 0:INNER])
                    mm(b_k[:, :], a, wl[:, INNER:2 * INNER]).then_inc(s["qk_done"], 1)

                def project_v(n, par):
                    N = base + n
                    wait(pe, s["ot_ready"], N - 1)
                    wait(pe, s["vcur_ready"], N)
                    mm(b_v[:, :], h_t[:, par * (P + 1):par * (P + 1) + P], wl[:, 2 * INNER:3 * INNER]
                       ).then_inc(s["v_done"], 1)

                def transpose_qk(n, par):
                    N = base + n
                    wait(pe, s["qr_ready"], N + 1)
                    wait(pe, s["pt0_ready"], N - 1)
                    for c in range(PAIRS):
                        at = par * 2 * INNER + c * P
                        ins = pe.transpose(b_t0[:, c * P:(c + 1) * P], qr[:, at:at + P], ident)
                    ins.then_inc(s["qt_done"], 1)
                    wait(pe, s["pt1_ready"], N - 1)
                    for c in range(PAIRS):
                        at = par * 2 * INNER + INNER + c * P
                        ins = pe.transpose(b_t1[:, c * P:(c + 1) * P], qr[:, at:at + P], ident)
                    ins.then_inc(s["kt_done"], 1)

                def scores(n, par, w):
                    N = base + n
                    b_s = (b_s0, b_s1)[w]
                    wait(pe, s["qbd0_ready"], N + 1)
                    wait(pe, s["qbd1_ready"], N + 1)
                    wait(pe, s["kt_ready"], N + 1)
                    wait(pe, s[f"p{w}_ready"], N)
                    first = isinstance(n, int) and n < B
                    m = (2 if first else 0) if w == 0 else 1
                    mask = masks_bf[:, m * P:(m + 1) * P].unsqueeze(1).to_broadcast([P, PAIRS, P])
                    mm(b_s[:, :].rearrange("p (c k) -> p c k", c=PAIRS), ident_bf[:, :], mask,
                       start=True, stop=False, skip=True)
                    for c in range(PAIRS):
                        kc = k_t[:, (par * PAIRS + c) * KC:(par * PAIRS + c + 1) * KC]
                        if w == 0:
                            kc = kc.rearrange("p (a k) -> p a k", k=W)[:, 0:3:2, :]
                        else:
                            kc = kc[:, 0:P]
                        at = ((par * PAIRS + c) * 2 + w) * P
                        o = b_s[:, c * P:(c + 1) * P]
                        if w == 0:
                            o = o.rearrange("p (a k) -> p a k", k=W)
                        ins = mm(o, q_bd[:, at:at + P], kc, start=False, stop=True, skip=True)
                    ins.then_inc(s[f"sc{w}_done"], 1)

                def transpose_probs(n, par):
                    N = base + n
                    wait(pe, s["pn_ready"], N + 1)
                    for w, (b_t, read) in enumerate(((b_t0, ("qbd0_ready", "qbd1_ready")), (b_t1, ("kt_ready",)))):
                        for r in read:
                            wait(pe, s[r], capped(N + 2, base + NT))
                        wait(pe, s["pt0_ready" if w == 0 else "pt1_ready"], N)
                        for c in range(PAIRS):
                            at = ((par * 2 + w) * PAIRS + c) * P
                            ins = pe.transpose(b_t[:, c * P:(c + 1) * P], probs[:, at:at + P], ident)
                        ins.then_inc(s[f"pt{w}_done"], 1)

                def weigh_values(n, par):
                    N = base + n
                    wait(pe, s["vmix_ready"], N + 1)
                    wait(pe, s["vcur_ready"], capped(N + 2, base + NT))
                    wait(pe, s["ot_ready"], N)
                    for w, vals in enumerate((v_mix, v_cur)):
                        wait(pe, s[f"pt{w}_ready"], N + 1)
                        for h in range(AH):
                            c, h2 = h // 2, h % 2
                            at = (w * PAIRS + c) * P + h2 * W
                            ins = mm(b_v[h2 * DH:(h2 + 1) * DH, c * P + w * W:c * P + (w + 1) * W],
                                     vals[:, par * INNER + h * DH:par * INNER + (h + 1) * DH],
                                     probs_t[:, at:at + W])
                    ins.then_inc(s["pv_done"], 1)

                def project_o(n, par):
                    N = base + n
                    wait(pe, s["ot_ready"], N + 1)
                    wait(pe, s["z_ready"], N)
                    for c in range(PAIRS):
                        at = (par * PAIRS + c) * P
                        ins = mm(b_m[:, P:2 * P], o_t[:, at:at + P],
                                 wo_sb[:, (l * PAIRS + c) * D:(l * PAIRS + c + 1) * D],
                                 start=(c == 0), stop=(c == PAIRS - 1))
                    ins.then_inc(s["wo_done"], 1)

                def shift_rows(n, par):
                    N = base + n
                    wait(pe, s["mid_ready"], N + 1)
                    o = b_m[:, 2 * P:2 * P + D // 2]
                    mm(o, shift, middle[:, bass.ds((n + 2) * D + D // 2, D // 2)], stop=False)
                    mm(o, carry, middle[:, bass.ds(n * D + D // 2, D // 2)], start=False
                       ).then_inc(s["hs_done"], 1)

                def transpose_z(n, par):
                    N = base + n
                    wait(pe, s["zn_ready"], N + 1)
                    wait(pe, s["ht_ready"], capped(N + 5, base + NT))
                    pe.transpose(b_m[:, 3 * P:4 * P], zn[:, par * P:(par + 1) * P], ident).then_inc(s["zt_done"], 1)

                def attn_step(k, par):
                    staged(project_qk, k, par, 1)
                    staged(transpose_qk, k, par, 0)
                    staged(transpose_in, k, par, 2)
                    staged(transpose_probs, k, par, -1)
                    staged(scores, k, par, 0, 0)
                    staged(transpose_z, k, par, -2)
                    staged(weigh_values, k, par, -1)
                    staged(scores, k, par, 0, 1)
                    staged(project_o, k, par, -1)
                    staged(project_v, k, par, 1)
                    staged(shift_rows, k, par, -1)
                iterate(pe, attn_step)

                if l == 0:
                    pe.wait_ge(d["d_ffn"], 16 * 7)
                pe.wait_ge(s["z_ready"], base + NT)
                NG = NT // GROUP
                FB = GROUP * P
                for g in range(NG + 1):
                    G = l * NG + g
                    if g < NG:
                        for j in range(NJ):
                            wait(pe, s["hid_ready"], (G - 1) * NJ + j + 1)
                            for half in (1, 0):
                                at = l * 2 * HID + half * HID + j * P
                                ins = mm(bank[2 * j + half][0:ROWS[j], :], w1_sb[:, at:at + ROWS[j]],
                                         z_t[:, g * FB:(g + 1) * FB])
                            ins.then_inc(s["h1_done"], 1)
                    if g:
                        G -= 1
                        wait(pe, s["hid_ready"], (G + 1) * NJ)
                        for half in range(2):
                            wait(pe, s["ffn_ready"], 2 * (G - 1) + half + 1)
                            for i in (2 * half, 2 * half + 1):
                                o = bank[6 + half][:, (i % 2) * P:(i % 2 + 1) * P]
                                for j in range(NJ):
                                    K = P if j < NJ - 1 else ROWS[j] + 1
                                    at = ((G % 2) * NJ + j) * FB + i * P
                                    ins = mm(o, hid[0:K, at:at + P],
                                             w2_sb[0:K, (l * NJ + j) * D:(l * NJ + j + 1) * D],
                                             start=(j == 0), stop=(j == NJ - 1))
                            ins.then_inc(s["h2_done"], 1)
                if l + 1 < DEPTH:
                    pe.wait_ge(s["ffn_ready"], 2 * NG * (l + 1))

        @block.scalar
        def _(act):
            act.preload_act_table_set("natural_log_exp_and_others")

            def rstd(dst, mid, var, mid_sem, dst_sem, count, width=1, scale=1.0):
                act.activation(mid, var, ACT.Ln, bias=eps_col, scale=scale).then_inc(mid_sem, 1)
                wait(act, mid_sem, count)
                act.activation(dst, mid, ACT.Exp, scale=-0.5).then_inc(dst_sem, 1)

            b_xt, b_qk, b_vg, b_at, b_kv, b_o, b_og, b_y = bank

            def rstd_of_x(n, par):
                wait(act, s["x_aggr"], n + 1)
                rstd(rstd_x[:, par:par + 1], ln_x[:, par:par + 1], mv_x[:, 2 * par + 1:2 * par + 2],
                     s["x_ln"], s["x_rstd"], n + 1)

            def copy_xn_t(n, par):
                wait(act, s["xt_done"], n + 1)
                wait(act, s["gk_done"], n - 1)
                act.activation(xn_t[:, par * P:(par + 1) * P], b_xt[:, 0:P], ACT.Copy).then_inc(s["xnt_ready"], 1)

            def copy_v(n, par):
                wait(act, s["vg_done"], n + 1)
                wait(act, s["go_done"], n - 1)
                act.activation(v_sb[:, par * GV:(par + 1) * GV], b_vg[:, 0:GV], ACT.Copy).then_inc(s["v_ready"], 1)
                act.activation(eg[:, :], b_vg[:, GV:2 * GV], ACT.Exp, scale=-1.0).then_inc(s["eg_ready"], 1)

            def copy_low(n, par):
                wait(act, s["proj_done"], n + 1)
                act.activation(low[0:RANK, :], b_qk[0:RANK, 3 * P:4 * P], ACT.Copy).then_inc(s["low_ready"], 1)

            def log_gate(n, par):
                wait(act, s["gk_done"], n + 1)
                wait(act, s["gmin_ready"], n)
                act.activation(gkb[:, :], b_qk[:, 2 * P:3 * P], ACT.Identity, bias=bgk2_col).then_inc(s["gkb_ready"], 1)
                wait(act, s["gkb_ready"], n + 1)
                act.activation(gk_abs[:, :], gkb[:, :], ACT.Abs).then_inc(s["gabs_ready"], 1)
                wait(act, s["gabs_ready"], n + 1)
                act.activation(gk_exp[:, :], gk_abs[:, :], ACT.Exp, scale=-1.0).then_inc(s["gexp_ready"], 1)
                wait(act, s["gexp_ready"], n + 1)
                wait(act, s["logsig_ready"], n)
                act.activation(gk_ln[:, :], gk_exp[:, :], ACT.Ln, bias=1.0).then_inc(s["gln_ready"], 1)

            def decays(n, par):
                wait(act, s["last_ready"], n + 1)
                wait(act, s["qg_ready"], n)
                act.activation(dec_q[:, :], cum[:, :], ACT.Exp, scale=GATE).then_inc(s["decq_ready"], 1)
                wait(act, s["kd_ready"], n)
                act.activation(dec_k[:, :], cum[:, :], ACT.Exp, scale=-GATE).then_inc(s["deck_ready"], 1)
                wait(act, s["kg_ready"], n)
                wait(act, s["s2_ready"], n - 1)
                for c in range(2):
                    act.activation(dec_g[:, c * CH:(c + 1) * CH], cum[:, c * CH:(c + 1) * CH], ACT.Exp,
                                   scale=-GATE, bias=last16[:, c:c + 1])
                act.activation(dlast[:, 2 * par:2 * par + 2], last16[:, :], ACT.Exp).then_inc(s["decg_ready"], 1)

            def copy_kg(n, par):
                wait(act, s["kgt_done"], n + 1)
                wait(act, s["kv_done"], n - 1)
                for c in range(2):
                    at = (par * 2 + c) * P
                    ins = act.activation(kg_tok[c * CH:(c + 1) * CH, at:at + P], b_kv[c * CH:(c + 1) * CH, 0:P], ACT.Copy)
                ins.then_inc(s["kgtok_ready"], 1)

            def square_o(n, par):
                wait(act, s["go_done"], n + 1)
                wait(act, s["oss_ready"], n)
                act.activation(o_sq[:, :], b_o[:, 0:GV], ACT.Square).then_inc(s["osq_ready"], 1)

            def rstd_of_o(n, par):
                wait(act, s["oss_ready"], n + 1)
                wait(act, s["og1_ready"], n)
                rstd(o_r[:, :], o_ln[:, :], o_ss[:, :], s["oln_ready"], s["or_ready"], n + 1, scale=1.0 / GDV)

            def rstd_of_y(n, par):
                wait(act, s["y_aggr"], n + 1)
                rstd(rstd_y[:, :], ln_y[:, :], mv_y[:, 1:2], s["y_ln"], s["y_rstd"], n + 1)

            def rstd_of_f(n, par):
                wait(act, s["f_aggr"], n + 1)
                rstd(rstd_f[:, :], ln_f[:, :], mv_f[:, 1:2], s["f_ln"], s["f_rstd"], n + 1)

            def gla_step(k, par):
                staged(copy_kg, k, par, 0)
                staged(rstd_of_x, k, par, 2)
                staged(rstd_of_y, k, par, -1)
                staged(copy_v, k, par, 1)
                staged(copy_low, k, par, 1)
                staged(log_gate, k, par, 1)
                staged(rstd_of_f, k, par, -1)
                staged(square_o, k, par, 0)
                staged(decays, k, par, 1)
                staged(rstd_of_o, k, par, 0)
                staged(copy_xn_t, k, par, 2)

            act.wait_ge(d["d_cols"], 13 * 16)
            act.wait_ge(s["col_consts"], 2)
            act.wait_ge(s["zero_dve"], 1)
            iterate(act, gla_step)

            act.wait_ge(s["zero_pool"], 1)
            for l in range(DEPTH):
                base = NT * l
                b_q, b_k, b_v, b_t0, b_t1, b_s0, b_s1, b_m = bank

                def copy_h_t(n, par):
                    N = base + n
                    o = h_t[:, par * (P + 1):(par + 1) * (P + 1)]
                    wait(act, s["v_done"], N - 1)
                    if l and isinstance(n, int) and n == 0:
                        act.wait_ge(s["carry_zero"], l)
                    act.activation(o[D // 2:P, 0:1], o[D // 2:P, P:P + 1], ACT.Copy).then_inc(s["carried"], 1)
                    wait(act, s["xtr_done"], N + 1)
                    wait(act, s["carried"], N + 1)
                    act.activation(o[0:D // 2, 0:P], b_m[0:D // 2, 0:P], ACT.Copy)
                    act.activation(o[D // 2:P, 1:P + 1], b_m[D // 2:P, 0:P], ACT.Copy).then_inc(s["ht_ready"], 1)

                def squares(n, par):
                    N = base + n
                    wait(act, s["qk_done"], N + 1)
                    wait(act, s["ss_ready"], N)
                    act.activation(sq[:, 0:INNER], b_q[:, :], ACT.Square)
                    act.activation(sq[:, INNER:2 * INNER], b_k[:, :], ACT.Square).then_inc(s["sq_ready"], 1)

                def inverse_norms(n, par):
                    N = base + n
                    wait(act, s["ssc_ready"], N + 1)
                    act.activation(ss_ln[:, :], ssc[:, :], ACT.Ln, scale=float(2 ** 30)).then_inc(s["ssl_ready"], 1)
                    wait(act, s["ssl_ready"], N + 1)
                    wait(act, s["qn_ready"], N)
                    act.activation(inv[:, :], ss_ln[:, :], ACT.Exp, scale=-0.5, bias=norm_bias_col
                                   ).then_inc(s["inv_ready"], 1)

                def copy_q_bd(n, par):
                    N = base + n
                    wait(act, s["qt_done"], N + 1)
                    wait(act, s["sc1_done"], N - 1)
                    dst, src = q_blocks(par, b_t0, 1)
                    act.activation(dst, src, ACT.Copy).then_inc(s["qbd1_ready"], 1)

                def copy_k_t(n, par):
                    N = base + n
                    wait(act, s["kt_done"], N + 1)
                    wait(act, s["kprev_ready"], N + 1)
                    kv = k_t[:, par * PAIRS * KC:(par + 1) * PAIRS * KC].rearrange("p (c k) -> p c k", k=KC)
                    act.activation(kv[:, :, 0:P], b_t1[:, :].rearrange("p (c k) -> p c k", k=P), ACT.Copy
                                   ).then_inc(s["kt_ready"], 1)

                def exponentials(n, par, w):
                    N = base + n
                    wait(act, s[f"max{w}_ready"], N + 1)
                    wait(act, s["pt1_done"], N - 1)
                    b_s = (b_s0, b_s1)[w]
                    for c in range(PAIRS):
                        at = ((par * 2 + w) * PAIRS + c) * P
                        r = (par * 2 + w) * PAIRS + c
                        ins = act.activation(probs[:, at:at + P], b_s[:, c * P:(c + 1) * P], ACT.Exp,
                                             bias=neg_max[:, w * PAIRS + c:w * PAIRS + c + 1],
                                             accum_out=row_sum[:, r:r + 1])
                    ins.then_inc(s[f"p{w}_ready"], 1)

                def copy_probs_t(n, par):
                    N = base + n
                    wait(act, s["pt0_done"], N + 1)
                    wait(act, s["pv_done"], N)
                    act.activation(probs_t[:, 0:PAIRS * P], b_t0[:, :], ACT.Copy).then_inc(s["pt0_ready"], 1)

                def copy_o_t(n, par):
                    N = base + n
                    wait(act, s["pv_done"], N + 1)
                    wait(act, s["wo_done"], N - 1)
                    act.activation(o_t[:, par * PAIRS * P:(par + 1) * PAIRS * P], b_v[:, :], ACT.Copy
                                   ).then_inc(s["ot_ready"], 1)

                def copy_v_cur(n, par):
                    N = base + n
                    wait(act, s["v_done"], N + 1)
                    wait(act, s["vup_ready"], N + 1)
                    wait(act, s["vmix_ready"], N - 1)
                    act.activation(v_cur[:, par * INNER:(par + 1) * INNER], b_v[:, :], ACT.Copy
                                   ).then_inc(s["vcur_ready"], 1)

                def copy_shifted(n, par):
                    N = base + n
                    wait(act, s["zn_ready"], N - 1)
                    wait(act, s["hs_done"], N + 1)
                    act.activation(hcat[:, par * P:par * P + D // 2],
                                   middle[:, bass.ds((n + 2) * D, D // 2)], ACT.Copy)
                    act.activation(hcat[:, par * P + D // 2:(par + 1) * P], b_m[:, 2 * P:2 * P + D // 2], ACT.Copy
                                   ).then_inc(s["hs_ready"], 1)

                def rstd_of_z(n, par):
                    N = base + n
                    wait(act, s["z_aggr"], N + 1)
                    rstd(rstd_z[:, :], ln_z[:, :], mv_z[:, 1:2], s["z_ln"], s["z_rstd"], N + 1)

                def copy_z_t(n, par):
                    N = base + n
                    wait(act, s["zt_done"], N + 1)
                    act.activation(z_t[:, bass.ds(n * P, P)], b_m[:, 3 * P:4 * P], ACT.Identity,
                                   bias=lnb_col[l], scale=lng_col[l]).then_inc(s["z_ready"], 1)

                def attn_step(k, par):
                    staged(squares, k, par, 1)
                    staged(copy_q_bd, k, par, 0)
                    staged(copy_k_t, k, par, 0)
                    staged(copy_h_t, k, par, 2)
                    staged(inverse_norms, k, par, 1)
                    staged(copy_probs_t, k, par, -1)
                    staged(copy_z_t, k, par, -2)
                    staged(copy_o_t, k, par, -1)
                    staged(exponentials, k, par, 0, 0)
                    staged(exponentials, k, par, 0, 1)
                    staged(copy_v_cur, k, par, 1)
                    staged(copy_shifted, k, par, -1)
                    staged(rstd_of_z, k, par, -1)
                iterate(act, attn_step)

                NG = NT // GROUP
                FB = GROUP * P
                for g in range(NG):
                    for j in range(NJ):
                        i = (l * NG + g) * NJ + j
                        act.wait_ge(s["h1_done"], i + 1)
                        wait(act, s["hid_ready"], i - 1)
                        act.activation(gelu[0:ROWS[j], (i % 2) * FB:(i % 2 + 1) * FB],
                                       bank[2 * j + 1][0:ROWS[j], :], ACT.Gelu, bias=b1_col(l, 1, j)
                                       ).then_inc(s["gelu_ready"], 1)
                act.preload_act_table_set("natural_log_exp_and_others")

            act.wait_ge(s["mvo_ready"], 1)
            rstd(rstd_o[:, :], ln_o[:, :], mv_o[:, 1:2 * NT:2], s["lno_ready"], s["rstdo_ready"], 1)

        @block.vector
        def _(dve):
            for buf in (qg, kg_tok, a_t, state):
                dve.memset(buf[:, :], 0.0)
            dve.memset(eps_col, EPS).then_inc(s["col_consts"], 1)
            dve.memset(norm_bias_col, 15 * LN2).then_inc(s["col_consts"], 1)
            dve.memset(st_x[:, :], 0.0).then_inc(s["zero_dve"], 1)
            dve.wait_ge(s["zero_dve"], 1)
            dve.wait_ge(d["d_const"], 16)
            dve.tensor_copy(ident_bf[:, :], ident).then_inc(s["cast_consts"], 1)
            dve.tensor_copy(masks_bf[:, :], consts[:, 3 * P:6 * P]).then_inc(s["cast_consts"], 1)
            b_xt, b_qk, b_vg, b_at, b_kv, b_o, b_og, b_y = bank

            def stats_x(n, par):
                if isinstance(n, int) and n == 0:
                    dve.wait_ge(d["d_x0"], 16)
                if isinstance(n, int) and n == B:
                    dve.wait_ge(d["d_x1"], 16 * B)
                st = st_x[:, 6 * par:6 * par + 6]
                dve.bn_stats(st, tile_of(x_in, n)).then_inc(s["x_stats"], 1)
                wait_apart(dve, (s["x_stats"], n + 1))
                dve.bn_aggr(mv_x[:, 2 * par:2 * par + 2], st).then_inc(s["x_aggr"], 1)

            def normalise_x(n, par):
                wait(dve, s["x_rstd"], n + 1)
                wait(dve, s["xt_done"], n - 1)
                dve.tensor_scalar(xn[:, par * P:(par + 1) * P], tile_of(x_in, n), mv_x[:, 2 * par:2 * par + 1],
                                  rstd_x[:, par:par + 1], ALU.subtract, ALU.mult).then_inc(s["xn_ready"], 1)

            def gate_silu(n, par):
                wait(dve, s["eg_ready"], n + 1)
                dve.tensor_scalar(eg1[:, :], eg[:, :], 1.0, None, ALU.add).then_inc(s["eg1_ready"], 1)
                wait(dve, s["eg1_ready"], n + 1)
                dve.reciprocal(rec[:, :], eg1[:, :]).then_inc(s["rec_ready"], 1)
                wait(dve, s["rec_ready"], n + 1)
                dve.tensor_tensor(silu[:, par * GV:(par + 1) * GV], b_vg[:, GV:2 * GV], rec[:, :], ALU.mult
                                  ).then_inc(s["silu_ready"], 1)

            def gate_sums(n, par):
                wait(dve, s["gkb_ready"], n + 1)
                dve.tensor_scalar(gk_min[:, :], gkb[:, :], 0.0, None, ALU.min).then_inc(s["gmin_ready"], 1)
                wait(dve, s["gmin_ready"], n + 1)
                wait(dve, s["gln_ready"], n + 1)
                dve.tensor_tensor(logsig[:, :], gk_min[:, :], gk_ln[:, :], ALU.subtract).then_inc(s["logsig_ready"], 1)
                wait(dve, s["logsig_ready"], n + 1)
                wait(dve, s["decg_ready"], n)
                dve.tensor_tensor_scan(cum[:, :], keep, logsig[:, :], 0.0, ALU.mult, ALU.add
                                       ).then_inc(s["cum_ready"], 1)
                wait(dve, s["cum_ready"], n + 1)
                dve.tensor_scalar(last16[:, :], cum[:, CH - 1:P:CH], GATE, None, ALU.mult).then_inc(s["last_ready"], 1)

            def decay_qk(n, par):
                wait(dve, s["decq_ready"], n + 1)
                wait(dve, s["proj_done"], n + 1)
                wait(dve, s["go_done"], n - 1)
                for h in range(GH):
                    r = slice(h * GDK, (h + 1) * GDK)
                    ins = dve.scalar_tensor_tensor(out=qg[r, (par * GH + h) * P:(par * GH + h + 1) * P],
                                                   in0=b_qk[r, 0:P], scalar=float(GDK) ** -0.5, in1=dec_q[r, :],
                                                   op0=ALU.mult, op1=ALU.mult)
                ins.then_inc(s["qg_ready"], 1)
                wait(dve, s["deck_ready"], n + 1)
                dve.tensor_tensor(kd[:, par * P:(par + 1) * P], b_qk[:, P:2 * P], dec_k[:, :], ALU.mult
                                  ).then_inc(s["kd_ready"], 1)
                wait(dve, s["decg_ready"], n + 1)
                wait(dve, s["kgt_done"], n)
                dve.tensor_tensor(kg[:, :], b_qk[:, P:2 * P], dec_g[:, :], ALU.mult).then_inc(s["kg_ready"], 1)

            def mask_scores(n, par):
                wait_apart(dve, (s["at_done"], n + 1))
                dve.copy_predicated(a_t[:, par * GH * P:(par + 1) * GH * P].rearrange("p (h t) -> p h t", h=GH),
                                    causal_bits.unsqueeze(1).to_broadcast([P, GH, P]),
                                    b_at[:, :].rearrange("p (h t) -> p h t", h=GH)).then_inc(s["atm_ready"], 1)

            def state_1(n, par):
                wait(dve, s["kv_done"], n + 1)
                wait(dve, s["s2_ready"], n - 1)
                st = state[:, par * 2 * GDV:(par + 1) * 2 * GDV]
                dve.scalar_tensor_tensor(out=st[:, GDV:2 * GDV], in0=st[:, 0:GDV], scalar=dlast[:, 2 * par:2 * par + 1],
                                         in1=b_kv[:, P:P + GDV], op0=ALU.mult, op1=ALU.add).then_inc(s["s1_ready"], 1)

            def state_2(n, par):
                wait(dve, s["go_done"], n + 1)
                wait(dve, s["s1_ready"], n + 1)
                st = state[:, par * 2 * GDV:(par + 1) * 2 * GDV]
                dve.scalar_tensor_tensor(out=st[:, 0:GDV], in0=st[:, GDV:2 * GDV],
                                         scalar=dlast[:, 2 * par + 1:2 * par + 2],
                                         in1=b_kv[:, P + GDV:P + 2 * GDV], op0=ALU.mult, op1=ALU.add
                                         ).then_inc(s["s2_ready"], 1)

            def sum_o(n, par):
                wait(dve, s["osq_ready"], n + 1)
                wait(dve, s["or_ready"], n)
                dve.tensor_reduce(o_ss[:, :], o_sq[:, :].rearrange("p (h v) -> p h v", h=GH), AX.X, ALU.add
                                  ).then_inc(s["oss_ready"], 1)

            def gate_o(n, par):
                wait(dve, s["or_ready"], n + 1)
                dve.tensor_tensor(og1[:, :].rearrange("p (h v) -> p h v", h=GH),
                                  b_o[:, 0:GV].rearrange("p (h v) -> p h v", h=GH),
                                  o_r[:, :].unsqueeze(2).to_broadcast([P, GH, GDV]), ALU.mult).then_inc(s["og1_ready"], 1)
                wait(dve, s["og1_ready"], n + 1)
                wait(dve, s["ogt_done"], n - 1)
                dve.tensor_tensor(og2[:, par * GV:(par + 1) * GV], og1[:, :], silu[:, par * GV:(par + 1) * GV],
                                  ALU.mult).then_inc(s["og2_ready"], 1)

            def scale_o_t(n, par):
                wait(dve, s["ogt_done"], n + 1)
                wait(dve, s["y_done"], n - 1)
                dve.tensor_scalar(og_t[:, par * 2 * P:(par + 1) * 2 * P], b_og[:, 0:2 * P], rms_col, None, ALU.mult
                                  ).then_inc(s["ogt_ready"], 1)

            def stats_y(n, par):
                wait_apart(dve, (s["y_done"], n + 1))
                dve.bn_stats(st_y[:, :], b_y[:, 0:D]).then_inc(s["y_stats"], 1)
                wait_apart(dve, (s["y_stats"], n + 1))
                dve.bn_aggr(mv_y[:, :], st_y[:, :]).then_inc(s["y_aggr"], 1)

            def add_y(n, par):
                wait(dve, s["y_rstd"], n + 1)
                dve.tensor_scalar(yn[:, :], b_y[:, 0:D], mv_y[:, 0:1], rstd_y[:, :], ALU.subtract, ALU.mult
                                  ).then_inc(s["yn_ready"], 1)
                wait(dve, s["yn_ready"], n + 1)
                dve.tensor_tensor(tile_of(x_attn, n), tile_of(x_in, n), yn[:, :], ALU.add).then_inc(s["x1_ready"], 1)
                wait_apart(dve, (s["x1_ready"], n + 1))
                dve.bn_stats(st_f[:, :], tile_of(x_attn, n)).then_inc(s["f_stats"], 1)
                wait_apart(dve, (s["f_stats"], n + 1))
                dve.bn_aggr(mv_f[:, :], st_f[:, :]).then_inc(s["f_aggr"], 1)

            def normalise_f(n, par):
                wait(dve, s["f_rstd"], n + 1)
                dve.tensor_scalar(tile_of(stream[0], n), tile_of(x_attn, n), mv_f[:, 0:1], rstd_f[:, :],
                                  ALU.subtract, ALU.mult).then_inc(s["xf_ready"], 1)

            def gla_step(k, par):
                staged(scale_o_t, k, par, -1)
                staged(mask_scores, k, par, 0)
                staged(stats_x, k, par, 2)
                staged(stats_y, k, par, -1)
                staged(gate_silu, k, par, 1)
                staged(normalise_x, k, par, 2)
                staged(add_y, k, par, -1)
                staged(state_1, k, par, 0)
                staged(gate_sums, k, par, 1)
                staged(normalise_f, k, par, -1)
                staged(state_2, k, par, 0)
                staged(sum_o, k, par, 0)
                staged(decay_qk, k, par, 1)
                staged(gate_o, k, par, 0)

            dve.wait_ge(d["d_cols"], 13 * 16)
            iterate(dve, gla_step)

            dve.wait_ge(d["d_tab"], 2 * 16)
            dve.wait_ge(d["d_scales"], 2 * DEPTH * 16)
            dve.wait_ge(s["zero_pool"], 1)
            for l in range(DEPTH):
                base = NT * l
                b_q, b_k, b_v, b_t0, b_t1, b_s0, b_s1, b_m = bank

                if l:
                    dve.wait_ge(s["rot2_ready"], base)
                sc = scales[:, l * 2 * DH:(l + 1) * 2 * DH]
                sc_b = sc.unsqueeze(1).to_broadcast([P, TILES_PER_BATCH, 2 * DH])
                dve.tensor_tensor(cos_t[:, :].rearrange("p (t c) -> p t c", c=2 * DH),
                                  cos_base[:, :].rearrange("p (t c) -> p t c", c=2 * DH), sc_b, ALU.mult
                                  ).then_inc(s["cos_ready"], 1)
                for i in range(2):
                    swapped = sc[:, i * DH:(i + 1) * DH].rearrange("p (e r) -> p e r", e=2)[:, ::-1, :]
                    ins = dve.tensor_tensor(
                        sin_t[:, :].rearrange("p (t c e r) -> p t c e r", c=2, e=2, r=DH // 2)[:, :, i],
                        sin_base[:, :].rearrange("p (t c e r) -> p t c e r", c=2, e=2, r=DH // 2)[:, :, i],
                        swapped.unsqueeze(1).to_broadcast([P, TILES_PER_BATCH, 2, DH // 2]), ALU.mult)
                ins.then_inc(s["table_ready"], 1)
                dve.wait_ge(s["table_ready"], l + 1)

                def sum_squares(n, par):
                    N = base + n
                    wait(dve, s["sq_ready"], N + 1)
                    dve.tensor_reduce(ss[:, :], sq[:, :].rearrange("p (h e) -> p h e", e=DH), AX.X, ALU.add
                                      ).then_inc(s["ss_ready"], 1)
                    wait(dve, s["ss_ready"], N + 1)
                    dve.tensor_scalar(ssc[:, :], ss[:, :], 1e-24, None, ALU.max).then_inc(s["ssc_ready"], 1)

                def normalise_qk(n, par):
                    N = base + n
                    wait(dve, s["inv_ready"], N + 1)
                    wait(dve, s["rot2_ready"], N)
                    for i, b_x in enumerate((b_q, b_k)):
                        ins = dve.tensor_tensor(
                            qn[:, i * INNER:(i + 1) * INNER].rearrange("p (h e) -> p h e", e=DH),
                            b_x[:, :].rearrange("p (h e) -> p h e", e=DH),
                            inv[:, i * AH:(i + 1) * AH].unsqueeze(2).to_broadcast([P, AH, DH]), ALU.mult)
                    ins.then_inc(s["qn_ready"], 1)

                def rotate_cos(n, par):
                    N = base + n
                    wait(dve, s["qn_ready"], N + 1)
                    for i in range(2):
                        tab = cos_t[:, bass.ds((n - par) * DH + i * DH, DH)]
                        ins = dve.tensor_tensor(
                            rot1[:, i * INNER:(i + 1) * INNER].rearrange("p (h e) -> p h e", e=DH),
                            qn[:, i * INNER:(i + 1) * INNER].rearrange("p (h e) -> p h e", e=DH),
                            tab.unsqueeze(1).to_broadcast([P, AH, DH]), ALU.mult)
                    ins.then_inc(s["rot1_ready"], 1)

                def rotate_add(n, par):
                    N = base + n
                    wait(dve, s["rot1_ready"], N + 1)
                    wait(dve, s["rot2_ready"], N + 1)
                    wait(dve, s["kt_done"], N - 1)
                    dve.tensor_tensor(qr[:, par * 2 * INNER:(par + 1) * 2 * INNER], rot1[:, :], rot2[:, :], ALU.add
                                      ).then_inc(s["qr_ready"], 1)

                def copy_q_bd(n, par):
                    N = base + n
                    wait(dve, s["qt_done"], N + 1)
                    wait(dve, s["sc1_done"], N - 1)
                    dst, src = q_blocks(par, b_t0, 0)
                    dve.tensor_copy(dst, src).then_inc(s["qbd0_ready"], 1)

                def row_max(n, par, w):
                    N = base + n
                    wait(dve, s[f"sc{w}_done"], N + 1)
                    wait(dve, s[f"p{w}_ready"], N)
                    dve.tensor_reduce(neg_max[:, w * PAIRS:(w + 1) * PAIRS],
                                      (b_s0, b_s1)[w][:, :].rearrange("p (c k) -> p c k", c=PAIRS),
                                      AX.X, ALU.max, negate=True).then_inc(s[f"max{w}_ready"], 1)

                def row_reciprocals(n, par):
                    N = base + n
                    wait(dve, s["p0_ready"], N + 1)
                    wait(dve, s["p1_ready"], N + 1)
                    wait(dve, s["pn_ready"], N)
                    dve.reciprocal(row_rec[:, :], row_sum[:, par * 2 * PAIRS:(par + 1) * 2 * PAIRS]
                                   ).then_inc(s["rec_sum_ready"], 1)

                def copy_probs_t(n, par):
                    N = base + n
                    wait(dve, s["pt1_done"], N + 1)
                    wait(dve, s["pv_done"], N)
                    dve.tensor_copy(probs_t[:, PAIRS * P:2 * PAIRS * P], b_t1[:, :]).then_inc(s["pt1_ready"], 1)

                def add_attention(n, par):
                    N = base + n
                    wait(dve, s["wo_done"], N + 1)
                    dve.tensor_tensor(middle[:, bass.ds((n + 2) * D, D)], b_m[:, P:2 * P], tile_of(stream[l], n),
                                      ALU.add).then_inc(s["mid_ready"], 1)

                def stats_z(n, par):
                    N = base + n
                    wait_apart(dve, (s["hs_ready"], N + 1))
                    dve.bn_stats(st_z[:, :], hcat[:, par * P:(par + 1) * P]).then_inc(s["z_stats"], 1)
                    wait_apart(dve, (s["z_stats"], N + 1))
                    dve.bn_aggr(mv_z[:, :], st_z[:, :]).then_inc(s["z_aggr"], 1)

                def normalise_z(n, par):
                    N = base + n
                    wait(dve, s["z_rstd"], N + 1)
                    wait(dve, s["zt_done"], N - 1)
                    dve.tensor_scalar(zn[:, par * P:(par + 1) * P], hcat[:, par * P:(par + 1) * P], mv_z[:, 0:1],
                                      rstd_z[:, :], ALU.subtract, ALU.mult).then_inc(s["zn_ready"], 1)

                def attn_step(k, par):
                    staged(normalise_z, k, par, -2)
                    staged(copy_q_bd, k, par, 0)
                    staged(sum_squares, k, par, 1)
                    staged(normalise_qk, k, par, 1)
                    staged(copy_probs_t, k, par, -1)
                    staged(row_max, k, par, 0, 0)
                    staged(rotate_cos, k, par, 1)
                    staged(row_max, k, par, 0, 1)
                    staged(add_attention, k, par, -1)
                    staged(rotate_add, k, par, 1)
                    staged(row_reciprocals, k, par, 0)
                    staged(stats_z, k, par, -1)
                iterate(dve, attn_step)

                NG = NT // GROUP
                FB = GROUP * P
                last = l == DEPTH - 1

                def add_ffn(g):
                    G = l * NG + g
                    for half in range(2):
                        n0 = g * GROUP + 2 * half
                        dve.wait_ge(s["h2_done"], 2 * G + half + 1)
                        dve.tensor_tensor(stream[l + 1][:, n0 * D:(n0 + 2) * D], bank[6 + half][:, 0:2 * D],
                                          middle[:, (n0 + 2) * D:(n0 + 4) * D], ALU.add
                                          ).then_inc(s["ffn_ready"], 1)
                        if last:
                            dve.wait_ge(s["ffn_ready"], 2 * G + half + 1)
                            for n in (n0, n0 + 1):
                                dve.bn_stats(st_o[:, 6 * n:6 * n + 6], tile_of(stream[l + 1], n)).then_inc(s["sto_ready"], 1)

                for g in range(NG):
                    for j in range(NJ):
                        i = (l * NG + g) * NJ + j
                        dve.wait_ge(s["gelu_ready"], i + 1)
                        if g < 2 and j == 0:
                            dve.wait_ge(s["ones_ready"], l + 1)
                        if j == 0:
                            wait(dve, s["h2_done"], 2 * (l * NG + g - 1))
                        at = (((l * NG + g) % 2) * NJ + j) * FB
                        dve.scalar_tensor_tensor(out=hid[0:ROWS[j], at:at + FB], in0=bank[2 * j][0:ROWS[j], :],
                                                 scalar=b1_col(l, 0, j),
                                                 in1=gelu[0:ROWS[j], (i % 2) * FB:(i % 2 + 1) * FB],
                                                 op0=ALU.add, op1=ALU.mult).then_inc(s["hid_ready"], 1)
                    if g:
                        add_ffn(g - 1)
                add_ffn(NG - 1)

            dve.wait_ge(s["sto_ready"], NT)
            for n in range(NT):
                ins = dve.bn_aggr(mv_o[:, 2 * n:2 * n + 2], st_o[:, 6 * n:6 * n + 6])
            ins.then_inc(s["mvo_ready"], 1)
            dve.wait_ge(s["rstdo_ready"], 1)
            for n in range(NT):
                ins = dve.tensor_scalar(tile_of(xo, n), tile_of(stream[DEPTH], n), mv_o[:, 2 * n:2 * n + 1],
                                        rstd_o[:, n:n + 1], ALU.subtract, ALU.mult)
                if n % GROUP == GROUP - 1:
                    ins.then_inc(s["xo_ready"], 1)
                    g = n // GROUP
                    c = slice(g * GROUP * D, (g + 1) * GROUP * D)
                    dve.wait_ge(s["xo_ready"], 1 + g)
                    dve.tensor_tensor(res[:, c], xo[:, c], x_attn[:, c], ALU.add).then_inc(s["res_ready"], 1)


def square_constants():
    import numpy as np
    i = np.arange(128)
    ident = (i[:, None] == i[None, :])
    shift = (i[:, None] + 1 == i[None, :])
    carry = (i[:, None] == 127) & (i[None, :] == 0)
    q = i[:, None] % 64
    k = i[None, :] % 64
    second = i[None, :] >= 64
    low = np.float32(-1e30)
    mask_b = np.where(np.where(second, k <= q, k >= q), np.float32(0), low)
    mask_a = np.where(np.where(second, k >= q, k <= q), np.float32(0), low)
    mask_a0 = np.where(~second & (k <= q), np.float32(0), low)
    causal = (i[:, None] // 64 == i[None, :] // 64) & (i[:, None] <= i[None, :])
    keep = np.broadcast_to(i[None, :] % 64 != 0, (128, 128))
    return np.concatenate([np.asarray(a, np.float32) for a in
                           (ident, shift, carry, mask_a, mask_b, mask_a0, causal, keep)], axis=1)


def rotary_tables(n, dh, window, qk_scale):
    import numpy as np
    half = np.arange(0, dh, 2, dtype=np.float32)
    freq = (np.float32(1.0) / np.power(np.float32(10000.0), half / np.float32(dh))).astype(np.float32)
    t = np.arange(n, dtype=np.float32)
    f = (t[:, None] * freq[None, :]).astype(np.float32).astype(np.float64)
    f = np.concatenate([f, f], axis=-1)
    base = ((half + np.float32(0.4 * dh)) / np.float32(1.4 * dh)).astype(np.float64)
    power = (t - n // 2).astype(np.float64) / (window // 2)
    sc = base[None, :] ** power[:, None]
    sc = np.concatenate([sc, sc], axis=-1)
    sign = np.where(np.arange(dh) < dh // 2, -1.0, 1.0)
    tabs = []
    for g in (np.cos(f), np.sin(f) * sign):
        both = np.stack([g * sc * qk_scale, g / sc], axis=1)
        tabs.append(np.ascontiguousarray(both.reshape(n // 128, 128, 2 * dh).transpose(1, 0, 2)
                                         .reshape(128, -1).astype(np.float32)))
    return tabs


_INS = ["L0_attn_x", "L0_attn_Wq", "L0_attn_Wk", "L0_attn_Wv", "L0_attn_Wg", "L0_attn_Wgk1", "L0_attn_Wgk2",
        "L0_attn_bgk2", "L0_attn_Wo", "L0_attn_rms_w", "L0_ffn_wqkv", "L0_ffn_q_scale", "L0_ffn_k_scale",
        "L0_ffn_wo", "L0_ffn_ln_g", "L0_ffn_ln_b", "L0_ffn_w1", "L0_ffn_b1", "L0_ffn_w2", "L0_ffn_b2"]


def kernel(**inputs):
    import numpy as np
    import concourse.bacc as bacc
    from concourse.bass_utils import run_bass_kernel_spmd

    nc = bacc.Bacc("TRN2", target_bir_lowering=False, num_devices=1)
    arrays = {f"in_{name}": np.ascontiguousarray(inputs[name]) for name in _INS}
    arrays["square_consts"] = square_constants()
    arrays["rotary_cos"], arrays["rotary_sin"] = rotary_tables(arrays["in_L0_attn_x"].shape[1], 64, 64, 8.0)
    args = [nc.dram_tensor(name, a.shape, mybir.dt.from_np(a.dtype), kind="ExternalInput").ap()
            for name, a in arrays.items()]
    shape = arrays["in_L0_attn_x"].shape
    args.append(nc.dram_tensor("out_x", shape, F32, kind="ExternalOutput").ap())
    build_program(nc, *args)
    r = run_bass_kernel_spmd(nc, [arrays], core_ids=[0])
    return r.results[0]["out_x"]
```

```python
from contextlib import ExitStack

import concourse.bass as bass
from concourse import mybir

F32 = mybir.dt.float32
BF16 = mybir.dt.bfloat16
U32 = mybir.dt.uint32
ALU = mybir.AluOpType
ACT = mybir.ActivationFunctionType
AX = mybir.AxisListType

P = 128
EPS = 1e-5
LN2 = 0.6931471805599453


def wait(engine, semaphore, count):
    if isinstance(count, int) and count <= 0:
        return
    engine.wait_ge(semaphore, count)


def build_program(nc, x, Wq, Wk, Wv, Wg, Wgk1, Wgk2, bgk2, Wo, rms_w,
                  wqkv, q_scale, k_scale, wo, ln_g, ln_b, w1, b1, w2, b2,
                  square_consts, rotary_cos, rotary_sin, out):
    B, T, D = x.shape
    TILES_PER_BATCH = T // P
    NT = B * TILES_PER_BATCH
    GH, GDK, GDV = 4, Wq.shape[1] // 4, Wv.shape[1] // 4
    GV = GH * GDV
    RANK = Wgk1.shape[1]
    CH = 64
    GATE = 1.0 / 16.0
    DEPTH, _, QKV = wqkv.shape
    INNER = QKV // 3
    DH = q_scale.shape[1]
    AH = INNER // DH
    PAIRS = AH // 2
    W = 64
    HID = w2.shape[1]
    NJ = (HID + P - 1) // P
    ROWS = [min(P, HID - j * P) for j in range(NJ)]
    GROUP = 4
    assert B == 2 and D == P and 2 * CH == P and 2 * W == P

    ctx = ExitStack()
    with ctx:
        def sb(name, cols, dt=F32):
            return ctx.enter_context(nc.sbuf_tensor(name, [P, cols], dt))

        def sems(names):
            return {k: ctx.enter_context(nc.semaphore(k)) for k in names.split()}

        bank = [ctx.enter_context(nc.psum_tensor(f"bank{i}", [P, 512], F32)) for i in range(8)]

        consts = sb("consts", 8 * P)
        ident, shift, carry, mask_a, mask_b, mask_a0, causal, keep = (
            consts[:, i * P:(i + 1) * P] for i in range(8))
        causal_bits = causal.bitcast(U32)
        ident_bf = sb("ident_bf", P, BF16)
        masks_bf = sb("masks_bf", 3 * P, BF16)
        cos_base = sb("cos_base", TILES_PER_BATCH * 2 * DH)
        sin_base = sb("sin_base", TILES_PER_BATCH * 2 * DH)
        cos_t = sb("cos_t", TILES_PER_BATCH * 2 * DH)
        sin_t = sb("sin_t", TILES_PER_BATCH * 2 * DH)
        scales = sb("scales", DEPTH * 2 * DH)
        wqk_sb = sb("wqk_sb", 2 * P)
        wvg_sb = sb("wvg_sb", 2 * GV)
        wgk1_sb = sb("wgk1_sb", RANK)
        wgk2_sb = sb("wgk2_sb", P)
        wout_sb = sb("wout_sb", 2 * D)
        columns = sb("columns", 4 + 2 * DEPTH + DEPTH * 2 * NJ)
        bgk2_col, rms_col = columns[:, 0:1], columns[:, 1:2]
        eps_col, norm_bias_col = columns[:, 2:3], columns[:, 3:4]
        lng_col = [columns[:, 4 + l:5 + l] for l in range(DEPTH)]
        lnb_col = [columns[:, 4 + DEPTH + l:5 + DEPTH + l] for l in range(DEPTH)]
        B1_AT = 4 + 2 * DEPTH
        wqkv_sb = sb("wqkv_sb", DEPTH * QKV)
        wo_sb = sb("wo_sb", DEPTH * PAIRS * D)
        w1_sb = sb("w1_sb", DEPTH * 2 * HID)
        w2_sb = sb("w2_sb", DEPTH * NJ * D)

        def b1_col(l, half, j):
            at = B1_AT + (l * 2 + half) * NJ + j
            return columns[0:ROWS[j], at:at + 1]

        x_in = sb("x_in", NT * D)
        x_attn = sb("x_attn", NT * D)
        ping, pong = sb("ping", NT * D), sb("pong", NT * D)
        stream = [(ping, pong)[l % 2] for l in range(DEPTH + 1)]
        middle = sb("middle", (NT + 2) * D)
        z_t = sb("z_t", NT * P)

        def tile_of(buf, n):
            return buf[:, bass.ds(n * D, D)]

        st_x = sb("st_x", 2 * 6)
        mv_x = sb("mv_x", 2 * 2)
        ln_x = sb("ln_x", 2)
        rstd_x = sb("rstd_x", 2)
        xn = sb("xn", 2 * P)
        xn_t = sb("xn_t", 2 * P)
        v_sb = sb("v_sb", 2 * GV)
        g_soft = sb("g_soft", GV)
        g_sig = sb("g_sig", GV)
        silu = sb("silu", 2 * GV)
        low = sb("low", P)
        gk_soft = sb("gk_soft", P)
        gk_min = sb("gk_min", P)
        logsig = sb("logsig", P)
        cum = sb("cum", P)
        last16 = sb("last16", 2)
        dlast = sb("dlast", 2 * 2)
        dec_q = sb("dec_q", P)
        dec_k = sb("dec_k", P)
        dec_g = sb("dec_g", P)
        qg = sb("qg", 2 * GH * P)
        kd = sb("kd", 2 * P)
        kg = sb("kg", P)
        kg_tok = sb("kg_tok", 2 * 2 * P)
        a_t = sb("a_t", 2 * GH * P)
        state = sb("state", 2 * 2 * GDV)
        o_sq = sb("o_sq", GV)
        o_ss = sb("o_ss", GH)
        o_ln = sb("o_ln", GH)
        o_r = sb("o_r", GH)
        og1 = sb("og1", GV)
        og2 = sb("og2", 2 * GV)
        og_t = sb("og_t", 2 * 2 * P)
        st_y = sb("st_y", 6)
        mv_y = sb("mv_y", 2)
        ln_y = sb("ln_y", 1)
        rstd_y = sb("rstd_y", 1)
        yn = sb("yn", P)
        st_f = sb("st_f", 6)
        mv_f = sb("mv_f", 2)
        ln_f = sb("ln_f", 1)
        rstd_f = sb("rstd_f", 1)

        h_t = sb("h_t", 2 * (P + 1))
        x_slot = sb("x_slot", 2 * P)
        sq = sb("sq", 2 * INNER)
        ss = sb("ss", 2 * AH)
        ssc = sb("ssc", 2 * AH)
        ss_ln = sb("ss_ln", 2 * AH)
        inv = sb("inv", 2 * AH)
        qn = sb("qn", 2 * INNER)
        rot1 = sb("rot1", 2 * INNER)
        rot2 = sb("rot2", 2 * INNER)
        qr = sb("qr", 2 * 2 * INNER)
        q_bd = sb("q_bd", 2 * PAIRS * 2 * P)
        KC = P + W
        k_t = sb("k_t", 2 * PAIRS * KC)
        v_cur = sb("v_cur", 2 * INNER)
        v_mix = sb("v_mix", 2 * INNER)
        neg_max = sb("neg_max", 2 * PAIRS)
        row_sum = sb("row_sum", 2 * 2 * PAIRS)
        row_rec = sb("row_rec", 2 * PAIRS)
        PROBS, PROBS_T = 2 * 2 * PAIRS * P, 2 * PAIRS * P
        shared = sb("shared", max(PROBS + PROBS_T, 2 * NJ * GROUP * P))
        probs, probs_t = shared[:, 0:PROBS], shared[:, PROBS:PROBS + PROBS_T]
        o_t = sb("o_t", 2 * PAIRS * P)
        hcat = sb("hcat", 2 * P)
        st_z = sb("st_z", 6)
        mv_z = sb("mv_z", 2)
        ln_z = sb("ln_z", 1)
        rstd_z = sb("rstd_z", 1)
        zn = sb("zn", 2 * P)

        gelu = sq[:, 0:2 * GROUP * P]
        hid = shared[:, 0:2 * NJ * GROUP * P]
        st_o = sb("st_o", NT * 6)
        mv_o = sb("mv_o", NT * 2)
        ln_o = sb("ln_o", NT)
        rstd_o = sb("rstd_o", NT)
        xo, res = x_in, stream[DEPTH - 1]

        d = sems("d_const d_x0 d_x1 d_gla d_qkv d_cols d_scales d_tab d_ffn d_out")
        s = sems(
            "zero_dve zero_pool cast_consts col_consts "
            "x_stats x_aggr x_ln x_rstd xn_ready xt_done xnt_ready vg_done proj_done v_ready gabs_ready "
            "gexp_ready gsoft_ready glog_ready gsig_ready silu_ready low_ready gk_done kabs_ready kexp_ready "
            "ksoft_ready gmin_ready logsig_ready cum_ready last_ready decq_ready deck_ready decg_ready qg_ready "
            "kd_ready kg_ready at_done kgt_done atm_ready kgtok_ready kv_done s1_ready s2_ready intra_done go_done "
            "osq_ready oss_ready oln_ready or_ready og1_ready og2_ready ogt_done ogt_ready y_done y_stats y_aggr "
            "y_ln y_rstd yn_ready x1_ready f_stats f_aggr f_ln f_rstd xf_ready "
            "slot_ready carry_zero table_ready cos_ready xtr_done carried ht_ready qk_done sq_ready ss_ready ssc_ready ssl_ready inv_ready "
            "qn_ready rot1_ready rot2_ready qr_ready qt_done kt_done qbd0_ready qbd1_ready kprev_ready kt_ready "
            "sc0_done sc1_done max0_ready max1_ready p0_ready p1_ready rs0_ready rs1_ready pn0_ready pn1_ready pt0_done pt1_done "
            "pt0_ready pt1_ready v_done vup_ready vcur_ready vmix_ready pv0_done pv_done ot_ready wo_done mid_ready "
            "half_ready hs_done hs_ready z_stats z_aggr z_ln z_rstd zn_ready zt_done z_ready "
            "ones_ready h1_done gelu_ready hid_ready h2_done ffn_ready sto_ready mvo_ready "
            "lno_ready rstdo_ready xo_ready res_ready")

        def q_blocks(par, b_t, h2):
            r = slice(h2 * DH, (h2 + 1) * DH)
            dst = q_bd[r, par * PAIRS * 2 * P:(par + 1) * PAIRS * 2 * P].rearrange("p (c w i) -> p c w i", c=PAIRS, w=2)
            return (dst[:, :, :, h2 * W:(h2 + 1) * W],
                    b_t[r, :].rearrange("p (c w i) -> p c w i", c=PAIRS, w=2))

        dve_engine = nc.vector

        def wait_apart(engine, *waits):
            if not isinstance(waits[0][1], int):
                waits = [(semaphore, engine.snap(engine.to_reg(count))) for semaphore, count in waits]
                engine.wait_ge(s["zero_dve" if engine is dve_engine else "zero_pool"], 1)
            for semaphore, count in waits:
                wait(engine, semaphore, count)

        block = ctx.enter_context(nc.Block())

        def iterate(engine, step):
            for k in range(-2, 4):
                step(k, k % 2)
            with engine.Fori(4, NT - 3, 2) as k:
                step(k, 0)
                step(k + 1, 1)
            for k in range(NT - 2, NT + 2):
                step(k, k % 2)

        def staged(fn, k, parity, lag, *args):
            n = k + lag
            if isinstance(n, int) and not 0 <= n < NT:
                return
            fn(n, (parity + lag) % 2, *args)

        def capped(count, most):
            return min(count, most) if isinstance(count, int) else count

        @block.sync
        def _(sp):
            xv = x_in[:, :].rearrange("p (n d) -> p n d", d=D)
            sp.dma_start(xv[:, 0:B, :], x[:, 0:P, :].rearrange("b p d -> p b d")).then_inc(d["d_x0"], 16)
            sp.dma_start(consts[:, :], square_consts).then_inc(d["d_const"], 16)
            sp.dma_start(wvg_sb[:, 0:GV], Wv).then_inc(d["d_gla"], 16)
            sp.dma_start(wvg_sb[:, GV:2 * GV], Wg).then_inc(d["d_gla"], 16)
            sp.dma_start(wqk_sb[:, 0:P], Wq).then_inc(d["d_gla"], 16)
            sp.dma_start(wqk_sb[:, P:2 * P], Wk).then_inc(d["d_gla"], 16)
            sp.dma_start(wgk1_sb[:, :], Wgk1).then_inc(d["d_gla"], 16)
            sp.dma_start(wgk2_sb[0:RANK, :], Wgk2).then_inc(d["d_gla"], 16)
            sp.dma_start(wout_sb[:, :].rearrange("p (c n) -> p c n", c=2),
                         Wo.rearrange("(c p) n -> p c n", p=P)).then_inc(d["d_gla"], 16)
            for b in range(B):
                sp.dma_start(xv[:, B + b:NT:B, :],
                             x[b, P:T, :].rearrange("(t p) d -> p t d", p=P)).then_inc(d["d_x1"], 16)
            sp.dma_start(cos_base[:, :], rotary_cos).then_inc(d["d_tab"], 16)
            sp.dma_start(sin_base[:, :], rotary_sin).then_inc(d["d_tab"], 16)
            sp.dma_start(wqkv_sb[:, :].rearrange("p (l n) -> p l n", l=DEPTH),
                         wqkv.rearrange("l k n -> k l n")).then_inc(d["d_qkv"], 16)
            sp.dma_start(wo_sb[:, :].rearrange("p (l c n) -> p l c n", l=DEPTH, c=PAIRS),
                         wo.rearrange("l (c p) n -> p l c n", p=P)).then_inc(d["d_qkv"], 16)
            sp.dma_start(w1_sb[:, :].rearrange("p (l n) -> p l n", l=DEPTH),
                         w1.rearrange("l k n -> k l n")).then_inc(d["d_ffn"], 16)
            w2v = w2_sb[:, :].rearrange("p (l c n) -> p l c n", l=DEPTH, c=NJ)
            for l in range(DEPTH):
                sp.dma_start(w2v[:, l, 0:NJ - 1, :],
                             w2[l, 0:(NJ - 1) * P, :].rearrange("(c p) n -> p c n", p=P)).then_inc(d["d_ffn"], 16)
                sp.dma_start(w2v[0:ROWS[-1], l, NJ - 1, :], w2[l, (NJ - 1) * P:HID, :]).then_inc(d["d_ffn"], 16)
                sp.dma_start(w2v[ROWS[-1]:ROWS[-1] + 1, l, NJ - 1, :], b2[l:l + 1, :]).then_inc(d["d_ffn"], 16)
            ov = res[:, :].rearrange("p (n d) -> p n d", d=D)
            for g in range(NT // GROUP):
                sp.wait_ge(s["res_ready"], g + 1)
                for b in range(B):
                    t0 = g * GROUP // B
                    sp.dma_start(out[b, t0 * P:(t0 + GROUP // B) * P, :].rearrange("(t p) d -> p t d", p=P),
                                 ov[:, g * GROUP + b:(g + 1) * GROUP:B, :]).then_inc(d["d_out"], 16)
            sp.wait_ge(d["d_out"], 16 * B * (NT // GROUP))

        @block.gpsimd
        def _(pool):
            pool.dma_start(columns[:, 0:1], bgk2.rearrange("(p a) -> p a", a=1)).then_inc(d["d_cols"], 16)
            for h2 in range(P // GDV):
                pool.dma_start(columns[h2 * GDV:(h2 + 1) * GDV, 1:2],
                               rms_w.rearrange("(p a) -> p a", a=1)).then_inc(d["d_cols"], 16)
            with nc.allow_non_contiguous_dma(reason="per-partition columns of the small vectors"):
                pool.dma_start(columns[:, 4:4 + DEPTH], ln_g.rearrange("l p -> p l")).then_inc(d["d_cols"], 16)
                pool.dma_start(columns[:, 4 + DEPTH:4 + 2 * DEPTH],
                               ln_b.rearrange("l p -> p l")).then_inc(d["d_cols"], 16)
                for l in range(DEPTH):
                    for half in range(2):
                        at = B1_AT + (l * 2 + half) * NJ
                        pool.dma_start(columns[:, at:at + NJ - 1],
                                       b1[l, half * HID:half * HID + (NJ - 1) * P].rearrange("(j p) -> p j", p=P)
                                       ).then_inc(d["d_cols"], 16)
                        pool.dma_start(columns[0:ROWS[-1], at + NJ - 1:at + NJ],
                                       b1[l, half * HID + (NJ - 1) * P:(half + 1) * HID].rearrange("(p a) -> p a", a=1)
                                       ).then_inc(d["d_cols"], 16)
                for l in range(DEPTH):
                    for i, src in enumerate((q_scale, k_scale)):
                        pool.dma_start(scales[:, (l * 2 + i) * DH:(l * 2 + i + 1) * DH],
                                       src[l, :].partition_broadcast(P)).then_inc(d["d_scales"], 16)
            for buf in (q_bd, k_t, v_cur, v_mix):
                pool.memset(buf[:, :], 0.0)
            pool.memset(middle[:, 0:2 * D], 0.0)
            pool.memset(h_t[:, :], 0.0).then_inc(s["zero_pool"], 1)
            pool.wait_ge(s["zero_pool"], 1)

            def gate_o(n, par):
                wait(pool, s["og1_ready"], n + 1)
                wait(pool, s["silu_ready"], n + 1)
                wait(pool, s["ogt_done"], n - 1)
                pool.tensor_tensor(og2[:, par * GV:(par + 1) * GV], og1[:, :], silu[:, par * GV:(par + 1) * GV],
                                   ALU.mult).then_inc(s["og2_ready"], 1)

            def add_y(n, par):
                wait(pool, s["yn_ready"], n + 1)
                pool.tensor_tensor(tile_of(x_attn, n), tile_of(x_in, n), yn[:, :], ALU.add).then_inc(s["x1_ready"], 1)

            def gla_step(k, par):
                staged(add_y, k, par, -2)
                staged(gate_o, k, par, 0)
            iterate(pool, gla_step)

            for l in range(DEPTH):
                base = NT * l

                def keep_prev_keys(n, par):
                    N = base + n
                    kv = k_t[:, par * PAIRS * KC:(par + 1) * PAIRS * KC].rearrange("p (c k) -> p c k", k=KC)
                    wait_apart(pool, (s["sc0_done"], N - 1), (s["sc1_done"], N - 1), (s["kt_ready"], N - 1),
                               (s["vmix_ready"], N - 1))
                    pool.tensor_scalar(kv[:, :, P:KC], kv[:, :, W:P], 1.0, 0.0, ALU.mult, ALU.add
                                       ).then_inc(s["kprev_ready"], 1)

                def keep_prev_values(n, par):
                    N = base + n
                    c = slice(par * INNER, (par + 1) * INNER)
                    wait_apart(pool, (s["pv_done"], N - 1), (s["vcur_ready"], N - 1),
                               (s["kprev_ready"], capped(N + 2, base + NT)))
                    pool.tensor_scalar(v_mix[W:P, c], v_cur[W:P, c], 1.0, 0.0, ALU.mult, ALU.add
                                       ).then_inc(s["vup_ready"], 1)

                def mix_values(n, par):
                    N = base + n
                    c = slice(par * INNER, (par + 1) * INNER)
                    wait_apart(pool, (s["vcur_ready"], N + 1), (s["pv_done"], N - 1),
                               (s["pn0_ready"], N + 1))
                    pool.tensor_scalar(v_mix[0:W, c], v_cur[0:W, c], 1.0, 0.0, ALU.mult, ALU.add
                                       ).then_inc(s["vmix_ready"], 1)

                def rotate_sin(n, par):
                    N = base + n
                    wait_apart(pool, (s["qn_ready"], N + 1), (s["qr_ready"], N),
                               (s["vup_ready"], N))
                    for i in range(2):
                        a = qn[:, i * INNER:(i + 1) * INNER].rearrange("p (h e r) -> p h e r", h=AH, e=2)
                        o = rot2[:, i * INNER:(i + 1) * INNER].rearrange("p (h e r) -> p h e r", h=AH, e=2)
                        tab = sin_t[:, bass.ds((n - par) * DH + i * DH, DH)].rearrange("p (e r) -> p e r", e=2)
                        ins = pool.tensor_tensor(o, a[:, :, ::-1, :], tab.unsqueeze(1).to_broadcast([P, AH, 2, DH // 2]),
                                                 ALU.mult)
                    ins.then_inc(s["rot2_ready"], 1)

                def normalise_probs(n, par, w):
                    N = base + n
                    if w == 0:
                        wait_apart(pool, (s["rs0_ready"], N + 1))
                    else:
                        wait_apart(pool, (s["rs1_ready"], N + 1))
                    for c in range(PAIRS):
                        wp = w * PAIRS + c
                        at = (par * 2 * PAIRS + wp) * P
                        ins = pool.tensor_scalar(probs[:, at:at + P], probs[:, at:at + P],
                                                 row_rec[:, wp:wp + 1], 1.0, ALU.mult, ALU.mult)
                    ins.then_inc(s[f"pn{w}_ready"], 1)

                if l:
                    pool.wait_ge(s["ffn_ready"], 2 * (NT // GROUP) * l)
                else:
                    pool.wait_ge(s["xf_ready"], NT)
                if l:
                    pool.wait_ge(s["v_done"], base)
                    pool.wait_ge(s["ht_ready"], base)
                    for b in range(B):
                        c = b * (P + 1) + P
                        ins = pool.memset(h_t[:, c:c + 1], 0.0)
                    ins.then_inc(s["carry_zero"], 1)

                def step(k, par):
                    staged(keep_prev_keys, k, par, 0)
                    staged(keep_prev_values, k, par, -1)
                    staged(rotate_sin, k, par, 0)
                    staged(normalise_probs, k, par, -1, 1)
                    staged(normalise_probs, k, par, -1, 0)
                    staged(mix_values, k, par, -1)
                iterate(pool, step)

                pool.wait_ge(s["z_ready"], base + NT)
                for slot in range(2):
                    at = (slot * NJ + NJ - 1) * GROUP * P
                    ins = pool.memset(hid[ROWS[-1] // 32 * 32:P, at:at + GROUP * P], 1.0)
                ins.then_inc(s["ones_ready"], 1)
                pool.wait_ge(s["ones_ready"], l + 1)

        @block.tensor
        def _(pe):
            def mm(o, w, m, start=True, stop=True, skip=False):
                return pe.matmul(o, w, m, start=start, stop=stop, skip_group_check=skip)

            b_xt, b_qk, b_vg, b_at, b_kv, b_o, b_og, b_y = bank

            def transpose_x(n, par):
                wait(pe, s["xn_ready"], n + 1)
                wait(pe, s["xnt_ready"], n)
                pe.transpose(b_xt[:, 0:P], xn[:, par * P:(par + 1) * P], ident).then_inc(s["xt_done"], 1)

            def project_vg(n, par):
                wait(pe, s["xnt_ready"], n + 1)
                wait(pe, s["v_ready"], n)
                wait(pe, s["silu_ready"], n)
                mm(b_vg[:, :], xn_t[:, par * P:(par + 1) * P], wvg_sb[:, :]).then_inc(s["vg_done"], 1)

            def project_qk(n, par):
                a = xn_t[:, par * P:(par + 1) * P]
                wait(pe, s["xnt_ready"], n + 1)
                for read in ("low_ready", "kabs_ready", "gmin_ready", "qg_ready", "kd_ready", "kg_ready"):
                    wait(pe, s[read], n)
                mm(b_qk[0:RANK, 3 * P:4 * P], wgk1_sb[:, :], a)
                mm(b_qk[:, 0:P], wqk_sb[:, 0:P], a)
                mm(b_qk[:, P:2 * P], wqk_sb[:, P:2 * P], a).then_inc(s["proj_done"], 1)

            def project_gate(n, par):
                wait(pe, s["low_ready"], n + 1)
                mm(b_qk[:, 2 * P:3 * P], wgk2_sb[0:RANK, :], low[0:RANK, :]).then_inc(s["gk_done"], 1)

            def intra_scores(n, par):
                wait(pe, s["qg_ready"], n + 1)
                wait(pe, s["kd_ready"], n + 1)
                wait(pe, s["atm_ready"], n)
                mm(b_at[:, :], kd[:, par * P:(par + 1) * P], qg[:, par * GH * P:(par + 1) * GH * P]
                   ).then_inc(s["at_done"], 1)

            def transpose_kg(n, par):
                wait(pe, s["kg_ready"], n + 1)
                wait(pe, s["s1_ready"], n)
                wait(pe, s["s2_ready"], n)
                pe.transpose(b_kv[:, 0:P], kg[:, :], ident).then_inc(s["kgt_done"], 1)

            def key_values(n, par):
                wait(pe, s["kgtok_ready"], n + 1)
                wait(pe, s["v_ready"], n + 1)
                for c in range(2):
                    for h in range(GH):
                        at = (par * 2 + c) * P + h * GDK
                        ins = mm(b_kv[h * GDK:(h + 1) * GDK, P + c * GDV:P + (c + 1) * GDV],
                                 kg_tok[:, at:at + GDK], v_sb[:, par * GV + h * GDV:par * GV + (h + 1) * GDV])
                ins.then_inc(s["kv_done"], 1)

            def intra_outputs(n, par):
                wait(pe, s["atm_ready"], n + 1)
                wait(pe, s["v_ready"], n + 1)
                wait(pe, s["og1_ready"], n)
                for h in range(GH):
                    ins = mm(b_o[:, h * GDV:(h + 1) * GDV], a_t[:, (par * GH + h) * P:(par * GH + h + 1) * P],
                             v_sb[:, par * GV + h * GDV:par * GV + (h + 1) * GDV], start=(h == 0), stop=False, skip=True)
                ins.then_inc(s["intra_done"], 1)

            def state_outputs(n, par):
                wait(pe, s["s2_ready"], n - 1)
                wait(pe, s["s1_ready"], n + 1)
                for c in range(2):
                    for h in range(GH):
                        ins = mm(b_o[c * CH:(c + 1) * CH, h * GDV:(h + 1) * GDV],
                                 qg[:, (par * GH + h) * P + c * CH:(par * GH + h) * P + (c + 1) * CH],
                                 state[:, (par * 2 + c) * GDV:(par * 2 + c + 1) * GDV],
                                 start=False, stop=True, skip=True)
                ins.then_inc(s["go_done"], 1)

            def transpose_o(n, par):
                wait(pe, s["og2_ready"], n + 1)
                wait(pe, s["ogt_ready"], n)
                for c in range(2):
                    ins = pe.transpose(b_og[:, c * P:(c + 1) * P],
                                       og2[:, par * GV + c * P:par * GV + (c + 1) * P], ident)
                ins.then_inc(s["ogt_done"], 1)

            def project_out(n, par):
                wait(pe, s["ogt_ready"], n + 1)
                wait(pe, s["yn_ready"], n)
                for c in range(2):
                    ins = mm(b_y[:, 0:D], og_t[:, (par * 2 + c) * P:(par * 2 + c + 1) * P],
                             wout_sb[:, c * D:(c + 1) * D], start=(c == 0), stop=(c == 1))
                ins.then_inc(s["y_done"], 1)

            def gla_step(k, par):
                staged(project_gate, k, par, 0)
                staged(key_values, k, par, -1)
                staged(project_out, k, par, -2)
                staged(intra_outputs, k, par, -1)
                staged(state_outputs, k, par, -1)
                staged(project_vg, k, par, 0)
                staged(transpose_x, k, par, 1)
                staged(transpose_kg, k, par, 0)
                staged(project_qk, k, par, 1)
                staged(transpose_o, k, par, -1)
                staged(intra_scores, k, par, 0)

            pe.wait_ge(d["d_const"], 16)
            pe.wait_ge(d["d_gla"], 7 * 16)
            pe.wait_ge(s["zero_dve"], 1)
            iterate(pe, gla_step)

            pe.wait_ge(d["d_qkv"], 32)
            pe.wait_ge(s["zero_pool"], 1)
            pe.wait_ge(s["cast_consts"], 2)
            pe.wait_ge(s["xf_ready"], NT)
            for l in range(DEPTH):
                base = NT * l
                b_q, b_k, b_v, b_t0, b_t1, b_s0, b_s1, b_m = bank
                wl = wqkv_sb[:, l * QKV:(l + 1) * QKV]

                def transpose_in(n, par):
                    N = base + n
                    wait(pe, s["slot_ready"], N + 1)
                    wait(pe, s["hs_ready"], N - 3)
                    wait(pe, s["z_ready"], N - 4)
                    wait(pe, s["mid_ready"], N - 3)
                    wait(pe, s["ht_ready"], N)
                    pe.transpose(b_m[:, 0:P], x_slot[:, par * P:(par + 1) * P], ident).then_inc(s["xtr_done"], 1)

                def project_qk(n, par):
                    N = base + n
                    a = h_t[:, par * (P + 1):par * (P + 1) + P]
                    wait(pe, s["ht_ready"], N + 1)
                    wait(pe, s["qn_ready"], N)
                    mm(b_q[:, :], a, wl[:, 0:INNER])
                    mm(b_k[:, :], a, wl[:, INNER:2 * INNER]).then_inc(s["qk_done"], 1)

                def project_v(n, par):
                    N = base + n
                    wait(pe, s["ht_ready"], N + 1)
                    wait(pe, s["ot_ready"], N - 1)
                    wait(pe, s["vcur_ready"], N)
                    mm(b_v[:, :], h_t[:, par * (P + 1):par * (P + 1) + P], wl[:, 2 * INNER:3 * INNER]
                       ).then_inc(s["v_done"], 1)

                def transpose_q(n, par):
                    N = base + n
                    wait(pe, s["qr_ready"], N + 1)
                    wait(pe, s["pt0_ready"], N - 1)
                    wait(pe, s["qbd0_ready"], N)
                    wait(pe, s["qbd1_ready"], N)
                    for c in range(PAIRS):
                        at = par * 2 * INNER + c * P
                        ins = pe.transpose(b_t0[:, c * P:(c + 1) * P], qr[:, at:at + P], ident)
                    ins.then_inc(s["qt_done"], 1)

                def transpose_k(n, par):
                    N = base + n
                    wait(pe, s["qr_ready"], N + 1)
                    wait(pe, s["pt1_ready"], N - 1)
                    wait(pe, s["kt_ready"], N)
                    for c in range(PAIRS):
                        at = par * 2 * INNER + INNER + c * P
                        ins = pe.transpose(b_t1[:, c * P:(c + 1) * P], qr[:, at:at + P], ident)
                    ins.then_inc(s["kt_done"], 1)

                def scores(n, par, w):
                    N = base + n
                    b_s = (b_s0, b_s1)[w]
                    wait(pe, s["qbd0_ready"], N + 1)
                    wait(pe, s["qbd1_ready"], N + 1)
                    wait(pe, s["kt_ready"], N + 1)
                    wait(pe, s[f"p{w}_ready"], N)
                    first = isinstance(n, int) and n < B
                    m = (2 if first else 0) if w == 0 else 1
                    mask = masks_bf[:, m * P:(m + 1) * P].unsqueeze(1).to_broadcast([P, PAIRS, P])
                    mm(b_s[:, :].rearrange("p (c k) -> p c k", c=PAIRS), ident_bf[:, :], mask,
                       start=True, stop=False, skip=True)
                    for c in range(PAIRS):
                        kc = k_t[:, (par * PAIRS + c) * KC:(par * PAIRS + c + 1) * KC]
                        if w == 0:
                            kc = kc.rearrange("p (a k) -> p a k", k=W)[:, 0:3:2, :]
                        else:
                            kc = kc[:, 0:P]
                        at = ((par * PAIRS + c) * 2 + w) * P
                        o = b_s[:, c * P:(c + 1) * P]
                        if w == 0:
                            o = o.rearrange("p (a k) -> p a k", k=W)
                        ins = mm(o, q_bd[:, at:at + P], kc, start=False, stop=True, skip=True)
                    ins.then_inc(s[f"sc{w}_done"], 1)

                def transpose_probs(n, par, w):
                    N = base + n
                    wait(pe, s[f"pn{w}_ready"], N + 1)
                    b_t = (b_t0, b_t1)[w]
                    if w == 0:
                        wait(pe, s["qbd0_ready"], capped(N + 2, base + NT))
                        wait(pe, s["qbd1_ready"], capped(N + 2, base + NT))
                        wait(pe, s["pt0_ready"], N)
                    else:
                        wait(pe, s["kt_ready"], capped(N + 2, base + NT))
                        wait(pe, s["pt1_ready"], N)
                    for c in range(PAIRS):
                        at = ((par * 2 + w) * PAIRS + c) * P
                        ins = pe.transpose(b_t[:, c * P:(c + 1) * P], probs[:, at:at + P], ident)
                    ins.then_inc(s[f"pt{w}_done"], 1)

                def weigh_values(n, par, w):
                    N = base + n
                    wait(pe, s[f"pt{w}_ready"], N + 1)
                    if w == 0:
                        wait(pe, s["vup_ready"], N + 1)
                        wait(pe, s["vmix_ready"], N + 1)
                        wait(pe, s["vcur_ready"], capped(N + 2, base + NT))
                        wait(pe, s["ot_ready"], N)
                    else:
                        wait(pe, s["vcur_ready"], N + 1)
                    for h in range(AH):
                        c, h2 = h // 2, h % 2
                        at = (w * PAIRS + c) * P + h2 * W
                        ins = mm(b_v[h2 * DH:(h2 + 1) * DH, c * P + w * W:c * P + (w + 1) * W],
                                 (v_mix, v_cur)[w][:, par * INNER + h * DH:par * INNER + (h + 1) * DH],
                                 probs_t[:, at:at + W])
                    ins.then_inc(s[("pv0_done", "pv_done")[w]], 1)

                def project_o(n, par):
                    N = base + n
                    wait(pe, s["ot_ready"], N + 1)
                    wait(pe, s["ht_ready"], capped(N + 4, base + NT))
                    wait(pe, s["hs_ready"], N)
                    wait(pe, s["z_ready"], N - 1)
                    wait(pe, s["mid_ready"], N)
                    for c in range(PAIRS):
                        at = (par * PAIRS + c) * P
                        ins = mm(b_m[:, P:2 * P], o_t[:, at:at + P],
                                 wo_sb[:, (l * PAIRS + c) * D:(l * PAIRS + c + 1) * D],
                                 start=(c == 0), stop=(c == PAIRS - 1))
                    ins.then_inc(s["wo_done"], 1)

                def shift_rows(n, par):
                    N = base + n
                    wait(pe, s["mid_ready"], N + 1)
                    wait(pe, s["z_ready"], N)
                    wait(pe, s["mid_ready"], N + 1)
                    wait(pe, s["ht_ready"], capped(N + 4, base + NT))
                    wait(pe, s["hs_ready"], N)
                    o = b_m[:, 2 * P:2 * P + D // 2]
                    mm(o, shift, middle[:, bass.ds((n + 2) * D + D // 2, D // 2)], stop=False)
                    mm(o, carry, middle[:, bass.ds(n * D + D // 2, D // 2)], start=False
                       ).then_inc(s["hs_done"], 1)

                def transpose_z(n, par):
                    N = base + n
                    wait(pe, s["zn_ready"], N + 1)
                    wait(pe, s["mid_ready"], capped(N + 2, base + NT))
                    wait(pe, s["ht_ready"], capped(N + 5, base + NT))
                    wait(pe, s["hs_ready"], N + 1)
                    wait(pe, s["z_ready"], N)
                    pe.transpose(b_m[:, 3 * P:4 * P], zn[:, par * P:(par + 1) * P], ident).then_inc(s["zt_done"], 1)

                def attn_step(k, par):
                    staged(transpose_in, k, par, 2)
                    staged(weigh_values, k, par, -1, 1)
                    staged(project_qk, k, par, 2)
                    staged(project_o, k, par, -1)
                    staged(transpose_q, k, par, 1)
                    staged(transpose_k, k, par, 1)
                    staged(project_v, k, par, 1)
                    staged(transpose_probs, k, par, 0, 0)
                    staged(transpose_z, k, par, -2)
                    staged(scores, k, par, 1, 1)
                    staged(transpose_probs, k, par, 0, 1)
                    staged(shift_rows, k, par, -1)
                    staged(scores, k, par, 1, 0)
                    staged(weigh_values, k, par, 0, 0)
                iterate(pe, attn_step)

                if l == 0:
                    pe.wait_ge(d["d_ffn"], 16 * 7)
                pe.wait_ge(s["z_ready"], base + NT)
                NG = NT // GROUP
                FB = GROUP * P
                for g in range(NG + 1):
                    G = l * NG + g
                    if g < NG:
                        for j in range(NJ):
                            wait(pe, s["hid_ready"], (G - 1) * NJ + j + 1)
                            for half in (1, 0):
                                at = l * 2 * HID + half * HID + j * P
                                ins = mm(bank[2 * j + half][0:ROWS[j], :], w1_sb[:, at:at + ROWS[j]],
                                         z_t[:, g * FB:(g + 1) * FB])
                            ins.then_inc(s["h1_done"], 1)
                    if g:
                        G -= 1
                        wait(pe, s["hid_ready"], (G + 1) * NJ)
                        for half in range(2):
                            wait(pe, s["ffn_ready"], 2 * (G - 1) + half + 1)
                            for i in (2 * half, 2 * half + 1):
                                o = bank[6 + half][:, (i % 2) * P:(i % 2 + 1) * P]
                                for j in range(NJ):
                                    K = P if j < NJ - 1 else ROWS[j] + 1
                                    at = ((G % 2) * NJ + j) * FB + i * P
                                    ins = mm(o, hid[0:K, at:at + P],
                                             w2_sb[0:K, (l * NJ + j) * D:(l * NJ + j + 1) * D],
                                             start=(j == 0), stop=(j == NJ - 1))
                            ins.then_inc(s["h2_done"], 1)
                if l + 1 < DEPTH:
                    pe.wait_ge(s["ffn_ready"], 2 * NG * (l + 1))

        @block.scalar
        def _(act):
            act.preload_act_table_set("natural_log_exp_and_others")

            def rstd(dst, mid, var, mid_sem, dst_sem, count, width=1, scale=1.0):
                act.activation(mid, var, ACT.Ln, bias=eps_col, scale=scale).then_inc(mid_sem, 1)
                wait(act, mid_sem, count)
                act.activation(dst, mid, ACT.Exp, scale=-0.5).then_inc(dst_sem, 1)

            b_xt, b_qk, b_vg, b_at, b_kv, b_o, b_og, b_y = bank

            def ln_of_x(n, par):
                wait(act, s["x_aggr"], n + 1)
                act.activation(ln_x[:, par:par + 1], mv_x[:, 2 * par + 1:2 * par + 2], ACT.Ln, bias=eps_col
                               ).then_inc(s["x_ln"], 1)

            def rstd_of_x(n, par):
                wait(act, s["x_ln"], n + 1)
                wait(act, s["xn_ready"], n - 1)
                act.activation(rstd_x[:, par:par + 1], ln_x[:, par:par + 1], ACT.Exp, scale=-0.5
                               ).then_inc(s["x_rstd"], 1)

            def copy_xn_t(n, par):
                wait(act, s["xt_done"], n + 1)
                wait(act, s["vg_done"], n - 1)
                wait(act, s["proj_done"], n - 1)
                act.activation(xn_t[:, par * P:(par + 1) * P], b_xt[:, 0:P], ACT.Copy).then_inc(s["xnt_ready"], 1)

            def copy_v(n, par):
                wait(act, s["vg_done"], n + 1)
                wait(act, s["go_done"], n - 1)
                act.activation(v_sb[:, par * GV:(par + 1) * GV], b_vg[:, 0:GV], ACT.Copy).then_inc(s["v_ready"], 1)

            def gate_abs(n, par):
                wait(act, s["vg_done"], n + 1)
                wait(act, s["glog_ready"], n)
                act.activation(g_soft[:, :], b_vg[:, GV:2 * GV], ACT.Abs).then_inc(s["gabs_ready"], 1)

            def gate_exp(n, par):
                wait(act, s["gabs_ready"], n + 1)
                act.activation(g_soft[:, :], g_soft[:, :], ACT.Exp, scale=-1.0).then_inc(s["gexp_ready"], 1)

            def gate_ln(n, par):
                wait(act, s["gexp_ready"], n + 1)
                act.activation(g_soft[:, :], g_soft[:, :], ACT.Ln, bias=1.0).then_inc(s["gsoft_ready"], 1)

            def gate_sigmoid(n, par):
                wait(act, s["glog_ready"], n + 1)
                act.activation(g_sig[:, :], g_sig[:, :], ACT.Exp).then_inc(s["gsig_ready"], 1)

            def copy_low(n, par):
                wait(act, s["proj_done"], n + 1)
                wait(act, s["gk_done"], n)
                act.activation(low[0:RANK, :], b_qk[0:RANK, 3 * P:4 * P], ACT.Copy).then_inc(s["low_ready"], 1)

            def decay_abs(n, par):
                wait(act, s["gk_done"], n + 1)
                wait(act, s["logsig_ready"], n)
                act.activation(gk_soft[:, :], b_qk[:, 2 * P:3 * P], ACT.Abs, bias=bgk2_col
                               ).then_inc(s["kabs_ready"], 1)

            def decay_exp(n, par):
                wait(act, s["kabs_ready"], n + 1)
                act.activation(gk_soft[:, :], gk_soft[:, :], ACT.Exp, scale=-1.0).then_inc(s["kexp_ready"], 1)

            def decay_ln(n, par):
                wait(act, s["kexp_ready"], n + 1)
                act.activation(gk_soft[:, :], gk_soft[:, :], ACT.Ln, bias=1.0).then_inc(s["ksoft_ready"], 1)

            def decay_of_q(n, par):
                wait(act, s["cum_ready"], n + 1)
                wait(act, s["qg_ready"], n)
                act.activation(dec_q[:, :], cum[:, :], ACT.Exp, scale=GATE).then_inc(s["decq_ready"], 1)

            def decay_of_k(n, par):
                wait(act, s["cum_ready"], n + 1)
                wait(act, s["kd_ready"], n)
                act.activation(dec_k[:, :], cum[:, :], ACT.Exp, scale=-GATE).then_inc(s["deck_ready"], 1)

            def decay_to_end(n, par):
                wait(act, s["last_ready"], n + 1)
                wait(act, s["kg_ready"], n)
                wait(act, s["s2_ready"], n - 1)
                for c in range(2):
                    act.activation(dec_g[:, c * CH:(c + 1) * CH], cum[:, c * CH:(c + 1) * CH], ACT.Exp,
                                   scale=-GATE, bias=last16[:, c:c + 1])
                act.activation(dlast[:, 2 * par:2 * par + 2], last16[:, :], ACT.Exp).then_inc(s["decg_ready"], 1)

            def copy_kg(n, par):
                wait(act, s["kgt_done"], n + 1)
                wait(act, s["kv_done"], n - 1)
                for c in range(2):
                    at = (par * 2 + c) * P
                    ins = act.activation(kg_tok[c * CH:(c + 1) * CH, at:at + P], b_kv[c * CH:(c + 1) * CH, 0:P], ACT.Copy)
                ins.then_inc(s["kgtok_ready"], 1)

            def square_o(n, par):
                wait(act, s["go_done"], n + 1)
                wait(act, s["oss_ready"], n)
                act.activation(o_sq[:, :], b_o[:, 0:GV], ACT.Square).then_inc(s["osq_ready"], 1)

            def ln_of_o(n, par):
                wait(act, s["oss_ready"], n + 1)
                act.activation(o_ln[:, :], o_ss[:, :], ACT.Ln, bias=eps_col, scale=1.0 / GDV
                               ).then_inc(s["oln_ready"], 1)

            def rstd_of_o(n, par):
                wait(act, s["oln_ready"], n + 1)
                wait(act, s["og1_ready"], n)
                act.activation(o_r[:, :], o_ln[:, :], ACT.Exp, scale=-0.5).then_inc(s["or_ready"], 1)

            def ln_of_y(n, par):
                wait(act, s["y_aggr"], n + 1)
                act.activation(ln_y[:, :], mv_y[:, 1:2], ACT.Ln, bias=eps_col).then_inc(s["y_ln"], 1)

            def rstd_of_y(n, par):
                wait(act, s["y_ln"], n + 1)
                wait(act, s["yn_ready"], n)
                act.activation(rstd_y[:, :], ln_y[:, :], ACT.Exp, scale=-0.5).then_inc(s["y_rstd"], 1)

            def ln_of_f(n, par):
                wait(act, s["f_aggr"], n + 1)
                act.activation(ln_f[:, :], mv_f[:, 1:2], ACT.Ln, bias=eps_col).then_inc(s["f_ln"], 1)

            def rstd_of_f(n, par):
                wait(act, s["f_ln"], n + 1)
                wait(act, s["xf_ready"], n)
                act.activation(rstd_f[:, :], ln_f[:, :], ACT.Exp, scale=-0.5).then_inc(s["f_rstd"], 1)

            def gla_step(k, par):
                staged(rstd_of_y, k, par, -2)
                staged(gate_exp, k, par, 0)
                staged(gate_ln, k, par, 0)
                staged(copy_v, k, par, 0)
                staged(copy_low, k, par, 1)
                staged(copy_kg, k, par, 0)
                staged(decay_abs, k, par, 1)
                staged(decay_exp, k, par, 1)
                staged(decay_ln, k, par, 1)
                staged(ln_of_f, k, par, -2)
                staged(ln_of_x, k, par, 2)
                staged(rstd_of_f, k, par, -2)
                staged(gate_sigmoid, k, par, 0)
                staged(rstd_of_x, k, par, 2)
                staged(square_o, k, par, 0)
                staged(decay_to_end, k, par, 1)
                staged(ln_of_o, k, par, 0)
                staged(rstd_of_o, k, par, 0)
                staged(decay_of_k, k, par, 1)
                staged(decay_of_q, k, par, 1)
                staged(ln_of_y, k, par, -1)
                staged(copy_xn_t, k, par, 2)
                staged(gate_abs, k, par, 1)

            act.wait_ge(d["d_cols"], 13 * 16)
            act.wait_ge(s["col_consts"], 2)
            act.wait_ge(s["zero_dve"], 1)
            iterate(act, gla_step)

            act.wait_ge(s["zero_pool"], 1)
            for l in range(DEPTH):
                base = NT * l
                b_q, b_k, b_v, b_t0, b_t1, b_s0, b_s1, b_m = bank

                def copy_in(n, par):
                    N = base + n
                    wait(act, s["xtr_done"], N - 1)
                    act.activation(x_slot[:, par * P:(par + 1) * P], tile_of(stream[l], n), ACT.Copy
                                   ).then_inc(s["slot_ready"], 1)

                def carry_column(n, par):
                    N = base + n
                    o = h_t[:, par * (P + 1):(par + 1) * (P + 1)]
                    wait(act, s["v_done"], N - 1)
                    wait(act, s["qk_done"], N - 1)
                    if l and isinstance(n, int) and n == 0:
                        act.wait_ge(s["carry_zero"], l)
                    act.activation(o[D // 2:P, 0:1], o[D // 2:P, P:P + 1], ACT.Copy).then_inc(s["carried"], 1)

                def copy_h_t(n, par):
                    N = base + n
                    o = h_t[:, par * (P + 1):(par + 1) * (P + 1)]
                    wait(act, s["xtr_done"], N + 1)
                    wait(act, s["carried"], N + 1)
                    act.activation(o[0:D // 2, 0:P], b_m[0:D // 2, 0:P], ACT.Copy)
                    act.activation(o[D // 2:P, 1:P + 1], b_m[D // 2:P, 0:P], ACT.Copy).then_inc(s["ht_ready"], 1)

                def squares(n, par):
                    N = base + n
                    wait(act, s["qk_done"], N + 1)
                    wait(act, s["ss_ready"], N)
                    act.activation(sq[:, 0:INNER], b_q[:, :], ACT.Square)
                    act.activation(sq[:, INNER:2 * INNER], b_k[:, :], ACT.Square).then_inc(s["sq_ready"], 1)

                def ln_of_squares(n, par):
                    N = base + n
                    wait(act, s["ssc_ready"], N + 1)
                    act.activation(ss_ln[:, :], ssc[:, :], ACT.Ln, scale=float(2 ** 30)).then_inc(s["ssl_ready"], 1)

                def inverse_norms(n, par):
                    N = base + n
                    wait(act, s["ssl_ready"], N + 1)
                    wait(act, s["qn_ready"], N)
                    act.activation(inv[:, :], ss_ln[:, :], ACT.Exp, scale=-0.5, bias=norm_bias_col
                                   ).then_inc(s["inv_ready"], 1)

                def copy_q_bd(n, par):
                    N = base + n
                    wait(act, s["qt_done"], N + 1)
                    wait(act, s["sc0_done"], N - 1)
                    wait(act, s["sc1_done"], N - 1)
                    dst, src = q_blocks(par, b_t0, 1)
                    act.activation(dst, src, ACT.Copy).then_inc(s["qbd1_ready"], 1)

                def copy_k_t(n, par):
                    N = base + n
                    wait(act, s["kt_done"], N + 1)
                    wait(act, s["kprev_ready"], N + 1)
                    kv = k_t[:, par * PAIRS * KC:(par + 1) * PAIRS * KC].rearrange("p (c k) -> p c k", k=KC)
                    act.activation(kv[:, :, 0:P], b_t1[:, :].rearrange("p (c k) -> p c k", k=P), ACT.Copy
                                   ).then_inc(s["kt_ready"], 1)

                def exponentials(n, par, w):
                    N = base + n
                    wait(act, s[f"max{w}_ready"], N + 1)
                    wait(act, s[f"pt{w}_done"], N - 1)
                    b_s = (b_s0, b_s1)[w]
                    for c in range(PAIRS):
                        at = ((par * 2 + w) * PAIRS + c) * P
                        r = (par * 2 + w) * PAIRS + c
                        ins = act.activation(probs[:, at:at + P], b_s[:, c * P:(c + 1) * P], ACT.Exp,
                                             bias=neg_max[:, w * PAIRS + c:w * PAIRS + c + 1],
                                             accum_out=row_sum[:, r:r + 1])
                    ins.then_inc(s[f"p{w}_ready"], 1)

                def copy_probs_t(n, par):
                    N = base + n
                    wait(act, s["pt0_done"], N + 1)
                    wait(act, s["pv0_done"], N)
                    act.activation(probs_t[:, 0:PAIRS * P], b_t0[:, :], ACT.Copy).then_inc(s["pt0_ready"], 1)

                def copy_o_t(n, par):
                    N = base + n
                    wait(act, s["pv_done"], N + 1)
                    wait(act, s["wo_done"], N - 1)
                    act.activation(o_t[:, par * PAIRS * P:(par + 1) * PAIRS * P], b_v[:, :], ACT.Copy
                                   ).then_inc(s["ot_ready"], 1)

                def copy_v_cur(n, par):
                    N = base + n
                    wait(act, s["v_done"], N + 1)
                    wait(act, s["vup_ready"], N + 1)
                    wait(act, s["vmix_ready"], N - 1)
                    wait(act, s["pv_done"], N - 1)
                    act.activation(v_cur[:, par * INNER:(par + 1) * INNER], b_v[:, :], ACT.Copy
                                   ).then_inc(s["vcur_ready"], 1)

                def copy_unshifted(n, par):
                    N = base + n
                    wait(act, s["mid_ready"], N + 1)
                    wait(act, s["zn_ready"], N - 1)
                    act.activation(hcat[:, par * P:par * P + D // 2],
                                   middle[:, bass.ds((n + 2) * D, D // 2)], ACT.Copy).then_inc(s["half_ready"], 1)

                def copy_shifted(n, par):
                    N = base + n
                    wait(act, s["hs_done"], N + 1)
                    wait(act, s["half_ready"], N + 1)
                    wait(act, s["zn_ready"], N - 1)
                    act.activation(hcat[:, par * P + D // 2:(par + 1) * P], b_m[:, 2 * P:2 * P + D // 2], ACT.Copy
                                   ).then_inc(s["hs_ready"], 1)

                def ln_of_z(n, par):
                    N = base + n
                    wait(act, s["z_aggr"], N + 1)
                    act.activation(ln_z[:, :], mv_z[:, 1:2], ACT.Ln, bias=eps_col).then_inc(s["z_ln"], 1)

                def rstd_of_z(n, par):
                    N = base + n
                    wait(act, s["z_ln"], N + 1)
                    wait(act, s["zn_ready"], N)
                    act.activation(rstd_z[:, :], ln_z[:, :], ACT.Exp, scale=-0.5).then_inc(s["z_rstd"], 1)

                def copy_z_t(n, par):
                    N = base + n
                    wait(act, s["zt_done"], N + 1)
                    act.activation(z_t[:, bass.ds(n * P, P)], b_m[:, 3 * P:4 * P], ACT.Identity,
                                   bias=lnb_col[l], scale=lng_col[l]).then_inc(s["z_ready"], 1)

                act.wait_ge(s["ffn_ready" if l else "xf_ready"], 2 * (NT // GROUP) * l if l else NT)

                def attn_step(k, par):
                    staged(copy_probs_t, k, par, -1)
                    staged(carry_column, k, par, 2)
                    staged(inverse_norms, k, par, 1)
                    staged(copy_v_cur, k, par, 0)
                    staged(copy_shifted, k, par, -2)
                    staged(copy_in, k, par, 2)
                    staged(exponentials, k, par, 0, 1)
                    staged(copy_h_t, k, par, 2)
                    staged(exponentials, k, par, 0, 0)
                    staged(copy_o_t, k, par, -1)
                    staged(ln_of_z, k, par, -2)
                    staged(rstd_of_z, k, par, -2)
                    staged(squares, k, par, 2)
                    staged(copy_q_bd, k, par, 1)
                    staged(copy_unshifted, k, par, -1)
                    staged(copy_k_t, k, par, 1)
                    staged(copy_z_t, k, par, -2)
                    staged(ln_of_squares, k, par, 2)
                iterate(act, attn_step)

                NG = NT // GROUP
                FB = GROUP * P
                for g in range(NG):
                    for j in range(NJ):
                        i = (l * NG + g) * NJ + j
                        act.wait_ge(s["h1_done"], i + 1)
                        wait(act, s["hid_ready"], i - 1)
                        act.activation(gelu[0:ROWS[j], (i % 2) * FB:(i % 2 + 1) * FB],
                                       bank[2 * j + 1][0:ROWS[j], :], ACT.Gelu, bias=b1_col(l, 1, j)
                                       ).then_inc(s["gelu_ready"], 1)
                act.preload_act_table_set("natural_log_exp_and_others")

            act.wait_ge(s["mvo_ready"], 1)
            rstd(rstd_o[:, :], ln_o[:, :], mv_o[:, 1:2 * NT:2], s["lno_ready"], s["rstdo_ready"], 1)

        @block.vector
        def _(dve):
            for buf in (qg, kg_tok, a_t, state):
                dve.memset(buf[:, :], 0.0)
            dve.memset(eps_col, EPS).then_inc(s["col_consts"], 1)
            dve.memset(norm_bias_col, 15 * LN2).then_inc(s["col_consts"], 1)
            dve.memset(st_x[:, :], 0.0).then_inc(s["zero_dve"], 1)
            dve.wait_ge(s["zero_dve"], 1)
            dve.wait_ge(d["d_const"], 16)
            dve.tensor_copy(ident_bf[:, :], ident).then_inc(s["cast_consts"], 1)
            dve.tensor_copy(masks_bf[:, :], consts[:, 3 * P:6 * P]).then_inc(s["cast_consts"], 1)
            b_xt, b_qk, b_vg, b_at, b_kv, b_o, b_og, b_y = bank

            def stats_x(n, par):
                if isinstance(n, int) and n == 0:
                    dve.wait_ge(d["d_x0"], 16)
                if isinstance(n, int) and n == B:
                    dve.wait_ge(d["d_x1"], 16 * B)
                dve.bn_stats(st_x[:, 6 * par:6 * par + 6], tile_of(x_in, n)).then_inc(s["x_stats"], 1)

            def aggregate_x(n, par):
                wait_apart(dve, (s["x_stats"], n + 1), (s["xn_ready"], n - 1))
                dve.bn_aggr(mv_x[:, 2 * par:2 * par + 2], st_x[:, 6 * par:6 * par + 6]).then_inc(s["x_aggr"], 1)

            def normalise_x(n, par):
                wait(dve, s["x_rstd"], n + 1)
                wait(dve, s["xt_done"], n - 1)
                dve.tensor_scalar(xn[:, par * P:(par + 1) * P], tile_of(x_in, n), mv_x[:, 2 * par:2 * par + 1],
                                  rstd_x[:, par:par + 1], ALU.subtract, ALU.mult).then_inc(s["xn_ready"], 1)

            def gate_log(n, par):
                wait(dve, s["gsoft_ready"], n + 1)
                wait(dve, s["v_ready"], n + 1)
                wait(dve, s["silu_ready"], n)
                dve.scalar_tensor_tensor(out=g_sig[:, :], in0=b_vg[:, GV:2 * GV], scalar=0.0, in1=g_soft[:, :],
                                         op0=ALU.min, op1=ALU.subtract).then_inc(s["glog_ready"], 1)

            def gate_silu(n, par):
                wait(dve, s["gsig_ready"], n + 1)
                wait(dve, s["og2_ready"], n - 1)
                dve.tensor_tensor(silu[:, par * GV:(par + 1) * GV], b_vg[:, GV:2 * GV], g_sig[:, :], ALU.mult
                                  ).then_inc(s["silu_ready"], 1)

            def decay_min(n, par):
                wait(dve, s["gk_done"], n + 1)
                wait(dve, s["kabs_ready"], n + 1)
                wait(dve, s["logsig_ready"], n)
                dve.tensor_scalar(gk_min[:, :], b_qk[:, 2 * P:3 * P], bgk2_col, 0.0, ALU.add, ALU.min
                                  ).then_inc(s["gmin_ready"], 1)

            def decay_log(n, par):
                wait(dve, s["gmin_ready"], n + 1)
                wait(dve, s["ksoft_ready"], n + 1)
                wait(dve, s["cum_ready"], n)
                dve.tensor_tensor(logsig[:, :], gk_min[:, :], gk_soft[:, :], ALU.subtract
                                  ).then_inc(s["logsig_ready"], 1)

            def decay_cumulate(n, par):
                wait(dve, s["logsig_ready"], n + 1)
                for read in ("decq_ready", "deck_ready", "decg_ready"):
                    wait(dve, s[read], n)
                dve.tensor_tensor_scan(cum[:, :], keep, logsig[:, :], 0.0, ALU.mult, ALU.add
                                       ).then_inc(s["cum_ready"], 1)

            def decay_last(n, par):
                wait(dve, s["cum_ready"], n + 1)
                wait(dve, s["decg_ready"], n)
                dve.tensor_scalar(last16[:, :], cum[:, CH - 1:P:CH], GATE, None, ALU.mult).then_inc(s["last_ready"], 1)

            def decay_q(n, par):
                wait(dve, s["decq_ready"], n + 1)
                wait(dve, s["proj_done"], n + 1)
                wait(dve, s["at_done"], n - 1)
                wait(dve, s["go_done"], n - 1)
                for h in range(GH):
                    r = slice(h * GDK, (h + 1) * GDK)
                    ins = dve.scalar_tensor_tensor(out=qg[r, (par * GH + h) * P:(par * GH + h + 1) * P],
                                                   in0=b_qk[r, 0:P], scalar=float(GDK) ** -0.5, in1=dec_q[r, :],
                                                   op0=ALU.mult, op1=ALU.mult)
                ins.then_inc(s["qg_ready"], 1)

            def decay_k(n, par):
                wait(dve, s["deck_ready"], n + 1)
                wait(dve, s["proj_done"], n + 1)
                wait(dve, s["at_done"], n - 1)
                dve.tensor_tensor(kd[:, par * P:(par + 1) * P], b_qk[:, P:2 * P], dec_k[:, :], ALU.mult
                                  ).then_inc(s["kd_ready"], 1)

            def decay_kg(n, par):
                wait(dve, s["decg_ready"], n + 1)
                wait(dve, s["proj_done"], n + 1)
                wait(dve, s["kgt_done"], n)
                dve.tensor_tensor(kg[:, :], b_qk[:, P:2 * P], dec_g[:, :], ALU.mult).then_inc(s["kg_ready"], 1)

            def mask_scores(n, par):
                wait_apart(dve, (s["at_done"], n + 1), (s["intra_done"], n - 1))
                dve.copy_predicated(a_t[:, par * GH * P:(par + 1) * GH * P].rearrange("p (h t) -> p h t", h=GH),
                                    causal_bits.unsqueeze(1).to_broadcast([P, GH, P]),
                                    b_at[:, :].rearrange("p (h t) -> p h t", h=GH)).then_inc(s["atm_ready"], 1)

            def state_1(n, par):
                wait(dve, s["kv_done"], n + 1)
                wait(dve, s["decg_ready"], n + 1)
                wait(dve, s["s2_ready"], n - 1)
                wait(dve, s["go_done"], n - 1)
                st = state[:, par * 2 * GDV:(par + 1) * 2 * GDV]
                dve.scalar_tensor_tensor(out=st[:, GDV:2 * GDV], in0=st[:, 0:GDV], scalar=dlast[:, 2 * par:2 * par + 1],
                                         in1=b_kv[:, P:P + GDV], op0=ALU.mult, op1=ALU.add).then_inc(s["s1_ready"], 1)

            def state_2(n, par):
                wait(dve, s["go_done"], n + 1)
                wait(dve, s["s1_ready"], n + 1)
                st = state[:, par * 2 * GDV:(par + 1) * 2 * GDV]
                dve.scalar_tensor_tensor(out=st[:, 0:GDV], in0=st[:, GDV:2 * GDV],
                                         scalar=dlast[:, 2 * par + 1:2 * par + 2],
                                         in1=b_kv[:, P + GDV:P + 2 * GDV], op0=ALU.mult, op1=ALU.add
                                         ).then_inc(s["s2_ready"], 1)

            def sum_o(n, par):
                wait(dve, s["osq_ready"], n + 1)
                wait(dve, s["oln_ready"], n)
                dve.tensor_reduce(o_ss[:, :], o_sq[:, :].rearrange("p (h v) -> p h v", h=GH), AX.X, ALU.add
                                  ).then_inc(s["oss_ready"], 1)

            def scale_o(n, par):
                wait(dve, s["or_ready"], n + 1)
                wait(dve, s["og2_ready"], n)
                dve.tensor_tensor(og1[:, :].rearrange("p (h v) -> p h v", h=GH),
                                  b_o[:, 0:GV].rearrange("p (h v) -> p h v", h=GH),
                                  o_r[:, :].unsqueeze(2).to_broadcast([P, GH, GDV]), ALU.mult).then_inc(s["og1_ready"], 1)

            def scale_o_t(n, par):
                wait(dve, s["ogt_done"], n + 1)
                wait(dve, s["y_done"], n - 1)
                dve.tensor_scalar(og_t[:, par * 2 * P:(par + 1) * 2 * P], b_og[:, 0:2 * P], rms_col, None, ALU.mult
                                  ).then_inc(s["ogt_ready"], 1)

            def stats_y(n, par):
                wait_apart(dve, (s["y_done"], n + 1), (s["y_aggr"], n))
                dve.bn_stats(st_y[:, :], b_y[:, 0:D]).then_inc(s["y_stats"], 1)

            def aggregate_y(n, par):
                wait_apart(dve, (s["y_stats"], n + 1), (s["yn_ready"], n))
                dve.bn_aggr(mv_y[:, :], st_y[:, :]).then_inc(s["y_aggr"], 1)

            def normalise_y(n, par):
                wait(dve, s["y_rstd"], n + 1)
                wait(dve, s["x1_ready"], n)
                dve.tensor_scalar(yn[:, :], b_y[:, 0:D], mv_y[:, 0:1], rstd_y[:, :], ALU.subtract, ALU.mult
                                  ).then_inc(s["yn_ready"], 1)

            def stats_f(n, par):
                wait_apart(dve, (s["x1_ready"], n + 1), (s["f_aggr"], n))
                dve.bn_stats(st_f[:, :], tile_of(x_attn, n)).then_inc(s["f_stats"], 1)

            def aggregate_f(n, par):
                wait_apart(dve, (s["f_stats"], n + 1), (s["xf_ready"], n))
                dve.bn_aggr(mv_f[:, :], st_f[:, :]).then_inc(s["f_aggr"], 1)

            def normalise_f(n, par):
                wait(dve, s["f_rstd"], n + 1)
                dve.tensor_scalar(tile_of(stream[0], n), tile_of(x_attn, n), mv_f[:, 0:1], rstd_f[:, :],
                                  ALU.subtract, ALU.mult).then_inc(s["xf_ready"], 1)

            def gla_step(k, par):
                staged(normalise_x, k, par, 1)
                staged(aggregate_y, k, par, -2)
                staged(state_2, k, par, -1)
                staged(decay_kg, k, par, 0)
                staged(scale_o, k, par, -1)
                staged(decay_k, k, par, 0)
                staged(decay_q, k, par, 0)
                staged(normalise_y, k, par, -2)
                staged(stats_x, k, par, 2)
                staged(scale_o_t, k, par, -1)
                staged(gate_log, k, par, 0)
                staged(stats_f, k, par, -2)
                staged(mask_scores, k, par, 0)
                staged(aggregate_f, k, par, -2)
                staged(decay_min, k, par, 1)
                staged(state_1, k, par, 0)
                staged(aggregate_x, k, par, 2)
                staged(decay_log, k, par, 1)
                staged(stats_y, k, par, -1)
                staged(decay_cumulate, k, par, 1)
                staged(normalise_f, k, par, -2)
                staged(decay_last, k, par, 1)
                staged(gate_silu, k, par, 0)
                staged(sum_o, k, par, 0)

            dve.wait_ge(d["d_cols"], 13 * 16)
            iterate(dve, gla_step)

            dve.wait_ge(d["d_tab"], 2 * 16)
            dve.wait_ge(d["d_scales"], 2 * DEPTH * 16)
            dve.wait_ge(s["zero_pool"], 1)
            for l in range(DEPTH):
                base = NT * l
                b_q, b_k, b_v, b_t0, b_t1, b_s0, b_s1, b_m = bank

                if l:
                    dve.wait_ge(s["rot2_ready"], base)
                sc = scales[:, l * 2 * DH:(l + 1) * 2 * DH]
                sc_b = sc.unsqueeze(1).to_broadcast([P, TILES_PER_BATCH, 2 * DH])
                dve.tensor_tensor(cos_t[:, :].rearrange("p (t c) -> p t c", c=2 * DH),
                                  cos_base[:, :].rearrange("p (t c) -> p t c", c=2 * DH), sc_b, ALU.mult
                                  ).then_inc(s["cos_ready"], 1)
                for i in range(2):
                    swapped = sc[:, i * DH:(i + 1) * DH].rearrange("p (e r) -> p e r", e=2)[:, ::-1, :]
                    ins = dve.tensor_tensor(
                        sin_t[:, :].rearrange("p (t c e r) -> p t c e r", c=2, e=2, r=DH // 2)[:, :, i],
                        sin_base[:, :].rearrange("p (t c e r) -> p t c e r", c=2, e=2, r=DH // 2)[:, :, i],
                        swapped.unsqueeze(1).to_broadcast([P, TILES_PER_BATCH, 2, DH // 2]), ALU.mult)
                ins.then_inc(s["table_ready"], 1)
                dve.wait_ge(s["table_ready"], l + 1)

                def sum_squares(n, par):
                    N = base + n
                    wait(dve, s["sq_ready"], N + 1)
                    wait(dve, s["ssc_ready"], N)
                    dve.tensor_reduce(ss[:, :], sq[:, :].rearrange("p (h e) -> p h e", e=DH), AX.X, ALU.add
                                      ).then_inc(s["ss_ready"], 1)

                def bound_squares(n, par):
                    N = base + n
                    wait(dve, s["ss_ready"], N + 1)
                    wait(dve, s["ssl_ready"], N)
                    dve.tensor_scalar(ssc[:, :], ss[:, :], 1e-24, None, ALU.max).then_inc(s["ssc_ready"], 1)

                def normalise_qk(n, par):
                    N = base + n
                    wait(dve, s["inv_ready"], N + 1)
                    wait(dve, s["rot1_ready"], N)
                    wait(dve, s["rot2_ready"], N)
                    for i, b_x in enumerate((b_q, b_k)):
                        ins = dve.tensor_tensor(
                            qn[:, i * INNER:(i + 1) * INNER].rearrange("p (h e) -> p h e", e=DH),
                            b_x[:, :].rearrange("p (h e) -> p h e", e=DH),
                            inv[:, i * AH:(i + 1) * AH].unsqueeze(2).to_broadcast([P, AH, DH]), ALU.mult)
                    ins.then_inc(s["qn_ready"], 1)

                def rotate_cos(n, par):
                    N = base + n
                    wait(dve, s["qn_ready"], N + 1)
                    wait(dve, s["qr_ready"], N)
                    for i in range(2):
                        tab = cos_t[:, bass.ds((n - par) * DH + i * DH, DH)]
                        ins = dve.tensor_tensor(
                            rot1[:, i * INNER:(i + 1) * INNER].rearrange("p (h e) -> p h e", e=DH),
                            qn[:, i * INNER:(i + 1) * INNER].rearrange("p (h e) -> p h e", e=DH),
                            tab.unsqueeze(1).to_broadcast([P, AH, DH]), ALU.mult)
                    ins.then_inc(s["rot1_ready"], 1)

                def rotate_add(n, par):
                    N = base + n
                    wait(dve, s["rot1_ready"], N + 1)
                    wait(dve, s["rot2_ready"], N + 1)
                    wait(dve, s["qt_done"], N - 1)
                    wait(dve, s["kt_done"], N - 1)
                    dve.tensor_tensor(qr[:, par * 2 * INNER:(par + 1) * 2 * INNER], rot1[:, :], rot2[:, :], ALU.add
                                      ).then_inc(s["qr_ready"], 1)

                def copy_q_bd(n, par):
                    N = base + n
                    wait(dve, s["qt_done"], N + 1)
                    wait(dve, s["sc0_done"], N - 1)
                    wait(dve, s["sc1_done"], N - 1)
                    dst, src = q_blocks(par, b_t0, 0)
                    dve.tensor_copy(dst, src).then_inc(s["qbd0_ready"], 1)

                def row_max(n, par, w):
                    N = base + n
                    wait(dve, s[f"sc{w}_done"], N + 1)
                    wait(dve, s[f"p{w}_ready"], N)
                    dve.tensor_reduce(neg_max[:, w * PAIRS:(w + 1) * PAIRS],
                                      (b_s0, b_s1)[w][:, :].rearrange("p (c k) -> p c k", c=PAIRS),
                                      AX.X, ALU.max, negate=True).then_inc(s[f"max{w}_ready"], 1)

                def row_reciprocals(n, par, w):
                    N = base + n
                    wait(dve, s[f"p{w}_ready"], N + 1)
                    wait(dve, s[f"pn{w}_ready"], N)
                    r = (par * 2 + w) * PAIRS
                    dve.reciprocal(row_rec[:, w * PAIRS:(w + 1) * PAIRS], row_sum[:, r:r + PAIRS]
                                   ).then_inc(s[f"rs{w}_ready"], 1)

                def copy_probs_t(n, par):
                    N = base + n
                    wait(dve, s["pt1_done"], N + 1)
                    wait(dve, s["pv_done"], N)
                    dve.tensor_copy(probs_t[:, PAIRS * P:2 * PAIRS * P], b_t1[:, :]).then_inc(s["pt1_ready"], 1)

                def add_attention(n, par):
                    N = base + n
                    wait(dve, s["wo_done"], N + 1)
                    dve.tensor_tensor(middle[:, bass.ds((n + 2) * D, D)], b_m[:, P:2 * P], tile_of(stream[l], n),
                                      ALU.add).then_inc(s["mid_ready"], 1)

                def stats_z(n, par):
                    N = base + n
                    wait_apart(dve, (s["hs_ready"], N + 1), (s["z_aggr"], N))
                    dve.bn_stats(st_z[:, :], hcat[:, par * P:(par + 1) * P]).then_inc(s["z_stats"], 1)

                def aggregate_z(n, par):
                    N = base + n
                    wait_apart(dve, (s["z_stats"], N + 1), (s["zn_ready"], N))
                    dve.bn_aggr(mv_z[:, :], st_z[:, :]).then_inc(s["z_aggr"], 1)

                def normalise_z(n, par):
                    N = base + n
                    wait(dve, s["z_rstd"], N + 1)
                    wait(dve, s["zt_done"], N - 1)
                    dve.tensor_scalar(zn[:, par * P:(par + 1) * P], hcat[:, par * P:(par + 1) * P], mv_z[:, 0:1],
                                      rstd_z[:, :], ALU.subtract, ALU.mult).then_inc(s["zn_ready"], 1)

                def attn_step(k, par):
                    staged(copy_q_bd, k, par, 1)
                    staged(sum_squares, k, par, 2)
                    staged(bound_squares, k, par, 2)
                    staged(row_max, k, par, 1, 1)
                    staged(normalise_qk, k, par, 2)
                    staged(copy_probs_t, k, par, 0)
                    staged(row_max, k, par, 1, 0)
                    staged(stats_z, k, par, -1)
                    staged(row_reciprocals, k, par, 1, 1)
                    staged(rotate_cos, k, par, 2)
                    staged(aggregate_z, k, par, -1)
                    staged(rotate_add, k, par, 2)
                    staged(row_reciprocals, k, par, 1, 0)
                    staged(normalise_z, k, par, -1)
                    staged(add_attention, k, par, 0)
                iterate(dve, attn_step)

                NG = NT // GROUP
                FB = GROUP * P
                last = l == DEPTH - 1

                def add_ffn(g):
                    G = l * NG + g
                    for half in range(2):
                        n0 = g * GROUP + 2 * half
                        dve.wait_ge(s["h2_done"], 2 * G + half + 1)
                        dve.tensor_tensor(stream[l + 1][:, n0 * D:(n0 + 2) * D], bank[6 + half][:, 0:2 * D],
                                          middle[:, (n0 + 2) * D:(n0 + 4) * D], ALU.add
                                          ).then_inc(s["ffn_ready"], 1)
                        if last:
                            dve.wait_ge(s["ffn_ready"], 2 * G + half + 1)
                            for n in (n0, n0 + 1):
                                dve.bn_stats(st_o[:, 6 * n:6 * n + 6], tile_of(stream[l + 1], n)).then_inc(s["sto_ready"], 1)

                for g in range(NG):
                    for j in range(NJ):
                        i = (l * NG + g) * NJ + j
                        dve.wait_ge(s["gelu_ready"], i + 1)
                        if g < 2 and j == 0:
                            dve.wait_ge(s["ones_ready"], l + 1)
                        if j == 0:
                            wait(dve, s["h2_done"], 2 * (l * NG + g - 1))
                        at = (((l * NG + g) % 2) * NJ + j) * FB
                        dve.scalar_tensor_tensor(out=hid[0:ROWS[j], at:at + FB], in0=bank[2 * j][0:ROWS[j], :],
                                                 scalar=b1_col(l, 0, j),
                                                 in1=gelu[0:ROWS[j], (i % 2) * FB:(i % 2 + 1) * FB],
                                                 op0=ALU.add, op1=ALU.mult).then_inc(s["hid_ready"], 1)
                    if g:
                        add_ffn(g - 1)
                add_ffn(NG - 1)

            dve.wait_ge(s["sto_ready"], NT)
            for n in range(NT):
                ins = dve.bn_aggr(mv_o[:, 2 * n:2 * n + 2], st_o[:, 6 * n:6 * n + 6])
            ins.then_inc(s["mvo_ready"], 1)
            dve.wait_ge(s["rstdo_ready"], 1)
            for n in range(NT):
                ins = dve.tensor_scalar(tile_of(xo, n), tile_of(stream[DEPTH], n), mv_o[:, 2 * n:2 * n + 1],
                                        rstd_o[:, n:n + 1], ALU.subtract, ALU.mult)
                if n % GROUP == GROUP - 1:
                    ins.then_inc(s["xo_ready"], 1)
                    g = n // GROUP
                    c = slice(g * GROUP * D, (g + 1) * GROUP * D)
                    dve.wait_ge(s["xo_ready"], 1 + g)
                    dve.tensor_tensor(res[:, c], xo[:, c], x_attn[:, c], ALU.add).then_inc(s["res_ready"], 1)


def square_constants():
    import numpy as np
    i = np.arange(128)
    ident = (i[:, None] == i[None, :])
    shift = (i[:, None] + 1 == i[None, :])
    carry = (i[:, None] == 127) & (i[None, :] == 0)
    q = i[:, None] % 64
    k = i[None, :] % 64
    second = i[None, :] >= 64
    low = np.float32(-1e30)
    mask_b = np.where(np.where(second, k <= q, k >= q), np.float32(0), low)
    mask_a = np.where(np.where(second, k >= q, k <= q), np.float32(0), low)
    mask_a0 = np.where(~second & (k <= q), np.float32(0), low)
    causal = (i[:, None] // 64 == i[None, :] // 64) & (i[:, None] <= i[None, :])
    keep = np.broadcast_to(i[None, :] % 64 != 0, (128, 128))
    return np.concatenate([np.asarray(a, np.float32) for a in
                           (ident, shift, carry, mask_a, mask_b, mask_a0, causal, keep)], axis=1)


def rotary_tables(n, dh, window, qk_scale):
    import numpy as np
    half = np.arange(0, dh, 2, dtype=np.float32)
    freq = (np.float32(1.0) / np.power(np.float32(10000.0), half / np.float32(dh))).astype(np.float32)
    t = np.arange(n, dtype=np.float32)
    f = (t[:, None] * freq[None, :]).astype(np.float32).astype(np.float64)
    f = np.concatenate([f, f], axis=-1)
    base = ((half + np.float32(0.4 * dh)) / np.float32(1.4 * dh)).astype(np.float64)
    power = (t - n // 2).astype(np.float64) / (window // 2)
    sc = base[None, :] ** power[:, None]
    sc = np.concatenate([sc, sc], axis=-1)
    sign = np.where(np.arange(dh) < dh // 2, -1.0, 1.0)
    tabs = []
    for g in (np.cos(f), np.sin(f) * sign):
        both = np.stack([g * sc * qk_scale, g / sc], axis=1)
        tabs.append(np.ascontiguousarray(both.reshape(n // 128, 128, 2 * dh).transpose(1, 0, 2)
                                         .reshape(128, -1).astype(np.float32)))
    return tabs


_INS = ["L0_attn_x", "L0_attn_Wq", "L0_attn_Wk", "L0_attn_Wv", "L0_attn_Wg", "L0_attn_Wgk1", "L0_attn_Wgk2",
        "L0_attn_bgk2", "L0_attn_Wo", "L0_attn_rms_w", "L0_ffn_wqkv", "L0_ffn_q_scale", "L0_ffn_k_scale",
        "L0_ffn_wo", "L0_ffn_ln_g", "L0_ffn_ln_b", "L0_ffn_w1", "L0_ffn_b1", "L0_ffn_w2", "L0_ffn_b2"]


def kernel(**inputs):
    import numpy as np
    import concourse.bacc as bacc
    from concourse.bass_utils import run_bass_kernel_spmd

    nc = bacc.Bacc("TRN2", target_bir_lowering=False, num_devices=1)
    arrays = {f"in_{name}": np.ascontiguousarray(inputs[name]) for name in _INS}
    arrays["square_consts"] = square_constants()
    arrays["rotary_cos"], arrays["rotary_sin"] = rotary_tables(arrays["in_L0_attn_x"].shape[1], 64, 64, 8.0)
    args = [nc.dram_tensor(name, a.shape, mybir.dt.from_np(a.dtype), kind="ExternalInput").ap()
            for name, a in arrays.items()]
    shape = arrays["in_L0_attn_x"].shape
    args.append(nc.dram_tensor("out_x", shape, F32, kind="ExternalOutput").ap())
    build_program(nc, *args)
    r = run_bass_kernel_spmd(nc, [arrays], core_ids=[0])
    return r.results[0]["out_x"]
```

```python
from contextlib import ExitStack

import concourse.bass as bass
from concourse import mybir

F32 = mybir.dt.float32
BF16 = mybir.dt.bfloat16
U32 = mybir.dt.uint32
ALU = mybir.AluOpType
ACT = mybir.ActivationFunctionType
AX = mybir.AxisListType

P = 128
EPS = 1e-5
LN2 = 0.6931471805599453


def wait(engine, semaphore, count):
    if isinstance(count, int) and count <= 0:
        return
    engine.wait_ge(semaphore, count)


def build_program(nc, x, Wq, Wk, Wv, Wg, Wgk1, Wgk2, bgk2, Wo, rms_w,
                  wqkv, q_scale, k_scale, wo, ln_g, ln_b, w1, b1, w2, b2,
                  square_consts, rotary_cos, rotary_sin, out):
    B, T, D = x.shape
    TILES_PER_BATCH = T // P
    NT = B * TILES_PER_BATCH
    GH, GDK, GDV = 4, Wq.shape[1] // 4, Wv.shape[1] // 4
    GV = GH * GDV
    RANK = Wgk1.shape[1]
    CH = 64
    GATE = 1.0 / 16.0
    DEPTH, _, QKV = wqkv.shape
    INNER = QKV // 3
    DH = q_scale.shape[1]
    AH = INNER // DH
    PAIRS = AH // 2
    W = 64
    HID = w2.shape[1]
    NJ = (HID + P - 1) // P
    ROWS = [min(P, HID - j * P) for j in range(NJ)]
    GROUP = 4
    assert B == 2 and D == P and 2 * CH == P and 2 * W == P

    ctx = ExitStack()
    with ctx:
        def sb(name, cols, dt=F32):
            return ctx.enter_context(nc.sbuf_tensor(name, [P, cols], dt))

        def sems(names):
            return {k: ctx.enter_context(nc.semaphore(k)) for k in names.split()}

        bank = [ctx.enter_context(nc.psum_tensor(f"bank{i}", [P, 512], F32)) for i in range(8)]

        consts = sb("consts", 8 * P)
        ident, causal, keep, shift, carry, mask_a, mask_b, mask_a0 = (
            consts[:, i * P:(i + 1) * P] for i in range(8))
        causal_bits = causal.bitcast(U32)
        ident_bf = sb("ident_bf", P, BF16)
        masks_bf = sb("masks_bf", 3 * P, BF16)
        cos_base = sb("cos_base", TILES_PER_BATCH * 2 * DH)
        sin_base = sb("sin_base", TILES_PER_BATCH * 2 * DH)
        cos_t = sb("cos_t", TILES_PER_BATCH * 2 * DH)
        sin_t = sb("sin_t", TILES_PER_BATCH * 2 * DH)
        scales = sb("scales", DEPTH * 2 * DH)
        wqk_sb = sb("wqk_sb", 2 * P)
        wvg_sb = sb("wvg_sb", 2 * GV)
        wgk1_sb = sb("wgk1_sb", RANK)
        wgk2_sb = sb("wgk2_sb", P)
        wout_sb = sb("wout_sb", 2 * D)
        columns = sb("columns", 4 + 2 * DEPTH + DEPTH * 2 * NJ)
        bgk2_col, rms_col = columns[:, 0:1], columns[:, 1:2]
        eps_col, norm_bias_col = columns[:, 2:3], columns[:, 3:4]
        lng_col = [columns[:, 4 + l:5 + l] for l in range(DEPTH)]
        lnb_col = [columns[:, 4 + DEPTH + l:5 + DEPTH + l] for l in range(DEPTH)]
        B1_AT = 4 + 2 * DEPTH
        wqkv_sb = sb("wqkv_sb", DEPTH * QKV)
        wo_sb = sb("wo_sb", DEPTH * PAIRS * D)
        w1_sb = sb("w1_sb", DEPTH * 2 * HID)
        w2_sb = sb("w2_sb", DEPTH * NJ * D)

        def b1_col(l, half, j):
            at = B1_AT + (l * 2 + half) * NJ + j
            return columns[0:ROWS[j], at:at + 1]

        x_in = sb("x_in", NT * D)
        x_attn = sb("x_attn", NT * D)
        ping, pong = sb("ping", NT * D), sb("pong", NT * D)
        stream = [(ping, pong)[l % 2] for l in range(DEPTH + 1)]
        middle = sb("middle", (NT + 2) * D)
        z_t = sb("z_t", NT * P)

        def tile_of(buf, n):
            return buf[:, bass.ds(n * D, D)]

        st_x = sb("st_x", 2 * 6)
        mv_x = sb("mv_x", 2 * 2)
        ln_x = sb("ln_x", 2)
        rstd_x = sb("rstd_x", 2)
        xn = sb("xn", 2 * P)
        xn_t = sb("xn_t", 2 * P)
        v_sb = sb("v_sb", 2 * GV)
        g_soft = sb("g_soft", GV)
        g_sig = sb("g_sig", GV)
        silu = sb("silu", 2 * GV)
        low = sb("low", P)
        gk_soft = sb("gk_soft", P)
        gk_min = sb("gk_min", P)
        logsig = sb("logsig", P)
        cum = sb("cum", P)
        last16 = sb("last16", 2)
        dlast = sb("dlast", 2 * 2)
        dec_q = sb("dec_q", P)
        dec_k = sb("dec_k", P)
        dec_g = sb("dec_g", P)
        qg = sb("qg", 2 * GH * P)
        kd = sb("kd", 2 * P)
        kg = sb("kg", P)
        kg_tok = sb("kg_tok", 2 * 2 * P)
        a_t = sb("a_t", 2 * GH * P)
        state = sb("state", 2 * 2 * GDV)
        o_sq = sb("o_sq", GV)
        o_ss = sb("o_ss", GH)
        o_ln = sb("o_ln", GH)
        o_r = sb("o_r", GH)
        og1 = sb("og1", GV)
        og2 = sb("og2", 2 * GV)
        og_t = sb("og_t", 2 * 2 * P)
        st_y = sb("st_y", 6)
        mv_y = sb("mv_y", 2)
        ln_y = sb("ln_y", 1)
        rstd_y = sb("rstd_y", 1)
        yn = sb("yn", P)
        st_f = sb("st_f", 6)
        mv_f = sb("mv_f", 2)
        ln_f = sb("ln_f", 1)
        rstd_f = sb("rstd_f", 1)

        h_t = sb("h_t", 2 * (P + 1))
        x_slot = sb("x_slot", 2 * P)
        sq = sb("sq", 2 * INNER)
        ss = sb("ss", 2 * AH)
        ssc = sb("ssc", 2 * AH)
        ss_ln = sb("ss_ln", 2 * AH)
        inv = sb("inv", 2 * AH)
        qn = sb("qn", 2 * INNER)
        rot1 = sb("rot1", 2 * INNER)
        rot2 = sb("rot2", 2 * INNER)
        qr = sb("qr", 2 * 2 * INNER)
        q_bd = sb("q_bd", 2 * PAIRS * 2 * P)
        KC = P + W
        k_t = sb("k_t", 2 * PAIRS * KC)
        v_cur = sb("v_cur", 2 * INNER)
        v_mix = sb("v_mix", 2 * INNER)
        neg_max = sb("neg_max", 2 * PAIRS)
        row_sum = sb("row_sum", 2 * 2 * PAIRS)
        row_rec = sb("row_rec", 2 * PAIRS)
        PROBS, PROBS_T = 2 * 2 * PAIRS * P, 2 * PAIRS * P
        shared = sb("shared", max(PROBS + PROBS_T, 2 * NJ * GROUP * P))
        probs, probs_t = shared[:, 0:PROBS], shared[:, PROBS:PROBS + PROBS_T]
        o_t = sb("o_t", 2 * PAIRS * P)
        hcat = sb("hcat", 2 * P)
        st_z = sb("st_z", 6)
        mv_z = sb("mv_z", 2)
        ln_z = sb("ln_z", 1)
        rstd_z = sb("rstd_z", 1)
        zn = sb("zn", 2 * P)

        gelu = qr[:, 2 * INNER:2 * INNER + 2 * GROUP * P]
        hid = shared[:, 0:2 * NJ * GROUP * P]
        st_o = sb("st_o", NT * 6)
        mv_o = sb("mv_o", NT * 2)
        ln_o = sb("ln_o", NT)
        rstd_o = sb("rstd_o", NT)
        shift_o = sb("shift_o", NT)
        ON_ACT = 6
        xo, res = x_in, stream[DEPTH - 1]

        d = sems("d_ident d_const d_masks d_x0 d_x1 d_gla d_gcols d_qkv d_cols d_scales d_tab d_ffn d_out")
        s = sems(
            "zero_dve zero_gla zero_pool cast_consts col_consts "
            "x_stats x_aggr x_ln x_rstd xn_ready xt_done xnt_ready vg_done lowp_done proj_done v_ready gabs_ready "
            "gexp_ready gsoft_ready glog_ready gsig_ready silu_ready low_ready gk_done kabs_ready kexp_ready "
            "ksoft_ready gmin_ready logsig_ready cum_ready last_ready decq_ready deck_ready decg_ready qg_ready "
            "kd_ready kg_ready at_done kgt_done atm_ready kgtok_ready kv_done s1_ready s2_ready intra_done go_done "
            "osq_ready oss_ready oln_ready or_ready og1_ready og2_ready ogt_done ogt_ready y_done y_stats y_aggr "
            "y_ln y_rstd yn_ready x1_ready f_stats f_aggr f_ln f_rstd xf_ready "
            "slot_ready carry_zero table_ready cos_ready xtr_done carried ht_ready qk_done sq_ready ss_ready ssc_ready "
            "ssl_ready inv_ready "
            "qn_ready rot1_ready rot2_ready qr_ready qt_done kt_done qbd0_ready qbd1_ready kprev_ready kt_ready "
            "sc0_done sc1_done max0_ready max1_ready p0_ready p1_ready rs0_ready rs1_ready pn0_ready pn1_ready "
            "pt0_done pt1_done "
            "pt0_ready pt1_ready v_done vup_ready vcur_ready vmix_ready pv0_done pv_done ot_ready wo_done mid_ready "
            "half_ready hs_done hs_ready z_stats z_aggr z_ln z_rstd zn_ready zt_done z_ready "
            "ones_ready h1_done gelu_ready hid_ready h2_done ffn_ready sto_ready mvo_ready "
            "lno_ready rstdo_ready shifto_ready xo_ready xo_act_ready res_ready last_res_ready")

        def q_blocks(par, b_t, h2):
            r = slice(h2 * DH, (h2 + 1) * DH)
            dst = q_bd[r, par * PAIRS * 2 * P:(par + 1) * PAIRS * 2 * P].rearrange("p (c w i) -> p c w i", c=PAIRS, w=2)
            return (dst[:, :, :, h2 * W:(h2 + 1) * W],
                    b_t[r, :].rearrange("p (c w i) -> p c w i", c=PAIRS, w=2))

        dve_engine = nc.vector

        def wait_apart(engine, *waits):
            if not isinstance(waits[0][1], int):
                waits = [(semaphore, engine.snap(engine.to_reg(count))) for semaphore, count in waits]
                engine.wait_ge(s["zero_dve" if engine is dve_engine else "zero_pool"], 1)
            for semaphore, count in waits:
                wait(engine, semaphore, count)

        block = ctx.enter_context(nc.Block())

        def iterate(engine, step, first=-2, end=NT + 2, before={}):
            for k in range(first, 4):
                if k in before:
                    before[k]()
                step(k, k % 2)
            with engine.Fori(4, NT - 3, 2) as k:
                step(k, 0)
                step(k + 1, 1)
            for k in range(NT - 2, end):
                if k in before:
                    before[k]()
                step(k, k % 2)

        def staged(fn, k, parity, lag, *args):
            n = k + lag
            if isinstance(n, int) and not 0 <= n < NT:
                return
            fn(n, (parity + lag) % 2, *args)

        NG, FB = NT // GROUP, GROUP * P
        LAST = NT - 1

        def block_banks(i):
            return ((6, 7), (4, 5), (1, 2), (0, 3))[i] if i < 4 else ((6, 7), (4, 5))[i % 2]

        def product_bank(g, half):
            return 7 if (g, half) == (NG - 1, 1) else 3

        def capped(count, most):
            return min(count, most) if isinstance(count, int) else count

        @block.sync
        def _(sp):
            xv = x_in[:, :].rearrange("p (n d) -> p n d", d=D)
            sp.dma_start(xv[:, 0:B, :], x[:, 0:P, :].rearrange("b p d -> p b d")).then_inc(d["d_x0"], 16)
            sp.dma_start(consts[:, 0:P], square_consts[:, 0:P]).then_inc(d["d_ident"], 16)
            sp.dma_start(wgk1_sb[:, :], Wgk1).then_inc(d["d_gla"], 16)
            sp.dma_start(wgk2_sb[0:RANK, :], Wgk2).then_inc(d["d_gla"], 16)
            sp.dma_start(wqk_sb[:, 0:P], Wq).then_inc(d["d_gla"], 16)
            sp.dma_start(wqk_sb[:, P:2 * P], Wk).then_inc(d["d_gla"], 16)
            sp.dma_start(wvg_sb[:, 0:GV], Wv).then_inc(d["d_gla"], 16)
            sp.dma_start(wvg_sb[:, GV:2 * GV], Wg).then_inc(d["d_gla"], 16)
            sp.dma_start(consts[:, P:3 * P], square_consts[:, P:3 * P]).then_inc(d["d_const"], 16)
            sp.dma_start(wout_sb[:, :].rearrange("p (c n) -> p c n", c=2),
                         Wo.rearrange("(c p) n -> p c n", p=P)).then_inc(d["d_gla"], 16)
            for b in range(B):
                sp.dma_start(xv[:, B + b:NT:B, :],
                             x[b, P:T, :].rearrange("(t p) d -> p t d", p=P)).then_inc(d["d_x1"], 16)
            sp.dma_start(consts[:, 3 * P:8 * P], square_consts[:, 3 * P:8 * P]).then_inc(d["d_masks"], 16)
            for l in range(DEPTH):
                for i, src in enumerate((q_scale, k_scale)):
                    sp.dma_start(scales[:, (l * 2 + i) * DH:(l * 2 + i + 1) * DH],
                                 src[l, :].partition_broadcast(P)).then_inc(d["d_scales"], 16)
            sp.dma_start(cos_base[:, :], rotary_cos).then_inc(d["d_tab"], 16)
            sp.dma_start(sin_base[:, :], rotary_sin).then_inc(d["d_tab"], 16)
            sp.dma_start(wqkv_sb[:, :].rearrange("p (l n) -> p l n", l=DEPTH),
                         wqkv.rearrange("l k n -> k l n")).then_inc(d["d_qkv"], 16)
            sp.dma_start(wo_sb[:, :].rearrange("p (l c n) -> p l c n", l=DEPTH, c=PAIRS),
                         wo.rearrange("l (c p) n -> p l c n", p=P)).then_inc(d["d_qkv"], 16)
            sp.dma_start(w1_sb[:, :].rearrange("p (l n) -> p l n", l=DEPTH),
                         w1.rearrange("l k n -> k l n")).then_inc(d["d_ffn"], 16)
            w2v = w2_sb[:, :].rearrange("p (l c n) -> p l c n", l=DEPTH, c=NJ)
            for l in range(DEPTH):
                sp.dma_start(w2v[:, l, 0:NJ - 1, :],
                             w2[l, 0:(NJ - 1) * P, :].rearrange("(c p) n -> p c n", p=P)).then_inc(d["d_ffn"], 16)
                sp.dma_start(w2v[0:ROWS[-1], l, NJ - 1, :], w2[l, (NJ - 1) * P:HID, :]).then_inc(d["d_ffn"], 16)
                sp.dma_start(w2v[ROWS[-1]:ROWS[-1] + 1, l, NJ - 1, :], b2[l:l + 1, :]).then_inc(d["d_ffn"], 16)
            ov = res[:, :].rearrange("p (n d) -> p n d", d=D)
            for g in range(NG - 1):
                sp.wait_ge(s["res_ready"], g + 1)
                for b in range(B):
                    t0 = g * GROUP // B
                    sp.dma_start(out[b, t0 * P:(t0 + GROUP // B) * P, :].rearrange("(t p) d -> p t d", p=P),
                                 ov[:, g * GROUP + b:(g + 1) * GROUP:B, :]).then_inc(d["d_out"], 16)
            for i in range(2):
                sp.wait_ge(s["last_res_ready"], i + 1)
                t0 = TILES_PER_BATCH - 2 + i
                sp.dma_start(out[:, t0 * P:(t0 + 1) * P, :].rearrange("b p d -> p b d"),
                             ov[:, t0 * B:(t0 + 1) * B, :]).then_inc(d["d_out"], 16)
            sp.wait_ge(d["d_out"], 16 * (B * (NG - 1) + 2))

        @block.gpsimd
        def _(pool):
            pool.dma_start(columns[:, 0:1], bgk2.rearrange("(p a) -> p a", a=1)).then_inc(d["d_gcols"], 16)
            for h2 in range(P // GDV):
                pool.dma_start(columns[h2 * GDV:(h2 + 1) * GDV, 1:2],
                               rms_w.rearrange("(p a) -> p a", a=1)).then_inc(d["d_gcols"], 16)
            for buf in (kg_tok, a_t):
                ins = pool.memset(buf[:, :], 0.0)
            ins.then_inc(s["zero_gla"], 1)
            with nc.allow_non_contiguous_dma(reason="per-partition columns of the small vectors"):
                pool.dma_start(columns[:, 4:4 + DEPTH], ln_g.rearrange("l p -> p l")).then_inc(d["d_cols"], 16)
                pool.dma_start(columns[:, 4 + DEPTH:4 + 2 * DEPTH],
                               ln_b.rearrange("l p -> p l")).then_inc(d["d_cols"], 16)
                for l in range(DEPTH):
                    for half in range(2):
                        at = B1_AT + (l * 2 + half) * NJ
                        pool.dma_start(columns[:, at:at + NJ - 1],
                                       b1[l, half * HID:half * HID + (NJ - 1) * P].rearrange("(j p) -> p j", p=P)
                                       ).then_inc(d["d_cols"], 16)
                        pool.dma_start(columns[0:ROWS[-1], at + NJ - 1:at + NJ],
                                       b1[l, half * HID + (NJ - 1) * P:(half + 1) * HID].rearrange("(p a) -> p a", a=1)
                                       ).then_inc(d["d_cols"], 16)
            for buf in (q_bd, k_t, v_cur, v_mix):
                pool.memset(buf[:, :], 0.0)
            pool.memset(middle[:, 0:2 * D], 0.0)
            pool.memset(h_t[:, :], 0.0).then_inc(s["zero_pool"], 1)
            pool.wait_ge(s["zero_pool"], 1)

            def cos_table(l):
                sc_b = scales[:, l * 2 * DH:(l + 1) * 2 * DH].unsqueeze(1).to_broadcast([P, TILES_PER_BATCH, 2 * DH])
                pool.tensor_tensor(cos_t[:, :].rearrange("p (t c) -> p t c", c=2 * DH),
                                   cos_base[:, :].rearrange("p (t c) -> p t c", c=2 * DH), sc_b, ALU.mult
                                   ).then_inc(s["cos_ready"], 1)

            def sin_table(l):
                for i in range(2):
                    at = (l * 2 + i) * DH
                    swapped = scales[:, at:at + DH].rearrange("p (e r) -> p e r", e=2)[:, ::-1, :]
                    ins = pool.tensor_tensor(
                        sin_t[:, :].rearrange("p (t c e r) -> p t c e r", c=2, e=2, r=DH // 2)[:, :, i],
                        sin_base[:, :].rearrange("p (t c e r) -> p t c e r", c=2, e=2, r=DH // 2)[:, :, i],
                        swapped.unsqueeze(1).to_broadcast([P, TILES_PER_BATCH, 2, DH // 2]), ALU.mult)
                ins.then_inc(s["table_ready"], 1)

            def first_cos_table():
                pool.wait_ge(d["d_tab"], 2 * 16)
                pool.wait_ge(d["d_scales"], 2 * DEPTH * 16)
                cos_table(0)

            def gate_o(n, par):
                wait(pool, s["og1_ready"], n + 1)
                wait(pool, s["silu_ready"], n + 1)
                wait(pool, s["ogt_done"], n - 1)
                pool.tensor_tensor(og2[:, par * GV:(par + 1) * GV], og1[:, :], silu[:, par * GV:(par + 1) * GV],
                                   ALU.mult).then_inc(s["og2_ready"], 1)

            def add_y(n, par):
                wait(pool, s["yn_ready"], n + 1)
                pool.tensor_tensor(tile_of(x_attn, n), tile_of(x_in, n), yn[:, :], ALU.add).then_inc(s["x1_ready"], 1)

            def gla_step(k, par):
                staged(gate_o, k, par, 0)
                staged(add_y, k, par, -1)
            iterate(pool, gla_step, before={2: first_cos_table, 3: lambda: sin_table(0)})

            for l in range(DEPTH):
                base = NT * l

                def keep_prev_keys(n, par):
                    N = base + n
                    kv = k_t[:, par * PAIRS * KC:(par + 1) * PAIRS * KC].rearrange("p (c k) -> p c k", k=KC)
                    wait_apart(pool, (s["sc0_done"], N - 1), (s["sc1_done"], N - 1), (s["kt_ready"], N - 1),
                               (s["vmix_ready"], N - 1),
                               (s["vup_ready"], N))
                    pool.tensor_scalar(kv[:, :, P:KC], kv[:, :, W:P], 1.0, 0.0, ALU.mult, ALU.add
                                       ).then_inc(s["kprev_ready"], 1)

                def keep_prev_values(n, par):
                    N = base + n
                    c = slice(par * INNER, (par + 1) * INNER)
                    wait_apart(pool, (s["pv_done"], N - 1), (s["vcur_ready"], N - 1),
                               (s["rot2_ready"], N + 1),
                               (s["kprev_ready"], N + 1),
                               (s["pn0_ready"], N - 1),
                               (s["vmix_ready"], N - 1))
                    pool.tensor_scalar(v_mix[W:P, c], v_cur[W:P, c], 1.0, 0.0, ALU.mult, ALU.add
                                       ).then_inc(s["vup_ready"], 1)

                def mix_values(n, par):
                    N = base + n
                    c = slice(par * INNER, (par + 1) * INNER)
                    wait_apart(pool, (s["vcur_ready"], N + 1), (s["pv_done"], N - 1),
                               (s["pn1_ready"], N + 1),
                               (s["vup_ready"], capped(N + 2, base + NT)),
                               (s["rot2_ready"], capped(N + 2, base + NT)))
                    pool.tensor_scalar(v_mix[0:W, c], v_cur[0:W, c], 1.0, 0.0, ALU.mult, ALU.add
                                       ).then_inc(s["vmix_ready"], 1)

                def rotate_sin(n, par):
                    N = base + n
                    if isinstance(n, int) and n == 0:
                        pool.wait_ge(s["table_ready"], l + 1)
                    wait_apart(pool, (s["qn_ready"], N + 1), (s["qr_ready"], N),
                               (s["vmix_ready"], N - 1),
                               (s["vup_ready"], N))
                    for i in range(2):
                        a = qn[:, i * INNER:(i + 1) * INNER].rearrange("p (h e r) -> p h e r", h=AH, e=2)
                        o = rot2[:, i * INNER:(i + 1) * INNER].rearrange("p (h e r) -> p h e r", h=AH, e=2)
                        tab = sin_t[:, bass.ds((n - par) * DH + i * DH, DH)].rearrange("p (e r) -> p e r", e=2)
                        ins = pool.tensor_tensor(o, a[:, :, ::-1, :],
                                                 tab.unsqueeze(1).to_broadcast([P, AH, 2, DH // 2]), ALU.mult)
                    ins.then_inc(s["rot2_ready"], 1)

                def normalise_probs(n, par, w):
                    N = base + n
                    if w == 0:
                        wait_apart(pool, (s["rs0_ready"], N + 1),
                               (s["vmix_ready"], N + 1),
                               (s["vup_ready"], capped(N + 2, base + NT)))
                    else:
                        wait_apart(pool, (s["rs1_ready"], N + 1),
                               (s["vup_ready"], capped(N + 2, base + NT)),
                               (s["vmix_ready"], N))
                    for c in range(PAIRS):
                        wp = w * PAIRS + c
                        at = (par * 2 * PAIRS + wp) * P
                        ins = pool.tensor_scalar(probs[:, at:at + P], probs[:, at:at + P],
                                                 row_rec[:, wp:wp + 1], 1.0, ALU.mult, ALU.mult)
                    ins.then_inc(s[f"pn{w}_ready"], 1)

                if l:
                    pool.wait_ge(s["v_done"], base)
                    pool.wait_ge(s["qk_done"], base)
                    for b in range(B):
                        c = b * (P + 1) + P
                        ins = pool.memset(h_t[:, c:c + 1], 0.0)
                    ins.then_inc(s["carry_zero"], 1)

                def step(k, par):
                    staged(mix_values, k, par, -1)
                    staged(normalise_probs, k, par, -1, 0)
                    staged(keep_prev_keys, k, par, 1)
                    staged(rotate_sin, k, par, 1)
                    staged(keep_prev_values, k, par, 1)
                    staged(normalise_probs, k, par, 0, 1)
                iterate(pool, step)

                pool.wait_ge(s["z_ready"], base + NT)
                for slot in range(2):
                    at = (slot * NJ + NJ - 1) * GROUP * P
                    ins = pool.memset(hid[ROWS[-1] // 32 * 32:P, at:at + GROUP * P], 1.0)
                ins.then_inc(s["ones_ready"], 1)
                pool.wait_ge(s["ones_ready"], l + 1)
                if l + 1 < DEPTH:
                    pool.wait_ge(s["rot1_ready"], base + NT)
                    cos_table(l + 1)
                    sin_table(l + 1)

            for g in range(NT // GROUP - 1):
                c = slice(g * GROUP * D, (g + 1) * GROUP * D)
                pool.wait_ge(s["xo_ready"], min(2 * (g + 1), ON_ACT // 2))
                wait(pool, s["xo_act_ready"], (g + 1) * GROUP - ON_ACT)
                pool.tensor_tensor(res[:, c], xo[:, c], x_attn[:, c], ALU.add).then_inc(s["res_ready"], 1)

        @block.tensor
        def _(pe):
            def mm(o, w, m, start=True, stop=True, skip=False):
                return pe.matmul(o, w, m, start=start, stop=stop, skip_group_check=skip)

            b_xg, b_qk, b_vg, b_at, b_kv, b_o, b_og, b_y = bank

            def transpose_x(n, par):
                wait(pe, s["xn_ready"], n + 1)
                wait(pe, s["kabs_ready"], n)
                wait(pe, s["gmin_ready"], n)
                wait(pe, s["low_ready"], n)
                wait(pe, s["xnt_ready"], n)
                pe.transpose(b_xg[:, 0:P], xn[:, par * P:(par + 1) * P], ident).then_inc(s["xt_done"], 1)

            def project_vg(n, par):
                wait(pe, s["xnt_ready"], n + 1)
                wait(pe, s["v_ready"], n)
                wait(pe, s["silu_ready"], n)
                mm(b_vg[:, :], xn_t[:, par * P:(par + 1) * P], wvg_sb[:, :]).then_inc(s["vg_done"], 1)

            def project_low(n, par):
                if isinstance(n, int) and n == 0:
                    pe.wait_ge(d["d_gla"], 7 * 16)
                wait(pe, s["xnt_ready"], n + 1)
                wait(pe, s["xnt_ready"], n + 1)
                wait(pe, s["kabs_ready"], n)
                wait(pe, s["gmin_ready"], n)
                wait(pe, s["low_ready"], n)
                mm(b_xg[0:RANK, 2 * P:3 * P], wgk1_sb[:, :], xn_t[:, par * P:(par + 1) * P]
                   ).then_inc(s["lowp_done"], 1)

            def project_qk(n, par):
                a = xn_t[:, par * P:(par + 1) * P]
                wait(pe, s["xnt_ready"], n + 1)
                for read in ("qg_ready", "kd_ready", "kg_ready"):
                    wait(pe, s[read], n)
                mm(b_qk[:, 0:P], wqk_sb[:, 0:P], a)
                mm(b_qk[:, P:2 * P], wqk_sb[:, P:2 * P], a).then_inc(s["proj_done"], 1)

            def project_gate(n, par):
                wait(pe, s["low_ready"], n + 1)
                wait(pe, s["low_ready"], n + 1)
                wait(pe, s["xnt_ready"], n + 1)
                wait(pe, s["kabs_ready"], n)
                wait(pe, s["gmin_ready"], n)
                mm(b_xg[:, P:2 * P], wgk2_sb[0:RANK, :], low[0:RANK, :]).then_inc(s["gk_done"], 1)

            def intra_scores(n, par):
                wait(pe, s["qg_ready"], n + 1)
                wait(pe, s["kd_ready"], n + 1)
                wait(pe, s["atm_ready"], n)
                mm(b_at[:, :], kd[:, par * P:(par + 1) * P], qg[:, par * GH * P:(par + 1) * GH * P]
                   ).then_inc(s["at_done"], 1)

            def transpose_kg(n, par):
                wait(pe, s["kg_ready"], n + 1)
                wait(pe, s["s1_ready"], n)
                wait(pe, s["s2_ready"], n)
                pe.transpose(b_kv[:, 0:P], kg[:, :], ident).then_inc(s["kgt_done"], 1)

            def key_values(n, par):
                wait(pe, s["kgtok_ready"], n + 1)
                wait(pe, s["v_ready"], n + 1)
                for c in range(2):
                    for h in range(GH):
                        at = (par * 2 + c) * P + h * GDK
                        ins = mm(b_kv[h * GDK:(h + 1) * GDK, P + c * GDV:P + (c + 1) * GDV],
                                 kg_tok[:, at:at + GDK], v_sb[:, par * GV + h * GDV:par * GV + (h + 1) * GDV])
                ins.then_inc(s["kv_done"], 1)

            def intra_outputs(n, par):
                wait(pe, s["atm_ready"], n + 1)
                wait(pe, s["v_ready"], n + 1)
                wait(pe, s["og1_ready"], n)
                for h in range(GH):
                    ins = mm(b_o[:, h * GDV:(h + 1) * GDV], a_t[:, (par * GH + h) * P:(par * GH + h + 1) * P],
                             v_sb[:, par * GV + h * GDV:par * GV + (h + 1) * GDV], start=(h == 0), stop=False, skip=True)
                ins.then_inc(s["intra_done"], 1)

            def state_outputs(n, par):
                wait(pe, s["s2_ready"], n - 1)
                wait(pe, s["s1_ready"], n + 1)
                for c in range(2):
                    for h in range(GH):
                        ins = mm(b_o[c * CH:(c + 1) * CH, h * GDV:(h + 1) * GDV],
                                 qg[:, (par * GH + h) * P + c * CH:(par * GH + h) * P + (c + 1) * CH],
                                 state[:, (par * 2 + c) * GDV:(par * 2 + c + 1) * GDV],
                                 start=False, stop=True, skip=True)
                ins.then_inc(s["go_done"], 1)

            def transpose_o(n, par):
                wait(pe, s["og2_ready"], n + 1)
                wait(pe, s["ogt_ready"], n)
                for c in range(2):
                    ins = pe.transpose(b_og[:, c * P:(c + 1) * P],
                                       og2[:, par * GV + c * P:par * GV + (c + 1) * P], ident)
                ins.then_inc(s["ogt_done"], 1)

            def project_out(n, par):
                wait(pe, s["ogt_ready"], n + 1)
                wait(pe, s["yn_ready"], n)
                for c in range(2):
                    ins = mm(b_y[:, 0:D], og_t[:, (par * 2 + c) * P:(par * 2 + c + 1) * P],
                             wout_sb[:, c * D:(c + 1) * D], start=(c == 0), stop=(c == 1))
                ins.then_inc(s["y_done"], 1)

            def gla_step(k, par):
                staged(state_outputs, k, par, -2)
                staged(project_low, k, par, 0)
                staged(project_vg, k, par, -1)
                staged(project_gate, k, par, 0)
                staged(intra_scores, k, par, -1)
                staged(transpose_kg, k, par, -1)
                staged(project_qk, k, par, 0)
                staged(transpose_o, k, par, -2)
                staged(transpose_x, k, par, 1)
                staged(key_values, k, par, -1)
                staged(intra_outputs, k, par, -1)
                staged(project_out, k, par, -2)

            pe.wait_ge(d["d_ident"], 16)
            iterate(pe, gla_step)

            def hidden_block(m, g, j):
                i = (m * NG + g) * NJ + j
                b = g * NJ + j
                if b > 3:
                    pe.wait_ge(s["hid_ready"], i - 1 if b > 5 else i - 3)
                for half in (1, 0):
                    at = m * 2 * HID + half * HID + j * P
                    ins = mm(bank[block_banks(b)[half]][0:ROWS[j], :], w1_sb[:, at:at + ROWS[j]],
                             z_t[:, g * FB:(g + 1) * FB])
                ins.then_inc(s["h1_done"], 1)

            def hidden_products(m, g, half):
                G = m * NG + g
                pe.wait_ge(s["hid_ready"], (G + 1) * NJ)
                if (g, half) == (0, 0):
                    pe.wait_ge(s["hid_ready"], (G + 1) * NJ + 1)
                elif product_bank(g, half) == product_bank(0, 0):
                    wait(pe, s["ffn_ready"], 2 * G + half)
                for i in (2 * half, 2 * half + 1):
                    o = bank[product_bank(g, half)][:, i * P:(i + 1) * P]
                    for j in range(NJ):
                        K = P if j < NJ - 1 else ROWS[j] + 1
                        at = ((G % 2) * NJ + j) * FB + i * P
                        ins = mm(o, hid[0:K, at:at + P], w2_sb[0:K, (m * NJ + j) * D:(m * NJ + j + 1) * D],
                                 start=(j == 0), stop=(j == NJ - 1))
                ins.then_inc(s["h2_done"], 1)

            def feed_forward(m, *first_tile):
                pe.wait_ge(s["z_ready"], NT * (m + 1))
                for g in range(NG):
                    for j in range(NJ):
                        if g == NG - 2 and j > 0 and first_tile:
                            first_tile[j - 1]()
                        if g > 0:
                            hidden_block(m, g, j)
                        if g > 0 and j > 0:
                            hidden_products(m, g - 1, j - 1)
                hidden_products(m, NG - 1, 0)
                hidden_products(m, NG - 1, 1)

            pe.wait_ge(d["d_qkv"], 32)
            pe.wait_ge(s["zero_pool"], 1)
            for l in range(DEPTH):
                base = NT * l
                b_m, b_q, b_k, b_v, b_t0, b_t1, b_s0, b_s1 = bank
                wl = wqkv_sb[:, l * QKV:(l + 1) * QKV]

                def free_bank(n, gla, ffn, left=0):
                    if isinstance(n, int) and n == 0:
                        for name in gla if l == 0 else ():
                            pe.wait_ge(s[name], NT)
                        if l:
                            a_layer = {"hid_ready": NG * NJ, "ffn_ready": 2 * NG}[ffn]
                            pe.wait_ge(s[ffn], a_layer * l - left)

                def transpose_in(n, par):
                    N = base + n
                    free_bank(n, ("xnt_ready", "low_ready", "kabs_ready", "gmin_ready"), "hid_ready", NG * NJ - 4)
                    wait(pe, s["slot_ready"], N + 1)
                    wait(pe, s["hs_ready"], N - 3)
                    wait(pe, s["z_ready"], N - 4)
                    wait(pe, s["mid_ready"], N - 3)
                    wait(pe, s["ht_ready"], N)
                    pe.transpose(b_m[:, 0:P], x_slot[:, par * P:(par + 1) * P], ident).then_inc(s["xtr_done"], 1)

                def project_qk(n, par):
                    N = base + n
                    a = h_t[:, par * (P + 1):par * (P + 1) + P]
                    wait(pe, s["ht_ready"], N + 1)
                    wait(pe, s["qn_ready"], N)
                    free_bank(n, ("qg_ready", "kd_ready", "kg_ready", "v_ready", "silu_ready"), "hid_ready",
                              NG * NJ - 3)
                    mm(b_q[:, :], a, wl[:, 0:INNER])
                    mm(b_k[:, :], a, wl[:, INNER:2 * INNER]).then_inc(s["qk_done"], 1)

                def project_v(n, par):
                    N = base + n
                    free_bank(n, ("atm_ready",), "ffn_ready")
                    wait(pe, s["ht_ready"], N + 1)
                    wait(pe, s["ot_ready"], N - 1)
                    wait(pe, s["vcur_ready"], N)
                    mm(b_v[:, :], h_t[:, par * (P + 1):par * (P + 1) + P], wl[:, 2 * INNER:3 * INNER]
                       ).then_inc(s["v_done"], 1)

                def transpose_q(n, par):
                    N = base + n
                    free_bank(n, ("s1_ready", "s2_ready"), "hid_ready")
                    wait(pe, s["qr_ready"], N + 1)
                    wait(pe, s["pt0_ready"], N - 1)
                    wait(pe, s["qbd0_ready"], N)
                    wait(pe, s["qbd1_ready"], N)
                    for c in range(PAIRS):
                        at = par * 2 * INNER + c * P
                        ins = pe.transpose(b_t0[:, c * P:(c + 1) * P], qr[:, at:at + P], ident)
                    ins.then_inc(s["qt_done"], 1)

                def transpose_k(n, par):
                    N = base + n
                    free_bank(n, ("og1_ready",), "hid_ready")
                    wait(pe, s["qr_ready"], N + 1)
                    wait(pe, s["pt1_ready"], N - 1)
                    wait(pe, s["kt_ready"], N)
                    for c in range(PAIRS):
                        at = par * 2 * INNER + INNER + c * P
                        ins = pe.transpose(b_t1[:, c * P:(c + 1) * P], qr[:, at:at + P], ident)
                    ins.then_inc(s["kt_done"], 1)

                def scores(n, par, w):
                    N = base + n
                    free_bank(n, (("ogt_ready",), ("yn_ready",))[w], "ffn_ready")
                    if l == 0 and isinstance(n, int) and n == 0:
                        pe.wait_ge(s["cast_consts"], 2)
                    b_s = (b_s0, b_s1)[w]
                    wait(pe, s["qbd0_ready"], N + 1)
                    wait(pe, s["qbd1_ready"], N + 1)
                    wait(pe, s["kt_ready"], N + 1)
                    wait(pe, s[f"p{w}_ready"], N)
                    first = isinstance(n, int) and n < B
                    m = (2 if first else 0) if w == 0 else 1
                    mask = masks_bf[:, m * P:(m + 1) * P].unsqueeze(1).to_broadcast([P, PAIRS, P])
                    mm(b_s[:, :].rearrange("p (c k) -> p c k", c=PAIRS), ident_bf[:, :], mask,
                       start=True, stop=False, skip=True)
                    for c in range(PAIRS):
                        kc = k_t[:, (par * PAIRS + c) * KC:(par * PAIRS + c + 1) * KC]
                        if w == 0:
                            kc = kc.rearrange("p (a k) -> p a k", k=W)[:, 0:3:2, :]
                        else:
                            kc = kc[:, 0:P]
                        at = ((par * PAIRS + c) * 2 + w) * P
                        o = b_s[:, c * P:(c + 1) * P]
                        if w == 0:
                            o = o.rearrange("p (a k) -> p a k", k=W)
                        ins = mm(o, q_bd[:, at:at + P], kc, start=False, stop=True, skip=True)
                    ins.then_inc(s[f"sc{w}_done"], 1)

                def transpose_probs(n, par, w):
                    N = base + n
                    wait(pe, s[f"pn{w}_ready"], N + 1)
                    b_t = (b_t0, b_t1)[w]
                    if w == 0:
                        wait(pe, s["qbd0_ready"], capped(N + 2, base + NT))
                        wait(pe, s["qbd1_ready"], capped(N + 2, base + NT))
                        wait(pe, s["pt0_ready"], N)
                    else:
                        wait(pe, s["kt_ready"], capped(N + 2, base + NT))
                        wait(pe, s["pt1_ready"], N)
                    for c in range(PAIRS):
                        at = ((par * 2 + w) * PAIRS + c) * P
                        ins = pe.transpose(b_t[:, c * P:(c + 1) * P], probs[:, at:at + P], ident)
                    ins.then_inc(s[f"pt{w}_done"], 1)

                def weigh_values(n, par, w):
                    N = base + n
                    wait(pe, s[f"pt{w}_ready"], N + 1)
                    if w == 0:
                        wait(pe, s["vup_ready"], N + 1)
                        wait(pe, s["vmix_ready"], N + 1)
                        wait(pe, s["vcur_ready"], capped(N + 2, base + NT))
                        wait(pe, s["ot_ready"], N)
                    else:
                        wait(pe, s["vcur_ready"], N + 1)
                    for h in range(AH):
                        c, h2 = h // 2, h % 2
                        at = (w * PAIRS + c) * P + h2 * W
                        ins = mm(b_v[h2 * DH:(h2 + 1) * DH, c * P + w * W:c * P + (w + 1) * W],
                                 (v_mix, v_cur)[w][:, par * INNER + h * DH:par * INNER + (h + 1) * DH],
                                 probs_t[:, at:at + W])
                    ins.then_inc(s[("pv0_done", "pv_done")[w]], 1)

                def project_o(n, par):
                    N = base + n
                    wait(pe, s["ot_ready"], N + 1)
                    wait(pe, s["ht_ready"], capped(N + 4, base + NT))
                    wait(pe, s["hs_ready"], N)
                    wait(pe, s["z_ready"], N - 1)
                    wait(pe, s["mid_ready"], N)
                    for c in range(PAIRS):
                        at = (par * PAIRS + c) * P
                        ins = mm(b_m[:, P:2 * P], o_t[:, at:at + P],
                                 wo_sb[:, (l * PAIRS + c) * D:(l * PAIRS + c + 1) * D],
                                 start=(c == 0), stop=(c == PAIRS - 1))
                    ins.then_inc(s["wo_done"], 1)

                def shift_rows(n, par):
                    N = base + n
                    wait(pe, s["mid_ready"], N + 1)
                    wait(pe, s["z_ready"], N)
                    wait(pe, s["mid_ready"], N + 1)
                    wait(pe, s["ht_ready"], capped(N + 4, base + NT))
                    wait(pe, s["hs_ready"], N)
                    o = b_m[:, 2 * P:2 * P + D // 2]
                    mm(o, shift, middle[:, bass.ds((n + 2) * D + D // 2, D // 2)], stop=False)
                    mm(o, carry, middle[:, bass.ds(n * D + D // 2, D // 2)], start=False
                       ).then_inc(s["hs_done"], 1)

                def transpose_z(n, par):
                    N = base + n
                    wait(pe, s["zn_ready"], N + 1)
                    wait(pe, s["mid_ready"], capped(N + 2, base + NT))
                    wait(pe, s["ht_ready"], capped(N + 5, base + NT))
                    wait(pe, s["hs_ready"], N + 1)
                    wait(pe, s["z_ready"], N)
                    pe.transpose(b_m[:, 3 * P:4 * P], zn[:, par * P:(par + 1) * P], ident).then_inc(s["zt_done"], 1)

                def attn_step(k, par):
                    staged(transpose_probs, k, par, -1, 1)
                    staged(scores, k, par, 0, 0)
                    staged(transpose_in, k, par, 2)
                    staged(weigh_values, k, par, -1, 0)
                    staged(weigh_values, k, par, -1, 1)
                    staged(project_qk, k, par, 2)
                    staged(project_o, k, par, -1)
                    staged(transpose_q, k, par, 1)
                    staged(transpose_k, k, par, 1)
                    staged(project_v, k, par, 1)
                    staged(transpose_z, k, par, -2)
                    staged(scores, k, par, 1, 1)
                    staged(shift_rows, k, par, -1)
                    staged(transpose_probs, k, par, 0, 0)
                def early_block_0():
                    if l == 0:
                        pe.wait_ge(d["d_ffn"], 16 * 7)
                    pe.wait_ge(s["z_ready"], base + GROUP)
                    pe.wait_ge(s["qn_ready"], base + NT)
                    pe.wait_ge(s["p0_ready"], base + NT)
                    pe.wait_ge(s["p1_ready"], base + NT)
                    hidden_block(l, 0, 0)

                def early_block_1():
                    pe.wait_ge(s["pt0_ready"], base + NT)
                    pe.wait_ge(s["pt1_ready"], base + NT)
                    hidden_block(l, 0, 1)
                    hidden_block(l, 0, 2)

                if l:
                    feed_forward(l - 1, lambda: transpose_in(0, 0), lambda: project_qk(0, 0))
                else:
                    transpose_in(0, 0)
                    project_qk(0, 0)
                iterate(pe, attn_step, first=-1, before={NT: early_block_0, NT + 1: early_block_1})
            feed_forward(DEPTH - 1)

        @block.scalar
        def _(act):
            act.preload_act_table_set("natural_log_exp_and_others")

            b_xg, b_qk, b_vg, b_at, b_kv, b_o, b_og, b_y = bank

            def ln_of_x(n, par):
                wait(act, s["x_aggr"], n + 1)
                act.activation(ln_x[:, par:par + 1], mv_x[:, 2 * par + 1:2 * par + 2], ACT.Ln, bias=eps_col
                               ).then_inc(s["x_ln"], 1)

            def rstd_of_x(n, par):
                wait(act, s["x_ln"], n + 1)
                wait(act, s["xn_ready"], n - 1)
                act.activation(rstd_x[:, par:par + 1], ln_x[:, par:par + 1], ACT.Exp, scale=-0.5
                               ).then_inc(s["x_rstd"], 1)

            def copy_xn_t(n, par):
                wait(act, s["xt_done"], n + 1)
                wait(act, s["lowp_done"], n - 1)
                wait(act, s["vg_done"], n - 1)
                wait(act, s["proj_done"], n - 1)
                act.activation(xn_t[:, par * P:(par + 1) * P], b_xg[:, 0:P], ACT.Copy).then_inc(s["xnt_ready"], 1)

            def copy_v(n, par):
                wait(act, s["vg_done"], n + 1)
                wait(act, s["go_done"], n - 1)
                act.activation(v_sb[:, par * GV:(par + 1) * GV], b_vg[:, 0:GV], ACT.Copy).then_inc(s["v_ready"], 1)

            def gate_abs(n, par):
                wait(act, s["vg_done"], n + 1)
                wait(act, s["glog_ready"], n)
                act.activation(g_soft[:, :], b_vg[:, GV:2 * GV], ACT.Abs).then_inc(s["gabs_ready"], 1)

            def gate_exp(n, par):
                wait(act, s["gabs_ready"], n + 1)
                act.activation(g_soft[:, :], g_soft[:, :], ACT.Exp, scale=-1.0).then_inc(s["gexp_ready"], 1)

            def gate_ln(n, par):
                wait(act, s["gexp_ready"], n + 1)
                act.activation(g_soft[:, :], g_soft[:, :], ACT.Ln, bias=1.0).then_inc(s["gsoft_ready"], 1)

            def gate_sigmoid(n, par):
                wait(act, s["glog_ready"], n + 1)
                act.activation(g_sig[:, :], g_sig[:, :], ACT.Exp).then_inc(s["gsig_ready"], 1)

            def copy_low(n, par):
                wait(act, s["lowp_done"], n + 1)
                wait(act, s["gk_done"], n)
                act.activation(low[0:RANK, :], b_xg[0:RANK, 2 * P:3 * P], ACT.Copy).then_inc(s["low_ready"], 1)

            def decay_abs(n, par):
                if isinstance(n, int) and n == 0:
                    act.wait_ge(d["d_gcols"], 3 * 16)
                wait(act, s["gk_done"], n + 1)
                wait(act, s["logsig_ready"], n)
                act.activation(gk_soft[:, :], b_xg[:, P:2 * P], ACT.Abs, bias=bgk2_col
                               ).then_inc(s["kabs_ready"], 1)

            def decay_exp(n, par):
                wait(act, s["kabs_ready"], n + 1)
                act.activation(gk_soft[:, :], gk_soft[:, :], ACT.Exp, scale=-1.0).then_inc(s["kexp_ready"], 1)

            def decay_ln(n, par):
                wait(act, s["kexp_ready"], n + 1)
                act.activation(gk_soft[:, :], gk_soft[:, :], ACT.Ln, bias=1.0).then_inc(s["ksoft_ready"], 1)

            def decay_of_q(n, par):
                wait(act, s["cum_ready"], n + 1)
                wait(act, s["qg_ready"], n)
                act.activation(dec_q[:, :], cum[:, :], ACT.Exp, scale=GATE).then_inc(s["decq_ready"], 1)

            def decay_of_k(n, par):
                wait(act, s["cum_ready"], n + 1)
                wait(act, s["kd_ready"], n)
                act.activation(dec_k[:, :], cum[:, :], ACT.Exp, scale=-GATE).then_inc(s["deck_ready"], 1)

            def decay_to_end(n, par):
                wait(act, s["last_ready"], n + 1)
                wait(act, s["kg_ready"], n)
                wait(act, s["s2_ready"], n - 1)
                for c in range(2):
                    act.activation(dec_g[:, c * CH:(c + 1) * CH], cum[:, c * CH:(c + 1) * CH], ACT.Exp,
                                   scale=-GATE, bias=last16[:, c:c + 1])
                act.activation(dlast[:, 2 * par:2 * par + 2], last16[:, :], ACT.Exp).then_inc(s["decg_ready"], 1)

            def copy_kg(n, par):
                if isinstance(n, int) and n == 0:
                    act.wait_ge(s["zero_gla"], 1)
                wait(act, s["kgt_done"], n + 1)
                wait(act, s["kv_done"], n - 1)
                for c in range(2):
                    at = (par * 2 + c) * P
                    ins = act.activation(kg_tok[c * CH:(c + 1) * CH, at:at + P], b_kv[c * CH:(c + 1) * CH, 0:P], ACT.Copy)
                ins.then_inc(s["kgtok_ready"], 1)

            def square_o(n, par):
                wait(act, s["go_done"], n + 1)
                wait(act, s["oss_ready"], n)
                act.activation(o_sq[:, :], b_o[:, 0:GV], ACT.Square).then_inc(s["osq_ready"], 1)

            def ln_of_o(n, par):
                wait(act, s["oss_ready"], n + 1)
                act.activation(o_ln[:, :], o_ss[:, :], ACT.Ln, bias=eps_col, scale=1.0 / GDV
                               ).then_inc(s["oln_ready"], 1)

            def rstd_of_o(n, par):
                wait(act, s["oln_ready"], n + 1)
                wait(act, s["og1_ready"], n)
                act.activation(o_r[:, :], o_ln[:, :], ACT.Exp, scale=-0.5).then_inc(s["or_ready"], 1)

            def scale_o_t(n, par):
                wait(act, s["ogt_done"], n + 1)
                wait(act, s["y_done"], n - 1)
                act.activation(og_t[:, par * 2 * P:(par + 1) * 2 * P], b_og[:, 0:2 * P], ACT.Copy, scale=rms_col
                               ).then_inc(s["ogt_ready"], 1)

            def ln_of_y(n, par):
                wait(act, s["y_aggr"], n + 1)
                act.activation(ln_y[:, :], mv_y[:, 1:2], ACT.Ln, bias=eps_col).then_inc(s["y_ln"], 1)

            def rstd_of_y(n, par):
                wait(act, s["y_ln"], n + 1)
                wait(act, s["yn_ready"], n)
                act.activation(rstd_y[:, :], ln_y[:, :], ACT.Exp, scale=-0.5).then_inc(s["y_rstd"], 1)

            def ln_of_f(n, par):
                wait(act, s["f_aggr"], n + 1)
                act.activation(ln_f[:, :], mv_f[:, 1:2], ACT.Ln, bias=eps_col).then_inc(s["f_ln"], 1)

            def rstd_of_f(n, par):
                wait(act, s["f_ln"], n + 1)
                wait(act, s["xf_ready"], n)
                act.activation(rstd_f[:, :], ln_f[:, :], ACT.Exp, scale=-0.5).then_inc(s["f_rstd"], 1)

            def gla_step(k, par):
                staged(copy_low, k, par, 1)
                staged(decay_to_end, k, par, 0)
                staged(ln_of_y, k, par, -2)
                staged(ln_of_o, k, par, -1)
                staged(ln_of_x, k, par, 2)
                staged(rstd_of_o, k, par, -1)
                staged(rstd_of_y, k, par, -2)
                staged(rstd_of_x, k, par, 2)
                staged(decay_abs, k, par, 1)
                staged(copy_v, k, par, 0)
                staged(decay_exp, k, par, 1)
                staged(gate_abs, k, par, 0)
                staged(decay_ln, k, par, 1)
                staged(copy_kg, k, par, 0)
                staged(gate_exp, k, par, 0)
                staged(scale_o_t, k, par, -1)
                staged(gate_ln, k, par, 0)
                staged(ln_of_f, k, par, -2)
                staged(copy_xn_t, k, par, 2)
                staged(rstd_of_f, k, par, -2)
                staged(decay_of_k, k, par, 1)
                staged(decay_of_q, k, par, 1)
                staged(gate_sigmoid, k, par, 0)
                staged(square_o, k, par, 0)

            act.wait_ge(s["col_consts"], 2)
            iterate(act, gla_step, end=NT + 1)

            def feed_forward(m, *first_tile):
                for g in range(NG):
                    for j in range(NJ):
                        if first_tile and g == NG - 2:
                            first_tile[j]()
                        i = (m * NG + g) * NJ + j
                        act.wait_ge(s["h1_done"], i + 1)
                        wait(act, s["hid_ready"], i - 1)
                        act.activation(gelu[0:ROWS[j], (i % 2) * FB:(i % 2 + 1) * FB],
                                       bank[block_banks(g * NJ + j)[1]][0:ROWS[j], :], ACT.Gelu, bias=b1_col(m, 1, j)
                                       ).then_inc(s["gelu_ready"], 1)
                act.preload_act_table_set("natural_log_exp_and_others")

            act.wait_ge(s["zero_pool"], 1)
            act.wait_ge(d["d_cols"], 10 * 16)
            for l in range(DEPTH):
                base = NT * l
                b_m, b_q, b_k, b_v, b_t0, b_t1, b_s0, b_s1 = bank

                def copy_in(n, par):
                    N = base + n
                    if l == 0:
                        wait(act, s["xf_ready"], n + 1)
                    elif isinstance(n, int) and n in (0, GROUP):
                        act.wait_ge(s["ffn_ready"], 2 * (NG * l if n else NG * (l - 1) + 1))
                    wait(act, s["xtr_done"], N - 1)
                    act.activation(x_slot[:, par * P:(par + 1) * P], tile_of(stream[l], n), ACT.Copy
                                   ).then_inc(s["slot_ready"], 1)

                def carry_column(n, par):
                    N = base + n
                    o = h_t[:, par * (P + 1):(par + 1) * (P + 1)]
                    wait(act, s["v_done"], N - 1)
                    wait(act, s["qk_done"], N - 1)
                    if l and isinstance(n, int) and n == 0:
                        act.wait_ge(s["carry_zero"], l)
                    act.activation(o[D // 2:P, 0:1], o[D // 2:P, P:P + 1], ACT.Copy).then_inc(s["carried"], 1)

                def copy_h_t(n, par):
                    N = base + n
                    o = h_t[:, par * (P + 1):(par + 1) * (P + 1)]
                    wait(act, s["xtr_done"], N + 1)
                    wait(act, s["carried"], N + 1)
                    act.activation(o[0:D // 2, 0:P], b_m[0:D // 2, 0:P], ACT.Copy)
                    act.activation(o[D // 2:P, 1:P + 1], b_m[D // 2:P, 0:P], ACT.Copy).then_inc(s["ht_ready"], 1)

                def squares(n, par):
                    N = base + n
                    wait(act, s["qk_done"], N + 1)
                    wait(act, s["ss_ready"], N)
                    act.activation(sq[:, 0:INNER], b_q[:, :], ACT.Square)
                    act.activation(sq[:, INNER:2 * INNER], b_k[:, :], ACT.Square).then_inc(s["sq_ready"], 1)

                def ln_of_squares(n, par):
                    N = base + n
                    wait(act, s["ssc_ready"], N + 1)
                    act.activation(ss_ln[:, :], ssc[:, :], ACT.Ln, scale=float(2 ** 30)).then_inc(s["ssl_ready"], 1)

                def inverse_norms(n, par):
                    N = base + n
                    wait(act, s["ssl_ready"], N + 1)
                    wait(act, s["qn_ready"], N)
                    act.activation(inv[:, :], ss_ln[:, :], ACT.Exp, scale=-0.5, bias=norm_bias_col
                                   ).then_inc(s["inv_ready"], 1)

                def copy_q_bd(n, par):
                    N = base + n
                    wait(act, s["qt_done"], N + 1)
                    wait(act, s["sc0_done"], N - 1)
                    wait(act, s["sc1_done"], N - 1)
                    dst, src = q_blocks(par, b_t0, 1)
                    act.activation(dst, src, ACT.Copy).then_inc(s["qbd1_ready"], 1)

                def copy_k_t(n, par):
                    N = base + n
                    wait(act, s["kt_done"], N + 1)
                    wait(act, s["kprev_ready"], N + 1)
                    kv = k_t[:, par * PAIRS * KC:(par + 1) * PAIRS * KC].rearrange("p (c k) -> p c k", k=KC)
                    act.activation(kv[:, :, 0:P], b_t1[:, :].rearrange("p (c k) -> p c k", k=P), ACT.Copy
                                   ).then_inc(s["kt_ready"], 1)

                def exponentials(n, par, w):
                    N = base + n
                    wait(act, s[f"max{w}_ready"], N + 1)
                    wait(act, s[f"pt{w}_done"], N - 1)
                    b_s = (b_s0, b_s1)[w]
                    for c in range(PAIRS):
                        at = ((par * 2 + w) * PAIRS + c) * P
                        r = (par * 2 + w) * PAIRS + c
                        ins = act.activation(probs[:, at:at + P], b_s[:, c * P:(c + 1) * P], ACT.Exp,
                                             bias=neg_max[:, w * PAIRS + c:w * PAIRS + c + 1],
                                             accum_out=row_sum[:, r:r + 1])
                    ins.then_inc(s[f"p{w}_ready"], 1)

                def copy_probs_t(n, par):
                    N = base + n
                    wait(act, s["pt0_done"], N + 1)
                    wait(act, s["pv0_done"], N)
                    act.activation(probs_t[:, 0:PAIRS * P], b_t0[:, :], ACT.Copy).then_inc(s["pt0_ready"], 1)

                def copy_o_t(n, par):
                    N = base + n
                    wait(act, s["pv_done"], N + 1)
                    wait(act, s["wo_done"], N - 1)
                    act.activation(o_t[:, par * PAIRS * P:(par + 1) * PAIRS * P], b_v[:, :], ACT.Copy
                                   ).then_inc(s["ot_ready"], 1)

                def copy_v_cur(n, par):
                    N = base + n
                    wait(act, s["v_done"], N + 1)
                    wait(act, s["vup_ready"], N + 1)
                    wait(act, s["vmix_ready"], N - 1)
                    wait(act, s["pv_done"], N - 1)
                    act.activation(v_cur[:, par * INNER:(par + 1) * INNER], b_v[:, :], ACT.Copy
                                   ).then_inc(s["vcur_ready"], 1)

                def copy_unshifted(n, par):
                    N = base + n
                    wait(act, s["mid_ready"], N + 1)
                    wait(act, s["zn_ready"], N - 1)
                    act.activation(hcat[:, par * P:par * P + D // 2],
                                   middle[:, bass.ds((n + 2) * D, D // 2)], ACT.Copy).then_inc(s["half_ready"], 1)

                def copy_shifted(n, par):
                    N = base + n
                    wait(act, s["hs_done"], N + 1)
                    wait(act, s["half_ready"], N + 1)
                    wait(act, s["zn_ready"], N - 1)
                    act.activation(hcat[:, par * P + D // 2:(par + 1) * P], b_m[:, 2 * P:2 * P + D // 2], ACT.Copy
                                   ).then_inc(s["hs_ready"], 1)

                def ln_of_z(n, par):
                    N = base + n
                    wait(act, s["z_aggr"], N + 1)
                    act.activation(ln_z[:, :], mv_z[:, 1:2], ACT.Ln, bias=eps_col).then_inc(s["z_ln"], 1)

                def rstd_of_z(n, par):
                    N = base + n
                    wait(act, s["z_ln"], N + 1)
                    wait(act, s["zn_ready"], N)
                    act.activation(rstd_z[:, :], ln_z[:, :], ACT.Exp, scale=-0.5).then_inc(s["z_rstd"], 1)

                def copy_z_t(n, par):
                    N = base + n
                    wait(act, s["zt_done"], N + 1)
                    act.activation(z_t[:, bass.ds(n * P, P)], b_m[:, 3 * P:4 * P], ACT.Identity,
                                   bias=lnb_col[l], scale=lng_col[l]).then_inc(s["z_ready"], 1)

                def attn_step(k, par):
                    if not (isinstance(k, int) and k == -1):
                        staged(inverse_norms, k, par, 1)
                    staged(copy_shifted, k, par, -2)
                    staged(carry_column, k, par, 2)
                    staged(copy_probs_t, k, par, -1)
                    staged(copy_in, k, par, 2)
                    staged(exponentials, k, par, 0, 1)
                    staged(copy_h_t, k, par, 2)
                    staged(ln_of_z, k, par, -2)
                    staged(rstd_of_z, k, par, -2)
                    staged(copy_o_t, k, par, -1)
                    staged(exponentials, k, par, 0, 0)
                    staged(squares, k, par, 2)
                    staged(copy_q_bd, k, par, 1)
                    staged(copy_k_t, k, par, 1)
                    staged(copy_z_t, k, par, -2)
                    staged(copy_v_cur, k, par, 1)
                    staged(ln_of_squares, k, par, 2)
                    staged(copy_unshifted, k, par, -1)
                if l:
                    def copy_input():
                        copy_in(0, 0)
                        carry_column(0, 0)
                    feed_forward(l - 1, copy_input, lambda: copy_h_t(0, 0), lambda: squares(0, 0))
                    ln_of_squares(0, 0)
                    inverse_norms(0, 0)
                else:
                    for stage, n in ((copy_in, 0), (carry_column, 0), (copy_h_t, 0), (ln_of_y, LAST), (rstd_of_y, LAST),
                                     (ln_of_f, LAST), (rstd_of_f, LAST), (squares, 0), (ln_of_squares, 0),
                                     (inverse_norms, 0)):
                        stage(n, n % 2)
                iterate(act, attn_step, first=-1)
            feed_forward(DEPTH - 1)

            bounds = [0] + list(range(NT - GROUP, NT + 1, 2))
            for i, (n0, n1) in enumerate(zip(bounds, bounds[1:])):
                act.wait_ge(s["mvo_ready"], n1)
                act.activation(ln_o[:, n0:n1], mv_o[:, 2 * n0 + 1:2 * n1:2], ACT.Ln, bias=eps_col
                               ).then_inc(s["lno_ready"], 1)
                act.wait_ge(s["lno_ready"], i + 1)
                act.activation(rstd_o[:, n0:n1], ln_o[:, n0:n1], ACT.Exp, scale=-0.5).then_inc(s["rstdo_ready"], 1)
                if i == 0:
                    act.wait_ge(s["shifto_ready"], 1)
                    for n in range(ON_ACT, NT - GROUP):
                        act.activation(tile_of(xo, n), tile_of(stream[DEPTH], n), ACT.Identity,
                                       bias=shift_o[:, n:n + 1], scale=rstd_o[:, n:n + 1]
                                       ).then_inc(s["xo_act_ready"], 1)

        @block.vector
        def _(dve):
            dve.memset(eps_col, EPS).then_inc(s["col_consts"], 1)
            dve.memset(norm_bias_col, 15 * LN2).then_inc(s["col_consts"], 1)
            for buf in (qg, state):
                ins = dve.memset(buf[:, :], 0.0)
            ins.then_inc(s["zero_dve"], 1)
            dve.wait_ge(s["zero_dve"], 1)
            b_xg, b_qk, b_vg, b_at, b_kv, b_o, b_og, b_y = bank

            def stats_x(n, par):
                if isinstance(n, int) and n == 0:
                    dve.wait_ge(d["d_x0"], 16)
                if isinstance(n, int) and n == B:
                    dve.wait_ge(d["d_x1"], 16 * B)
                dve.bn_stats(st_x[:, 6 * par:6 * par + 6], tile_of(x_in, n)).then_inc(s["x_stats"], 1)

            def aggregate_x(n, par):
                wait_apart(dve, (s["x_stats"], n + 1), (s["xn_ready"], n - 1))
                dve.bn_aggr(mv_x[:, 2 * par:2 * par + 2], st_x[:, 6 * par:6 * par + 6]).then_inc(s["x_aggr"], 1)

            def normalise_x(n, par):
                wait(dve, s["x_rstd"], n + 1)
                wait(dve, s["xt_done"], n - 1)
                dve.tensor_scalar(xn[:, par * P:(par + 1) * P], tile_of(x_in, n), mv_x[:, 2 * par:2 * par + 1],
                                  rstd_x[:, par:par + 1], ALU.subtract, ALU.mult).then_inc(s["xn_ready"], 1)

            def gate_log(n, par):
                wait(dve, s["gsoft_ready"], n + 1)
                wait(dve, s["v_ready"], n + 1)
                wait(dve, s["silu_ready"], n)
                dve.scalar_tensor_tensor(out=g_sig[:, :], in0=b_vg[:, GV:2 * GV], scalar=0.0, in1=g_soft[:, :],
                                         op0=ALU.min, op1=ALU.subtract).then_inc(s["glog_ready"], 1)

            def gate_silu(n, par):
                wait(dve, s["gsig_ready"], n + 1)
                wait(dve, s["og2_ready"], n - 1)
                dve.tensor_tensor(silu[:, par * GV:(par + 1) * GV], b_vg[:, GV:2 * GV], g_sig[:, :], ALU.mult
                                  ).then_inc(s["silu_ready"], 1)

            def decay_min(n, par):
                if isinstance(n, int) and n == 0:
                    dve.wait_ge(d["d_gcols"], 3 * 16)
                wait(dve, s["gk_done"], n + 1)
                wait(dve, s["kabs_ready"], n + 1)
                wait(dve, s["logsig_ready"], n)
                dve.tensor_scalar(gk_min[:, :], b_xg[:, P:2 * P], bgk2_col, 0.0, ALU.add, ALU.min
                                  ).then_inc(s["gmin_ready"], 1)

            def decay_log(n, par):
                wait(dve, s["gmin_ready"], n + 1)
                wait(dve, s["ksoft_ready"], n + 1)
                wait(dve, s["cum_ready"], n)
                dve.tensor_tensor(logsig[:, :], gk_min[:, :], gk_soft[:, :], ALU.subtract
                                  ).then_inc(s["logsig_ready"], 1)

            def decay_cumulate(n, par):
                if isinstance(n, int) and n == 0:
                    dve.wait_ge(d["d_const"], 16)
                wait(dve, s["logsig_ready"], n + 1)
                for read in ("decq_ready", "deck_ready", "decg_ready"):
                    wait(dve, s[read], n)
                dve.tensor_tensor_scan(cum[:, :], keep, logsig[:, :], 0.0, ALU.mult, ALU.add
                                       ).then_inc(s["cum_ready"], 1)

            def decay_last(n, par):
                wait(dve, s["cum_ready"], n + 1)
                wait(dve, s["decg_ready"], n)
                dve.tensor_scalar(last16[:, :], cum[:, CH - 1:P:CH], GATE, None, ALU.mult).then_inc(s["last_ready"], 1)

            def decay_q(n, par):
                wait(dve, s["decq_ready"], n + 1)
                wait(dve, s["proj_done"], n + 1)
                wait(dve, s["at_done"], n - 1)
                wait(dve, s["go_done"], n - 1)
                for h in range(GH):
                    r = slice(h * GDK, (h + 1) * GDK)
                    ins = dve.scalar_tensor_tensor(out=qg[r, (par * GH + h) * P:(par * GH + h + 1) * P],
                                                   in0=b_qk[r, 0:P], scalar=float(GDK) ** -0.5, in1=dec_q[r, :],
                                                   op0=ALU.mult, op1=ALU.mult)
                ins.then_inc(s["qg_ready"], 1)

            def decay_k(n, par):
                wait(dve, s["deck_ready"], n + 1)
                wait(dve, s["proj_done"], n + 1)
                wait(dve, s["at_done"], n - 1)
                dve.tensor_tensor(kd[:, par * P:(par + 1) * P], b_qk[:, P:2 * P], dec_k[:, :], ALU.mult
                                  ).then_inc(s["kd_ready"], 1)

            def decay_kg(n, par):
                wait(dve, s["decg_ready"], n + 1)
                wait(dve, s["proj_done"], n + 1)
                wait(dve, s["kgt_done"], n)
                dve.tensor_tensor(kg[:, :], b_qk[:, P:2 * P], dec_g[:, :], ALU.mult).then_inc(s["kg_ready"], 1)

            def mask_scores(n, par):
                if isinstance(n, int) and n == 0:
                    dve.wait_ge(s["zero_gla"], 1)
                wait_apart(dve, (s["at_done"], n + 1), (s["intra_done"], n - 1))
                dve.copy_predicated(a_t[:, par * GH * P:(par + 1) * GH * P].rearrange("p (h t) -> p h t", h=GH),
                                    causal_bits.unsqueeze(1).to_broadcast([P, GH, P]),
                                    b_at[:, :].rearrange("p (h t) -> p h t", h=GH)).then_inc(s["atm_ready"], 1)

            def state_1(n, par):
                wait(dve, s["kv_done"], n + 1)
                wait(dve, s["decg_ready"], n + 1)
                wait(dve, s["s2_ready"], n - 1)
                wait(dve, s["go_done"], n - 1)
                st = state[:, par * 2 * GDV:(par + 1) * 2 * GDV]
                dve.scalar_tensor_tensor(out=st[:, GDV:2 * GDV], in0=st[:, 0:GDV], scalar=dlast[:, 2 * par:2 * par + 1],
                                         in1=b_kv[:, P:P + GDV], op0=ALU.mult, op1=ALU.add).then_inc(s["s1_ready"], 1)

            def state_2(n, par):
                wait(dve, s["go_done"], n + 1)
                wait(dve, s["s1_ready"], n + 1)
                st = state[:, par * 2 * GDV:(par + 1) * 2 * GDV]
                dve.scalar_tensor_tensor(out=st[:, 0:GDV], in0=st[:, GDV:2 * GDV],
                                         scalar=dlast[:, 2 * par + 1:2 * par + 2],
                                         in1=b_kv[:, P + GDV:P + 2 * GDV], op0=ALU.mult, op1=ALU.add
                                         ).then_inc(s["s2_ready"], 1)

            def sum_o(n, par):
                wait(dve, s["osq_ready"], n + 1)
                wait(dve, s["oln_ready"], n)
                dve.tensor_reduce(o_ss[:, :], o_sq[:, :].rearrange("p (h v) -> p h v", h=GH), AX.X, ALU.add
                                  ).then_inc(s["oss_ready"], 1)

            def scale_o(n, par):
                wait(dve, s["or_ready"], n + 1)
                wait(dve, s["og2_ready"], n)
                dve.tensor_tensor(og1[:, :].rearrange("p (h v) -> p h v", h=GH),
                                  b_o[:, 0:GV].rearrange("p (h v) -> p h v", h=GH),
                                  o_r[:, :].unsqueeze(2).to_broadcast([P, GH, GDV]), ALU.mult).then_inc(s["og1_ready"], 1)

            def stats_y(n, par):
                wait_apart(dve, (s["y_done"], n + 1), (s["y_aggr"], n))
                dve.bn_stats(st_y[:, :], b_y[:, 0:D]).then_inc(s["y_stats"], 1)

            def aggregate_y(n, par):
                wait_apart(dve, (s["y_stats"], n + 1), (s["yn_ready"], n))
                dve.bn_aggr(mv_y[:, :], st_y[:, :]).then_inc(s["y_aggr"], 1)

            def normalise_y(n, par):
                wait(dve, s["y_rstd"], n + 1)
                wait(dve, s["x1_ready"], n)
                dve.tensor_scalar(yn[:, :], b_y[:, 0:D], mv_y[:, 0:1], rstd_y[:, :], ALU.subtract, ALU.mult
                                  ).then_inc(s["yn_ready"], 1)

            def stats_f(n, par):
                wait_apart(dve, (s["x1_ready"], n + 1), (s["f_aggr"], n))
                dve.bn_stats(st_f[:, :], tile_of(x_attn, n)).then_inc(s["f_stats"], 1)

            def aggregate_f(n, par):
                wait_apart(dve, (s["f_stats"], n + 1), (s["xf_ready"], n))
                dve.bn_aggr(mv_f[:, :], st_f[:, :]).then_inc(s["f_aggr"], 1)

            def normalise_f(n, par):
                wait(dve, s["f_rstd"], n + 1)
                dve.tensor_scalar(tile_of(stream[0], n), tile_of(x_attn, n), mv_f[:, 0:1], rstd_f[:, :],
                                  ALU.subtract, ALU.mult).then_inc(s["xf_ready"], 1)

            def gla_step(k, par):
                staged(stats_y, k, par, -2)
                staged(stats_x, k, par, 2)
                staged(decay_k, k, par, 0)
                staged(aggregate_x, k, par, 2)
                staged(gate_silu, k, par, -1)
                staged(aggregate_y, k, par, -2)
                staged(sum_o, k, par, -1)
                staged(decay_q, k, par, 0)
                staged(decay_kg, k, par, 0)
                staged(scale_o, k, par, -1)
                staged(state_2, k, par, -1)
                staged(normalise_x, k, par, 2)
                staged(normalise_y, k, par, -2)
                staged(decay_min, k, par, 1)
                staged(mask_scores, k, par, 0)
                staged(stats_f, k, par, -2)
                staged(decay_log, k, par, 1)
                staged(aggregate_f, k, par, -2)
                staged(state_1, k, par, 0)
                staged(decay_cumulate, k, par, 1)
                staged(gate_log, k, par, 0)
                staged(decay_last, k, par, 1)
                staged(normalise_f, k, par, -2)

            iterate(dve, gla_step, end=NT + 1)

            def add_ffn(m, g, half):
                G = m * NG + g
                n0 = g * GROUP + 2 * half
                dve.wait_ge(s["h2_done"], 2 * G + half + 1)
                dve.tensor_tensor(stream[m + 1][:, n0 * D:(n0 + 2) * D],
                                  bank[product_bank(g, half)][:, half * 2 * D:(half + 1) * 2 * D],
                                  middle[:, (n0 + 2) * D:(n0 + 4) * D], ALU.add).then_inc(s["ffn_ready"], 1)
                if m == DEPTH - 1:
                    dve.wait_ge(s["ffn_ready"], 2 * G + half + 1)
                    for n in (n0, n0 + 1):
                        dve.bn_stats(st_o[:, 6 * n:6 * n + 6], tile_of(stream[m + 1], n)).then_inc(s["sto_ready"], 1)
                    for n in (n0, n0 + 1):
                        dve.wait_ge(s["sto_ready"], n + 1)
                        dve.bn_aggr(mv_o[:, 2 * n:2 * n + 2], st_o[:, 6 * n:6 * n + 6]).then_inc(s["mvo_ready"], 1)

            def normalise_out(n):
                dve.wait_ge(s["rstdo_ready"], 1 if n < NT - GROUP else 2 + (n - (NT - GROUP)) // 2)
                for m in (n, n + 1):
                    ins = dve.tensor_scalar(tile_of(xo, m), tile_of(stream[DEPTH], m), mv_o[:, 2 * m:2 * m + 1],
                                            rstd_o[:, m:m + 1], ALU.subtract, ALU.mult)
                ins.then_inc(s["xo_ready"], 1)

            def feed_forward(m, *first_tile):
                for g in range(NG):
                    for j in range(NJ):
                        i = (m * NG + g) * NJ + j
                        dve.wait_ge(s["gelu_ready"], i + 1)
                        if g < 2 and j == 0:
                            dve.wait_ge(s["ones_ready"], m + 1)
                        if j == 0:
                            wait(dve, s["h2_done"], 2 * (m * NG + g - 1))
                        at = (((m * NG + g) % 2) * NJ + j) * FB
                        dve.scalar_tensor_tensor(out=hid[0:ROWS[j], at:at + FB],
                                                 in0=bank[block_banks(g * NJ + j)[0]][0:ROWS[j], :], scalar=b1_col(m, 0, j),
                                                 in1=gelu[0:ROWS[j], (i % 2) * FB:(i % 2 + 1) * FB],
                                                 op0=ALU.add, op1=ALU.mult).then_inc(s["hid_ready"], 1)
                        if g and j > 0:
                            add_ffn(m, g - 1, j - 1)
                    if first_tile and g == NG - 2:
                        for stage in first_tile[0]:
                            stage(0, 0)
                if m == DEPTH - 1:
                    dve.wait_ge(s["rstdo_ready"], 1)
                    dve.scalar_tensor_tensor(out=shift_o[:, 0:NT - GROUP], in0=mv_o[:, 0:2 * (NT - GROUP):2], scalar=-1.0,
                                             in1=rstd_o[:, 0:NT - GROUP], op0=ALU.mult, op1=ALU.mult
                                             ).then_inc(s["shifto_ready"], 1)
                    for n in range(0, ON_ACT, 2):
                        normalise_out(n)
                for half in range(2):
                    for stage in first_tile[half + 1:half + 2]:
                        for fn in stage:
                            fn(0, 0)
                    add_ffn(m, NG - 1, half)

            dve.wait_ge(d["d_cols"], 10 * 16)
            dve.wait_ge(d["d_masks"], 16)
            dve.tensor_copy(ident_bf[:, :], ident).then_inc(s["cast_consts"], 1)
            dve.tensor_copy(masks_bf[:, :], consts[:, 5 * P:8 * P]).then_inc(s["cast_consts"], 1)
            dve.wait_ge(s["zero_pool"], 1)
            for l in range(DEPTH):
                base = NT * l
                b_m, b_q, b_k, b_v, b_t0, b_t1, b_s0, b_s1 = bank

                def sum_squares(n, par):
                    N = base + n
                    wait(dve, s["sq_ready"], N + 1)
                    wait(dve, s["ssc_ready"], N)
                    dve.tensor_reduce(ss[:, :], sq[:, :].rearrange("p (h e) -> p h e", e=DH), AX.X, ALU.add
                                      ).then_inc(s["ss_ready"], 1)

                def bound_squares(n, par):
                    N = base + n
                    wait(dve, s["ss_ready"], N + 1)
                    wait(dve, s["ssl_ready"], N)
                    dve.tensor_scalar(ssc[:, :], ss[:, :], 1e-24, None, ALU.max).then_inc(s["ssc_ready"], 1)

                def normalise_qk(n, par):
                    N = base + n
                    wait(dve, s["inv_ready"], N + 1)
                    wait(dve, s["rot1_ready"], N)
                    wait(dve, s["rot2_ready"], N)
                    for i, b_x in enumerate((b_q, b_k)):
                        ins = dve.tensor_tensor(
                            qn[:, i * INNER:(i + 1) * INNER].rearrange("p (h e) -> p h e", e=DH),
                            b_x[:, :].rearrange("p (h e) -> p h e", e=DH),
                            inv[:, i * AH:(i + 1) * AH].unsqueeze(2).to_broadcast([P, AH, DH]), ALU.mult)
                    ins.then_inc(s["qn_ready"], 1)

                def rotate_cos(n, par):
                    N = base + n
                    if isinstance(n, int) and n == 0:
                        dve.wait_ge(s["table_ready"], l + 1)
                    wait(dve, s["qn_ready"], N + 1)
                    wait(dve, s["qr_ready"], N)
                    for i in range(2):
                        tab = cos_t[:, bass.ds((n - par) * DH + i * DH, DH)]
                        ins = dve.tensor_tensor(
                            rot1[:, i * INNER:(i + 1) * INNER].rearrange("p (h e) -> p h e", e=DH),
                            qn[:, i * INNER:(i + 1) * INNER].rearrange("p (h e) -> p h e", e=DH),
                            tab.unsqueeze(1).to_broadcast([P, AH, DH]), ALU.mult)
                    ins.then_inc(s["rot1_ready"], 1)

                def rotate_add(n, par):
                    N = base + n
                    wait(dve, s["rot1_ready"], N + 1)
                    wait(dve, s["rot2_ready"], N + 1)
                    wait(dve, s["qt_done"], N - 1)
                    wait(dve, s["kt_done"], N - 1)
                    dve.tensor_tensor(qr[:, par * 2 * INNER:(par + 1) * 2 * INNER], rot1[:, :], rot2[:, :], ALU.add
                                      ).then_inc(s["qr_ready"], 1)

                def copy_q_bd(n, par):
                    N = base + n
                    wait(dve, s["qt_done"], N + 1)
                    wait(dve, s["sc0_done"], N - 1)
                    wait(dve, s["sc1_done"], N - 1)
                    dst, src = q_blocks(par, b_t0, 0)
                    dve.tensor_copy(dst, src).then_inc(s["qbd0_ready"], 1)

                def row_max(n, par, w):
                    N = base + n
                    wait(dve, s[f"sc{w}_done"], N + 1)
                    wait(dve, s[f"p{w}_ready"], N)
                    dve.tensor_reduce(neg_max[:, w * PAIRS:(w + 1) * PAIRS],
                                      (b_s0, b_s1)[w][:, :].rearrange("p (c k) -> p c k", c=PAIRS),
                                      AX.X, ALU.max, negate=True).then_inc(s[f"max{w}_ready"], 1)

                def row_reciprocals(n, par, w):
                    N = base + n
                    wait(dve, s[f"p{w}_ready"], N + 1)
                    wait(dve, s[f"pn{w}_ready"], N)
                    r = (par * 2 + w) * PAIRS
                    dve.reciprocal(row_rec[:, w * PAIRS:(w + 1) * PAIRS], row_sum[:, r:r + PAIRS]
                                   ).then_inc(s[f"rs{w}_ready"], 1)

                def copy_probs_t(n, par):
                    N = base + n
                    wait(dve, s["pt1_done"], N + 1)
                    wait(dve, s["pv_done"], N)
                    dve.tensor_copy(probs_t[:, PAIRS * P:2 * PAIRS * P], b_t1[:, :]).then_inc(s["pt1_ready"], 1)

                def add_attention(n, par):
                    N = base + n
                    wait(dve, s["wo_done"], N + 1)
                    dve.tensor_tensor(middle[:, bass.ds((n + 2) * D, D)], b_m[:, P:2 * P], tile_of(stream[l], n),
                                      ALU.add).then_inc(s["mid_ready"], 1)

                def stats_z(n, par):
                    N = base + n
                    wait_apart(dve, (s["hs_ready"], N + 1), (s["z_aggr"], N))
                    dve.bn_stats(st_z[:, :], hcat[:, par * P:(par + 1) * P]).then_inc(s["z_stats"], 1)

                def aggregate_z(n, par):
                    N = base + n
                    wait_apart(dve, (s["z_stats"], N + 1), (s["zn_ready"], N))
                    dve.bn_aggr(mv_z[:, :], st_z[:, :]).then_inc(s["z_aggr"], 1)

                def normalise_z(n, par):
                    N = base + n
                    wait(dve, s["z_rstd"], N + 1)
                    wait(dve, s["zt_done"], N - 1)
                    dve.tensor_scalar(zn[:, par * P:(par + 1) * P], hcat[:, par * P:(par + 1) * P], mv_z[:, 0:1],
                                      rstd_z[:, :], ALU.subtract, ALU.mult).then_inc(s["zn_ready"], 1)

                def attn_step(k, par):
                    staged(row_reciprocals, k, par, 0, 0)
                    staged(copy_q_bd, k, par, 1)
                    staged(add_attention, k, par, -1)
                    staged(sum_squares, k, par, 2)
                    staged(bound_squares, k, par, 2)
                    staged(row_max, k, par, 1, 1)
                    staged(normalise_qk, k, par, 2)
                    staged(stats_z, k, par, -1)
                    staged(copy_probs_t, k, par, 0)
                    staged(aggregate_z, k, par, -1)
                    staged(row_max, k, par, 1, 0)
                    staged(rotate_cos, k, par, 2)
                    staged(row_reciprocals, k, par, 1, 1)
                    staged(rotate_add, k, par, 2)
                    staged(normalise_z, k, par, -1)
                if l:
                    feed_forward(l - 1, (sum_squares, bound_squares), (normalise_qk,), (rotate_cos,))
                    rotate_add(0, 0)
                else:
                    for stage, n in ((stats_y, LAST), (aggregate_y, LAST), (normalise_y, LAST), (stats_f, LAST),
                                     (aggregate_f, LAST), (sum_squares, 0), (bound_squares, 0), (normalise_f, LAST),
                                     (normalise_qk, 0), (rotate_cos, 0), (rotate_add, 0)):
                        stage(n, n % 2)
                iterate(dve, attn_step, first=-1)
            feed_forward(DEPTH - 1)
            for n in range(NT - GROUP, NT, 2):
                normalise_out(n)
                dve.wait_ge(s["xo_ready"], (ON_ACT + n - (NT - GROUP)) // 2 + 1)
                c = slice(n * D, (n + 2) * D)
                dve.tensor_tensor(res[:, c], xo[:, c], x_attn[:, c], ALU.add).then_inc(s["last_res_ready"], 1)


def square_constants():
    import numpy as np
    i = np.arange(128)
    ident = (i[:, None] == i[None, :])
    shift = (i[:, None] + 1 == i[None, :])
    carry = (i[:, None] == 127) & (i[None, :] == 0)
    q = i[:, None] % 64
    k = i[None, :] % 64
    second = i[None, :] >= 64
    low = np.float32(-1e30)
    mask_b = np.where(np.where(second, k <= q, k >= q), np.float32(0), low)
    mask_a = np.where(np.where(second, k >= q, k <= q), np.float32(0), low)
    mask_a0 = np.where(~second & (k <= q), np.float32(0), low)
    causal = (i[:, None] // 64 == i[None, :] // 64) & (i[:, None] <= i[None, :])
    keep = np.broadcast_to(i[None, :] % 64 != 0, (128, 128))
    return np.concatenate([np.asarray(a, np.float32) for a in
                           (ident, causal, keep, shift, carry, mask_a, mask_b, mask_a0)], axis=1)


def rotary_tables(n, dh, window, qk_scale):
    import numpy as np
    half = np.arange(0, dh, 2, dtype=np.float32)
    freq = (np.float32(1.0) / np.power(np.float32(10000.0), half / np.float32(dh))).astype(np.float32)
    t = np.arange(n, dtype=np.float32)
    f = (t[:, None] * freq[None, :]).astype(np.float32).astype(np.float64)
    f = np.concatenate([f, f], axis=-1)
    base = ((half + np.float32(0.4 * dh)) / np.float32(1.4 * dh)).astype(np.float64)
    power = (t - n // 2).astype(np.float64) / (window // 2)
    sc = base[None, :] ** power[:, None]
    sc = np.concatenate([sc, sc], axis=-1)
    sign = np.where(np.arange(dh) < dh // 2, -1.0, 1.0)
    tabs = []
    for g in (np.cos(f), np.sin(f) * sign):
        both = np.stack([g * sc * qk_scale, g / sc], axis=1)
        tabs.append(np.ascontiguousarray(both.reshape(n // 128, 128, 2 * dh).transpose(1, 0, 2)
                                         .reshape(128, -1).astype(np.float32)))
    return tabs


_INS = ["L0_attn_x", "L0_attn_Wq", "L0_attn_Wk", "L0_attn_Wv", "L0_attn_Wg", "L0_attn_Wgk1", "L0_attn_Wgk2",
        "L0_attn_bgk2", "L0_attn_Wo", "L0_attn_rms_w", "L0_ffn_wqkv", "L0_ffn_q_scale", "L0_ffn_k_scale",
        "L0_ffn_wo", "L0_ffn_ln_g", "L0_ffn_ln_b", "L0_ffn_w1", "L0_ffn_b1", "L0_ffn_w2", "L0_ffn_b2"]


def kernel(**inputs):
    import numpy as np
    import concourse.bacc as bacc
    from concourse.bass_utils import run_bass_kernel_spmd

    nc = bacc.Bacc("TRN2", target_bir_lowering=False, num_devices=1)
    arrays = {f"in_{name}": np.ascontiguousarray(inputs[name]) for name in _INS}
    arrays["square_consts"] = square_constants()
    arrays["rotary_cos"], arrays["rotary_sin"] = rotary_tables(arrays["in_L0_attn_x"].shape[1], 64, 64, 8.0)
    args = [nc.dram_tensor(name, a.shape, mybir.dt.from_np(a.dtype), kind="ExternalInput").ap()
            for name, a in arrays.items()]
    shape = arrays["in_L0_attn_x"].shape
    args.append(nc.dram_tensor("out_x", shape, F32, kind="ExternalOutput").ap())
    build_program(nc, *args)
    r = run_bass_kernel_spmd(nc, [arrays], core_ids=[0])
    return r.results[0]["out_x"]
```
